# Optimizing a Trainium2 kernel written in Bass

```python
import numpy as np
import jax
import jax.numpy as jnp

def _softmax(x, axis=-1):
    return jax.nn.softmax(x, axis=axis)

def _gelu(x):
    return jax.nn.gelu(x, approximate=True)

def _silu(x):
    return jax.nn.silu(x)

def _sigmoid(x):
    return jax.nn.sigmoid(x)

def _layernorm(x, axis=-1, eps=1e-05):
    m = jnp.mean(x, axis=axis, keepdims=True)
    v = jnp.var(x, axis=axis, keepdims=True)
    return (x - m) / jnp.sqrt(v + eps)

def _scatter_add(tgt, idx, src, axis=0):
    return tgt.at[idx].add(src)

def _segment_sum(src, seg, n):
    return jax.ops.segment_sum(src, seg, n)
kernel_name = 'mk_seq_postln_d1_jaxref_r8_814f01'

def setup_inputs(seed: int=0):
    np.random.seed(seed)
    _w = jnp.asarray

    def _L0_attn_setup():
        import jax, jax.numpy as jnp
        import numpy as np
        B, T, D = (4, 256, 128)
        H, DK, DV = (8, 128, 128)

        def _l2norm(u, eps=1e-12):
            n = jnp.sqrt(jnp.sum(u * u, axis=-1, keepdims=True))
            return u / jnp.maximum(n, eps)
        key = jax.random.key(seed)
        ks = jax.random.split(key, 6)
        s = 0.02
        x = jax.random.normal(ks[0], (B, T, D), dtype=jnp.float32)
        Wq = jax.random.normal(ks[1], (D, H * DK), dtype=jnp.float32) * s
        Wk = jax.random.normal(ks[2], (D, H * DK), dtype=jnp.float32) * s
        Wv = jax.random.normal(ks[3], (D, H * DV), dtype=jnp.float32) * s
        Wg = jax.random.normal(ks[4], (D, H * DK), dtype=jnp.float32) * s
        Wo = jax.random.normal(ks[5], (H * DV, D), dtype=jnp.float32) * s
        return {'x': x, 'Wq': Wq, 'Wk': Wk, 'Wv': Wv, 'Wg': Wg, 'Wo': Wo}
    _L0_attn_in = _L0_attn_setup()

    def _L0_ffn_setup():
        import jax, jax.numpy as jnp
        import numpy as np
        B, S, D = (2, 256, 128)
        E, K, H = (8, 4, 128)
        SH = 2 * H

        def _silu(x):
            return x * jax.nn.sigmoid(x)

        def _swiglu(x, w1, b1, w2, b2):
            return _silu(x @ w1 + b1) * (x @ w2 + b2)

        def _moe(x, gate_w, exp_w1, exp_w3, exp_w2, sh_w1, sh_w3, sh_w2):
            b, s, d = x.shape
            t = b * s
            xt = x.reshape(t, d)
            scores = jax.nn.softmax(xt @ gate_w.T, axis=-1)
            topv, topi = jax.lax.top_k(scores, K)
            topv = topv / jnp.sum(topv, axis=-1, keepdims=True)
            combine = jnp.zeros((t, E), xt.dtype).at[jnp.arange(t)[:, None], topi].set(topv)
            g = _silu(jnp.einsum('td,edh->eth', xt, exp_w1))
            u = jnp.einsum('td,edh->eth', xt, exp_w3)
            yexp = jnp.einsum('eth,ehd->etd', g * u, exp_w2)
            routed = jnp.einsum('te,etd->td', combine, yexp)
            shared = _silu(xt @ sh_w1) * (xt @ sh_w3) @ sh_w2
            return (routed + shared).reshape(b, s, d)
        key = jax.random.key(seed)
        ks = jax.random.split(key, 24)
        f = lambda k, shape: jax.random.normal(k, shape, dtype=jnp.float32) * 0.02
        return {'x': jax.random.normal(ks[0], (B, S, D), dtype=jnp.float32), 'lin0_w': f(ks[1], (D, D)), 'lin0_b': f(ks[2], (D,)), 'swi1_w1': f(ks[3], (D, D)), 'swi1_b1': f(ks[4], (D,)), 'swi1_w2': f(ks[5], (D, D)), 'swi1_b2': f(ks[6], (D,)), 'gate_w': f(ks[7], (E, D)), 'exp_w1': f(ks[8], (E, D, H)), 'exp_w3': f(ks[9], (E, D, H)), 'exp_w2': f(ks[10], (E, H, D)), 'sh_w1': f(ks[11], (D, SH)), 'sh_w3': f(ks[12], (D, SH)), 'sh_w2': f(ks[13], (SH, D)), 'lin1_w': f(ks[14], (D, D)), 'lin1_b': f(ks[15], (D,)), 'swi2_w1': f(ks[16], (D, D)), 'swi2_b1': f(ks[17], (D,)), 'swi2_w2': f(ks[18], (D, D)), 'swi2_b2': f(ks[19], (D,))}
    _L0_ffn_in = _L0_ffn_setup()
    _d = {'L0_attn_x': _L0_attn_in['x'], 'L0_attn_Wq': _L0_attn_in['Wq'], 'L0_attn_Wk': _L0_attn_in['Wk'], 'L0_attn_Wv': _L0_attn_in['Wv'], 'L0_attn_Wg': _L0_attn_in['Wg'], 'L0_attn_Wo': _L0_attn_in['Wo'], 'L0_ffn_lin0_w': _L0_ffn_in['lin0_w'], 'L0_ffn_lin0_b': _L0_ffn_in['lin0_b'], 'L0_ffn_swi1_w1': _L0_ffn_in['swi1_w1'], 'L0_ffn_swi1_b1': _L0_ffn_in['swi1_b1'], 'L0_ffn_swi1_w2': _L0_ffn_in['swi1_w2'], 'L0_ffn_swi1_b2': _L0_ffn_in['swi1_b2'], 'L0_ffn_gate_w': _L0_ffn_in['gate_w'], 'L0_ffn_exp_w1': _L0_ffn_in['exp_w1'], 'L0_ffn_exp_w3': _L0_ffn_in['exp_w3'], 'L0_ffn_exp_w2': _L0_ffn_in['exp_w2'], 'L0_ffn_sh_w1': _L0_ffn_in['sh_w1'], 'L0_ffn_sh_w3': _L0_ffn_in['sh_w3'], 'L0_ffn_sh_w2': _L0_ffn_in['sh_w2'], 'L0_ffn_lin1_w': _L0_ffn_in['lin1_w'], 'L0_ffn_lin1_b': _L0_ffn_in['lin1_b'], 'L0_ffn_swi2_w1': _L0_ffn_in['swi2_w1'], 'L0_ffn_swi2_b1': _L0_ffn_in['swi2_b1'], 'L0_ffn_swi2_w2': _L0_ffn_in['swi2_w2'], 'L0_ffn_swi2_b2': _L0_ffn_in['swi2_b2']}
    _x0 = _d['L0_attn_x']
    _d['L0_attn_x'] = jax.random.normal(jax.random.fold_in(jax.random.key(seed), 1), (16, 512, 128), dtype=_x0.dtype)
    del _x0
    return _d

def reference(L0_attn_x, L0_attn_Wq, L0_attn_Wk, L0_attn_Wv, L0_attn_Wg, L0_attn_Wo, L0_ffn_lin0_w, L0_ffn_lin0_b, L0_ffn_swi1_w1, L0_ffn_swi1_b1, L0_ffn_swi1_w2, L0_ffn_swi1_b2, L0_ffn_gate_w, L0_ffn_exp_w1, L0_ffn_exp_w3, L0_ffn_exp_w2, L0_ffn_sh_w1, L0_ffn_sh_w3, L0_ffn_sh_w2, L0_ffn_lin1_w, L0_ffn_lin1_b, L0_ffn_swi2_w1, L0_ffn_swi2_b1, L0_ffn_swi2_w2, L0_ffn_swi2_b2):

    def _L0_attn_ref(x, Wq, Wk, Wv, Wg, Wo):
        import jax, jax.numpy as jnp
        import numpy as np
        B, T, D = (4, 256, 128)
        H, DK, DV = (8, 128, 128)

        def _l2norm(u, eps=1e-12):
            n = jnp.sqrt(jnp.sum(u * u, axis=-1, keepdims=True))
            return u / jnp.maximum(n, eps)
        Bb, Tt, _ = x.shape
        q = _l2norm((x @ Wq).reshape(Bb, Tt, H, DK))
        k = _l2norm((x @ Wk).reshape(Bb, Tt, H, DK))
        v = (x @ Wv).reshape(Bb, Tt, H, DV)
        alpha = jax.nn.sigmoid(x @ Wg).reshape(Bb, Tt, H, DK)

        def step(S, qkva):
            q_t, k_t, v_t, a_t = qkva
            S = a_t[..., None] * S + k_t[..., None] * v_t[:, :, None, :]
            o_t = jnp.einsum('bhkv,bhk->bhv', S, q_t)
            return (S, o_t)
        S0 = jnp.zeros((Bb, H, DK, DV), dtype=x.dtype)
        xs = (q.swapaxes(0, 1), k.swapaxes(0, 1), v.swapaxes(0, 1), alpha.swapaxes(0, 1))
        _, o = jax.lax.scan(step, S0, xs)
        o = o.swapaxes(0, 1).reshape(Bb, Tt, H * DV)
        return o @ Wo

    def _L0_ffn_ref(x, lin0_w, lin0_b, swi1_w1, swi1_b1, swi1_w2, swi1_b2, gate_w, exp_w1, exp_w3, exp_w2, sh_w1, sh_w3, sh_w2, lin1_w, lin1_b, swi2_w1, swi2_b1, swi2_w2, swi2_b2):
        import jax, jax.numpy as jnp
        import numpy as np
        B, S, D = (2, 256, 128)
        E, K, H = (8, 4, 128)
        SH = 2 * H

        def _silu(x):
            return x * jax.nn.sigmoid(x)

        def _swiglu(x, w1, b1, w2, b2):
            return _silu(x @ w1 + b1) * (x @ w2 + b2)

        def _moe(x, gate_w, exp_w1, exp_w3, exp_w2, sh_w1, sh_w3, sh_w2):
            b, s, d = x.shape
            t = b * s
            xt = x.reshape(t, d)
            scores = jax.nn.softmax(xt @ gate_w.T, axis=-1)
            topv, topi = jax.lax.top_k(scores, K)
            topv = topv / jnp.sum(topv, axis=-1, keepdims=True)
            combine = jnp.zeros((t, E), xt.dtype).at[jnp.arange(t)[:, None], topi].set(topv)
            g = _silu(jnp.einsum('td,edh->eth', xt, exp_w1))
            u = jnp.einsum('td,edh->eth', xt, exp_w3)
            yexp = jnp.einsum('eth,ehd->etd', g * u, exp_w2)
            routed = jnp.einsum('te,etd->td', combine, yexp)
            shared = _silu(xt @ sh_w1) * (xt @ sh_w3) @ sh_w2
            return (routed + shared).reshape(b, s, d)
        h = x @ lin0_w + lin0_b
        h = _swiglu(h, swi1_w1, swi1_b1, swi1_w2, swi1_b2)
        h = _moe(h, gate_w, exp_w1, exp_w3, exp_w2, sh_w1, sh_w3, sh_w2)
        h = h @ lin1_w + lin1_b
        h = _swiglu(h, swi2_w1, swi2_b1, swi2_w2, swi2_b2)
        return h
    x = L0_attn_x
    x = _layernorm(x + _L0_attn_ref(x, L0_attn_Wq, L0_attn_Wk, L0_attn_Wv, L0_attn_Wg, L0_attn_Wo), axis=-1)
    x = _layernorm(x + _L0_ffn_ref(x, L0_ffn_lin0_w, L0_ffn_lin0_b, L0_ffn_swi1_w1, L0_ffn_swi1_b1, L0_ffn_swi1_w2, L0_ffn_swi1_b2, L0_ffn_gate_w, L0_ffn_exp_w1, L0_ffn_exp_w3, L0_ffn_exp_w2, L0_ffn_sh_w1, L0_ffn_sh_w3, L0_ffn_sh_w2, L0_ffn_lin1_w, L0_ffn_lin1_b, L0_ffn_swi2_w1, L0_ffn_swi2_b1, L0_ffn_swi2_w2, L0_ffn_swi2_b2), axis=-1)
    return x

_drawn_inputs = setup_inputs


def setup_inputs(seed=0):
    import zlib

    import numpy as np

    out = dict(_drawn_inputs(seed))
    spreads = {}
    factors = {'L0_attn_Wq': 3.8,
     'L0_attn_Wk': 3.79,
     'L0_attn_Wv': 3.822,
     'L0_attn_Wg': 8.0,
     'L0_attn_Wo': 3.827,
     'L0_ffn_lin0_w': 8.0,
     'L0_ffn_lin0_b': 8.0,
     'L0_ffn_swi1_w1': 8.0,
     'L0_ffn_swi1_b1': 8.0,
     'L0_ffn_swi1_w2': 8.0,
     'L0_ffn_swi1_b2': 8.0,
     'L0_ffn_gate_w': 8.0,
     'L0_ffn_exp_w1': 8.0,
     'L0_ffn_exp_w3': 8.0,
     'L0_ffn_exp_w2': 8.0,
     'L0_ffn_sh_w1': 8.0,
     'L0_ffn_sh_w3': 8.0,
     'L0_ffn_sh_w2': 8.0,
     'L0_ffn_lin1_w': 8.0,
     'L0_ffn_lin1_b': 8.0,
     'L0_ffn_swi2_w1': 8.0,
     'L0_ffn_swi2_b1': 8.0,
     'L0_ffn_swi2_w2': 8.0,
     'L0_ffn_swi2_b2': 8.0}
    for name, (base, spread) in spreads.items():
        noise = np.random.default_rng([zlib.crc32(name.encode()), seed]).standard_normal(out[name].shape)
        drawn = base * np.exp(spread * noise) if base else spread * noise
        out[name] = jnp.asarray(drawn.astype(out[name].dtype))
    for name, factor in factors.items():
        out[name] = (out[name] * factor).astype(out[name].dtype)
    return out
```

```python
import concourse.bass as bass
from concourse import mybir
from contextlib import ExitStack


def gated_linear_attention_and_moe_block(
    nc: bass.Bass,
    x: bass.AP,
    Wq: bass.AP,
    Wk: bass.AP,
    Wv: bass.AP,
    Wg: bass.AP,
    Wo: bass.AP,
    lin0_w: bass.AP,
    lin0_b: bass.AP,
    swi1_w1: bass.AP,
    swi1_b1: bass.AP,
    swi1_w2: bass.AP,
    swi1_b2: bass.AP,
    gate_w: bass.AP,
    exp_w1: bass.AP,
    exp_w3: bass.AP,
    exp_w2: bass.AP,
    sh_w1: bass.AP,
    sh_w3: bass.AP,
    sh_w2: bass.AP,
    lin1_w: bass.AP,
    lin1_b: bass.AP,
    swi2_w1: bass.AP,
    swi2_b1: bass.AP,
    swi2_w2: bass.AP,
    swi2_b2: bass.AP,
    out: bass.AP,
):
    fp32 = mybir.dt.float32
    i32 = mybir.dt.int32
    ALU = mybir.AluOpType
    ACT = mybir.ActivationFunctionType
    AX = mybir.AxisListType

    B, T, D = x.shape
    H = Wq.shape[1] // D
    C = 128
    NC = T // C
    HP = 2
    NP = H // HP
    G = HP * NC
    W = HP * T
    E, _, FH = exp_w1.shape
    NS = sh_w1.shape[1] // FH
    NE = E + NS
    TOPK = 4
    LN_EPS = 1e-5
    L2_EPS = 1e-12
    STEPS = 8
    HALF = {j: 2 ** (j - 1) for j in range(2, STEPS)}

    ctx = ExitStack()
    with ctx:
        def sb(name, shape, dt=fp32):
            return ctx.enter_context(nc.sbuf_tensor(name, shape, dt))

        def sem(name):
            return ctx.enter_context(nc.semaphore(name))

        banks = [ctx.enter_context(nc.psum_tensor(f"bank{n}", [128, 512], fp32)) for n in range(8)]

        wq = sb("wq", [128, H * D])
        wk = sb("wk", [128, H * D])
        wg = sb("wg", [128, H * D])
        wvo = sb("wvo", [128, H * D])
        wv_raw = sb("wv_raw", [128, H * D])
        wo = sb("wo", [128, H, D])
        ew1 = sb("ew1", [128, NE, FH])
        ew3 = sb("ew3", [128, NE, FH])
        ew2 = sb("ew2", [128, NE, D])
        lin = sb("lin", [128, 2, D])
        swi = sb("swi", [128, 2, 2 * D])
        swf = sb("swf", [128, 2, 2 * D])
        gate_rows = sb("gate_rows", [E, D])
        gate_t = sb("gate_t", [128, E])
        lin_b = sb("lin_b", [128, 2])
        swi_b = sb("swi_b", [128, 4])
        swf_b = sb("swf_b", [128, 4])
        ident = sb("ident", [128, 128])
        ones = sb("ones", [128, 128])
        mask_odd = sb("mask_odd", [128, 64])
        mask_half = sb("mask_half", [128, 4, 64])
        earlier = sb("earlier", [128, E, E])
        expo = sb("expo", [128, 16])

        x_all = sb("x_all", [128, B * NC, D])
        x_nat = sb("x_nat", [128, NC, D])
        xT = sb("xT", [128, T])

        q_sb = [sb(f"q_sb{i}", [128, W]) for i in range(2)]
        k_sb = [sb(f"k_sb{i}", [128, W]) for i in range(2)]
        a_sb = [sb(f"a_sb{i}", [128, W]) for i in range(2)]
        qd_sb = [sb(f"qd_sb{i}", [128, W]) for i in range(2)]
        tot_sb = [sb(f"tot_sb{i}", [128, W]) for i in range(2)]
        at_sb = [sb(f"at_sb{i}", [128, G, C]) for i in range(2)]
        v_sb = [sb(f"v_sb{i}", [128, NC, HP * D]) for i in range(2)]
        sq_sb = sb("sq_sb", [128, 2, HP, T])
        kt_sb = sb("kt_sb", [128, HP, NC - 1, 128])
        s_sb = sb("s_sb", [128, HP, NC - 1, D])
        ss_sb = sb("ss_sb", [128, 16])
        rn_sb = [sb(f"rn_sb{i}", [128, 2, HP, NC]) for i in range(2)]

        res = sb("res", [128, NC, D])
        stats = sb("stats", [128, NC, 6])
        lt = sb("lt", [128, 5, NC])
        mean = sb("mean", [128, NC])
        ve = sb("ve", [128, NC])
        rstd = sb("rstd", [128, NC])

        x1T = sb("x1T", [128, T])
        s1 = sb("s1", [128, T])
        xt_sb = [sb(f"xt_sb{i}", [128, T]) for i in range(2)]
        comb = [sb(f"comb{i}", [128, NC, E]) for i in range(2)]
        lg = sb("lg", [128, NC, E])
        lmax = sb("lmax", [128, NC])
        ex = sb("ex", [128, NC, E])
        gt = sb("gt", [128, NC * E, E])
        eq = sb("eq", [128, NC * E, E])
        eqe = sb("eqe", [128, NC * E, E])
        rank = sb("rank", [128, NC, E])
        picked = sb("picked", [128, NC, E])
        den = sb("den", [128, NC])
        rden = sb("rden", [128, NC])
        sg = [sb(f"sg{i}", [128, T]) for i in range(2)]
        gu = [sb(f"gu{i}", [128, T]) for i in range(2)]
        gc = [sb(f"gc{i}", [128, T]) for i in range(2)]
        r_sb = sb("r_sb", [128, T])
        s2 = sb("s2", [128, T])
        h_sb = sb("h_sb", [128, T])
        o_sb = [sb(f"o_sb{i}", [128, NC, D]) for i in range(2)]

        pj = [banks[0], banks[1]]
        sc = [banks[2], banks[3]]
        y_ps = banks[4]
        nb_ps = banks[5]
        kt_ps = banks[6]
        su_ps = banks[7]
        g_ps = [banks[0], banks[1]]
        u_ps = [banks[2], banks[3]]
        h0_ps = banks[4]
        h1_ps = banks[5]
        cb_ps = banks[6]
        r_ps = banks[7]

        w_in = sem("w_in")
        x_in = sem("x_in")
        xn_in = sem("xn_in")
        const_pool = sem("const_pool")
        const_dve = sem("const_dve")
        fold_pe = sem("fold_pe")
        fold_sb = sem("fold_sb")
        fold_bias = sem("fold_bias")
        pj_full = sem("pj_full")
        pj_evac = sem("pj_evac")
        xt_full = sem("xt_full")
        xt_evac = sem("xt_evac")
        sq_done = sem("sq_done")
        ss_full = sem("ss_full")
        ss_evac = sem("ss_evac")
        rn_done = sem("rn_done")
        rb_full = sem("rb_full")
        qn_done = sem("qn_done")
        q1_done = sem("q1_done")
        k_up = sem("k_up")
        q_up = sem("q_up")
        tot_done = sem("tot_done")
        qk_full = sem("qk_full")
        sc_evac = sem("sc_evac")
        sc_act = sem("sc_act")
        kt_full = sem("kt_full")
        kt_evac = sem("kt_evac")
        su_full = sem("su_full")
        s_done = sem("s_done")
        av_done = sem("av_done")
        res_done = sem("res_done")
        ln_chain = sem("ln_chain")
        ve_done = sem("ve_done")
        rstd_done = sem("rstd_done")
        x1_done = sem("x1_done")
        out_done = sem("out_done")
        nat_in = sem("nat_in")
        f_x1T = sem("f_x1T")
        f_z = sem("f_z")
        f_gate = sem("f_gate")
        f_g = sem("f_g")
        f_u = sem("f_u")
        f_cb = sem("f_cb")
        f_down = sem("f_down")
        f_zo = sem("f_zo")
        f_hT = sem("f_hT")
        a_x1T = sem("a_x1T")
        a_s1 = sem("a_s1")
        a_ex = sem("a_ex")
        a_sg = sem("a_sg")
        a_r = sem("a_r")
        a_s2 = sem("a_s2")
        v_xt = sem("v_xt")
        v_lg = sem("v_lg")
        v_comb = sem("v_comb")
        v_top = sem("v_top")
        v_gu = sem("v_gu")
        v_mid = sem("v_mid")
        v_h = sem("v_h")

        block = ctx.enter_context(nc.Block())

        def await_count(eng, s, count):
            if not (isinstance(count, int) and count <= 0):
                eng.wait_ge(s, count)

        def halves(ap, m):
            return ap.rearrange("p (n two m) -> p n two m", two=2, m=m)

        def tot(par, m):
            if m == 1:
                return a_sb[par][:, :]
            at = W - 2 * W // m
            return tot_sb[par][:, at:at + W // m]

        def slots(b, first, last):
            for p in range(NP):
                yield p, b * NP + p, not (first and p == 0), not (last and p == NP - 1)


        @block.sync
        def _(sp):
            sp.dma_start(x_nat[:, :, :], x[0].rearrange("(c t) d -> t c d", t=C)).then_inc(xn_in, 16)
            sp.dma_start(wq[:, :], Wq).then_inc(w_in, 16)
            sp.dma_start(wk[:, :], Wk).then_inc(w_in, 16)
            sp.dma_start(wg[:, :], Wg).then_inc(w_in, 16)
            sp.dma_start(wv_raw[:, :], Wv).then_inc(w_in, 16)
            sp.dma_start(wo[:, :, :], Wo.rearrange("(h v) d -> v h d", v=D)).then_inc(w_in, 16)
            sp.dma_start(lin[:, 0, :], lin0_w).then_inc(w_in, 16)
            sp.dma_start(lin[:, 1, :], lin1_w).then_inc(w_in, 16)
            sp.dma_start(swi[:, 0, 0:D], swi1_w1).then_inc(w_in, 16)
            sp.dma_start(swi[:, 0, D:2 * D], swi1_w2).then_inc(w_in, 16)
            sp.dma_start(swi[:, 1, 0:D], swi2_w1).then_inc(w_in, 16)
            sp.dma_start(swi[:, 1, D:2 * D], swi2_w2).then_inc(w_in, 16)
            sp.dma_start(gate_rows[:, :], gate_w).then_inc(w_in, 16)
            for n, bias in enumerate((lin0_b, lin1_b)):
                sp.dma_start(lin_b[:, n:n + 1], bias.rearrange("(p a) -> p a", a=1)).then_inc(w_in, 16)
            for n, bias in enumerate((swi1_b1, swi1_b2, swi2_b1, swi2_b2)):
                sp.dma_start(swi_b[:, n:n + 1], bias.rearrange("(p a) -> p a", a=1)).then_inc(w_in, 16)
            sp.dma_start(x_all[:, :, :], x.rearrange("b (c t) d -> t (b c) d", t=C)).then_inc(x_in, 16)
            for dst, routed, shared in ((ew1, exp_w1, sh_w1), (ew3, exp_w3, sh_w3)):
                sp.dma_start(dst[:, 0:E, :], routed.rearrange("e d f -> d e f")).then_inc(x_in, 16)
                sp.dma_start(dst[:, E:NE, :], shared.rearrange("d (n f) -> d n f", f=FH)).then_inc(x_in, 16)
            sp.dma_start(ew2[:, 0:E, :], exp_w2.rearrange("e f d -> f e d")).then_inc(x_in, 16)
            sp.dma_start(ew2[:, E:NE, :], sh_w2.rearrange("(n f) d -> f n d", f=FH)).then_inc(x_in, 16)

            def next_x(b):
                sp.wait_ge(xt_full, b)
                sp.dma_start(x_nat[:, :, :], x[bass.ds(b, 1)].rearrange("a (c t) d -> t (a c) d", t=C)).then_inc(xn_in, 16)

            with sp.Fori(1, B) as b:
                next_x(b)

            def ffn_io(b, first=False, last=False):
                for par in range(2):
                    n = b + par
                    if not (first and par == 0):
                        sp.wait_ge(f_x1T, n)
                    sp.dma_start(x_nat[:, :, :], x_all[:, bass.ds(n * NC, NC), :]).then_inc(nat_in, 16)
                    if not (first and par == 0):
                        store(n - 1, 1 - par)

            def store(n, par):
                sp.wait_ge(x1_done, B + n + 1)
                sp.dma_start(out[bass.ds(n, 1)].rearrange("a (c t) d -> t (a c) d", t=C), o_sb[par][:, :, :]).then_inc(out_done, 16)

            sp.wait_ge(x1_done, B)
            sp.wait_ge(xt_full, B)
            ffn_io(0, first=True)
            with sp.Fori(1, B // 2) as i:
                ffn_io(2 * i)
            store(B - 1, 1)
            sp.wait_ge(out_done, 16 * B)

        W_ALL = 18 * 16
        X_ALL = 7 * 16

        def pool_setup(pool):
            nc.gpsimd.memset(ident[:, :], 0.0).then_inc(const_pool, 1)
            nc.gpsimd.memset(ones[:, :], 1.0).then_inc(const_pool, 1)
            nc.gpsimd.memset(mask_half[:, :, :], 1.0).then_inc(const_pool, 1)
            nc.gpsimd.memset(earlier[:, :, :], 1.0).then_inc(const_pool, 1)
            nc.gpsimd.memset(expo[:, :], -0.5).then_inc(const_pool, 1)
            pool.wait_ge(const_pool, 5)
            nc.gpsimd.affine_select(out=ident[:, :], in_=ident[:, :], compare_op=ALU.not_equal, fill=1.0,
                                    base=0, pattern=[[-1, 128]], channel_multiplier=1).then_inc(const_pool, 1)
            nc.gpsimd.affine_select(out=earlier[:, :, :], in_=earlier[:, :, :], compare_op=ALU.is_ge, fill=0.0,
                                    base=-1, pattern=[[1, E], [-1, E]], channel_multiplier=0).then_inc(const_pool, 1)
            for i, m in enumerate((2, 4, 8, 16)):
                view = mask_half[:, i, :].rearrange("p (n m) -> p n m", m=m)
                nc.gpsimd.affine_select(out=view, in_=view, compare_op=ALU.is_ge, fill=0.0,
                                        base=0, pattern=[[-2 * m, 64 // m], [0, m]], channel_multiplier=1).then_inc(const_pool, 1)
            pool.wait_ge(const_pool, 11)
            for i, m in enumerate((2, 4, 8, 16)):
                view = mask_half[:, i, :].rearrange("p (n m) -> p n m", m=m)
                nc.gpsimd.affine_select(out=view, in_=view, compare_op=ALU.is_ge, fill=0.0,
                                        base=m - 1, pattern=[[2 * m, 64 // m], [0, m]], channel_multiplier=-1).then_inc(const_pool, 1)

        CONST_POOL = 15

        @block.gpsimd
        def _(pool):
            pool_setup(pool)

            def norms(par, P):
                await_count(pool, ss_full, P)
                for h in range(HP):
                    for i, src in enumerate((q_sb, k_sb)):
                        pool.wait_ge(pj_evac, P * 8 + 2 * h + i + 1)
                        seg = src[par][:, h * T:(h + 1) * T]
                        nc.gpsimd.tensor_tensor(sq_sb[:, i, h, :], seg, seg, ALU.mult).then_inc(sq_done, 1)
                pool.wait_ge(ss_evac, P + 1)
                nc.gpsimd.tensor_tensor(rn_sb[par][:, :, :, :].rearrange("p i h c -> p (i h c)"), ss_sb[:, :],
                                        expo[:, :], ALU.pow).then_inc(rn_done, 1)

            def ln_rstd(n):
                pool.wait_ge(ve_done, n + 1)
                nc.gpsimd.tensor_tensor(rstd[:, :], ve[:, :], expo[:, 0:NC], ALU.pow).then_inc(rstd_done, 1)

            def body(b, first=False, last=False):
                for p, P, has_prev, has_next in slots(b, first, last):
                    if has_next:
                        norms((p + 1) % 2, P + 1)
                    if p == 0 and has_prev:
                        ln_rstd(b - 1)

            norms(0, 0)
            body(0, first=True)
            with pool.Fori(1, B - 1) as b:
                body(b)
            body(B - 1, last=True)
            ln_rstd(B - 1)

            with pool.Fori(0, B) as b:
                ln_rstd(b + B)

        @block.tensor
        def _(pe):
            def transposes_of_x(n):
                pe.wait_ge(xn_in, (n + 1) * 16)
                await_count(pe, qn_done, n * NP * HP)
                for c in range(NC):
                    mm = nc.tensor.transpose(nb_ps[:, c * C:(c + 1) * C], x_nat[:, c, :], ident[:, :])
                mm.then_inc(xt_full, 1)

            def bank_of(P, n):
                await_count(pe, pj_evac, P * 8 + n - 1)
                return pj[n % 2]

            def project_qk(p, P, h):
                col = (p * HP + h) * D
                for i, w in enumerate((wq, wk)):
                    bank = bank_of(P, 2 * h + i)
                    nc.tensor.matmul(bank[:, :], w[:, col:col + D], xT[:, :], start=True, stop=True).then_inc(pj_full, 1)

            def project_gate(p, P):
                for h in range(HP):
                    bank = bank_of(P, 4 + h)
                    col = (p * HP + h) * D
                    nc.tensor.matmul(bank[:, :], wg[:, col:col + D], xT[:, :], start=True, stop=True).then_inc(pj_full, 1)

            def project_values(p, P):
                for n in range(2):
                    bank = bank_of(P, 6 + n)
                    for i in range(2):
                        c = 2 * n + i
                        mm = nc.tensor.matmul(bank[:, i * HP * D:(i + 1) * HP * D], xT[:, c * C:(c + 1) * C],
                                              wvo[:, p * HP * D:(p + 1) * HP * D], start=True, stop=True)
                    mm.then_inc(pj_full, 1)

            def sums_of_squares(P, n_x):
                pe.wait_ge(sq_done, (P + 1) * 4)
                pe.wait_ge(xt_evac, n_x)
                await_count(pe, qn_done, P * HP)
                for i in range(2):
                    for h in range(HP):
                        for c in range(NC):
                            col = (i * HP + h) * NC + c
                            mm = nc.tensor.matmul(nb_ps[:, col:col + 1], sq_sb[:, i, h, c * C:(c + 1) * C],
                                                  ones[:, 0:1], start=True, stop=True)
                mm.then_inc(ss_full, 1)

            def spread_norms(par, P):
                pe.wait_ge(rn_done, P + 1)
                await_count(pe, kt_evac, P * HP - HP)
                for h, bank in enumerate((nb_ps, kt_ps)):
                    for c in range(NC):
                        mm = nc.tensor.transpose(bank[:, c * C:(c + 1) * C],
                                                 rn_sb[par][:, 0, h, c:c + 1].to_broadcast([128, 128]), ident[:, :])
                    mm.then_inc(rb_full, 1)

            def scores(par, P, j):
                if j == 0:
                    await_count(pe, sc_act, P * 3 - 1)
                    pe.wait_ge(qn_done, (P + 1) * HP)
                elif j == 1:
                    await_count(pe, sc_act, P * 3)
                    pe.wait_ge(k_up, P * 7 + 1)
                else:
                    pe.wait_ge(sc_evac, P * 6 + j - 1)
                    pe.wait_ge(k_up, P * 7 + j - 1)
                    if j == 2:
                        pe.wait_ge(q1_done, 2 * (P + 1))
                    else:
                        pe.wait_ge(q_up, P * 6 + j - 2)
                for g in range(G):
                    lo = g * C
                    if j < 2:
                        moving = q_sb[par][:, lo + j:lo + C:2]
                    else:
                        moving = halves(qd_sb[par][:, lo:lo + C], HALF[j])[:, :, 1, :]
                    mm = nc.tensor.matmul(sc[j % 2][:, g * 64:(g + 1) * 64], k_sb[par][:, lo:lo + C], moving,
                                          start=True, stop=True)
                mm.then_inc(qk_full, 1)

            def transposes_of_k(par, P, h):
                if h == 0:
                    pe.wait_ge(k_up, (P + 1) * 7)
                    pe.wait_ge(qn_done, (P + 2) * HP)
                else:
                    pe.wait_ge(kt_evac, P * HP + 1)
                for c in range(NC - 1):
                    lo = h * T + c * C
                    mm = nc.tensor.transpose(kt_ps[:, c * C:(c + 1) * C], k_sb[par][:, lo:lo + C], ident[:, :])
                mm.then_inc(kt_full, 1)

            def last_transposes_of_k(par, P, h):
                if h == 0:
                    pe.wait_ge(k_up, (P + 1) * 7)
                else:
                    pe.wait_ge(kt_evac, P * HP + 1)
                for c in range(NC - 1):
                    lo = h * T + c * C
                    mm = nc.tensor.transpose(kt_ps[:, c * C:(c + 1) * C], k_sb[par][:, lo:lo + C], ident[:, :])
                mm.then_inc(kt_full, 1)

            def state_updates(par, P, h):
                pe.wait_ge(kt_evac, P * HP + h + 1)
                pe.wait_ge(pj_evac, (P + 1) * 8)
                await_count(pe, s_done, (P * HP + h) * (NC - 1))
                for c in range(NC - 1):
                    mm = nc.tensor.matmul(su_ps[:, c * D:(c + 1) * D], kt_sb[:, h, c, :],
                                          v_sb[par][:, c, h * D:(h + 1) * D], start=True, stop=True)
                mm.then_inc(su_full, 1)

            def outputs(p, P, b, h):
                par = p % 2
                pe.wait_ge(sc_evac, (P + 1) * 6)
                pe.wait_ge(sc_act, (P + 1) * 3)
                pe.wait_ge(s_done, (P * HP + h + 1) * (NC - 1))
                pe.wait_ge(q_up, (P + 1) * 6)
                if p == 0 and h == 0:
                    await_count(pe, res_done, b)
                for c in range(NC):
                    first_mm = p == 0 and h == 0 and c == 0
                    last_mm = p == NP - 1 and h == HP - 1 and c == NC - 1
                    y = y_ps[:, c * D:(c + 1) * D]
                    mm = nc.tensor.matmul(y, at_sb[par][:, h * NC + c, :], v_sb[par][:, c, h * D:(h + 1) * D],
                                          start=first_mm, stop=last_mm and c == 0, skip_group_check=True)
                    if c > 0:
                        lo = h * T + c * C
                        mm = nc.tensor.matmul(y, qd_sb[par][:, lo:lo + C], s_sb[:, h, c - 1, :],
                                              start=False, stop=last_mm, skip_group_check=True)
                mm.then_inc(av_done, 1)

            pe.wait_ge(const_pool, CONST_POOL)
            transposes_of_x(0)
            pe.wait_ge(w_in, W_ALL)
            for n in range(2):
                for i in range(4):
                    h = 4 * n + i
                    mm = nc.tensor.transpose(pj[n][:, i * D:(i + 1) * D], wv_raw[:, h * D:(h + 1) * D], ident[:, :])
                mm.then_inc(fold_pe, 1)
            for i in range(2):
                nc.tensor.transpose(sc[0][:, i * D:(i + 1) * D], lin[:, i, :], ident[:, :])
            nc.tensor.transpose(sc[0][:, 2 * D:2 * D + E], gate_rows[:, :], ident[0:E, 0:E]).then_inc(fold_pe, 1)
            for i in range(2):
                for n in range(2):
                    mm = nc.tensor.matmul(sc[1][:, 2 * i + n:2 * i + n + 1], swi[:, i, n * D:(n + 1) * D],
                                          lin_b[:, i:i + 1], start=True, stop=True)
            mm.then_inc(fold_pe, 1)
            pe.wait_ge(fold_sb, 4)
            for n in range(2):
                for i in range(4):
                    h = 4 * n + i
                    mm = nc.tensor.matmul(pj[n][:, i * D:(i + 1) * D],
                                          sq_sb[:, 0, n, i * D:(i + 1) * D], wo[:, h, :], start=True, stop=True)
                mm.then_inc(fold_pe, 1)
            for i in range(2):
                mm = nc.tensor.matmul(sc[0][:, i * 2 * D:(i + 1) * 2 * D], s1[:, i * D:(i + 1) * D], swi[:, i, :],
                                      start=True, stop=True)
            mm.then_inc(fold_pe, 1)
            pe.wait_ge(fold_sb, 7)
            pe.wait_ge(fold_bias, 1)

            pe.wait_ge(xt_evac, 1)
            for h in range(HP):
                project_qk(0, 0, h)
            project_gate(0, 0)
            sums_of_squares(0, 1)
            project_values(0, 0)
            spread_norms(0, 0)

            def body(b, first=False, last=False):
                for p, P, has_prev, has_next in slots(b, first, last):
                    par = p % 2
                    prev_p, next_p = (p - 1) % NP, (p + 1) % NP
                    scores(par, P, 0)
                    if has_prev:
                        transposes_of_k(1 - par, P - 1, 0)
                        transposes_of_k(1 - par, P - 1, 1)
                    scores(par, P, 1)
                    if has_next:
                        if p == NP - 1:
                            pe.wait_ge(xt_evac, b + 2)
                        project_qk(next_p, P + 1, 0)
                    scores(par, P, 2)
                    if has_next:
                        project_qk(next_p, P + 1, 1)
                    scores(par, P, 3)
                    if has_prev:
                        state_updates(1 - par, P - 1, 0)
                    if has_next:
                        project_gate(next_p, P + 1)
                    if has_prev:
                        state_updates(1 - par, P - 1, 1)
                    scores(par, P, 4)
                    if has_prev:
                        outputs(prev_p, P - 1, b if p else b - 1, 0)
                    scores(par, P, 5)
                    if has_next:
                        sums_of_squares(P + 1, b + 2 if p == NP - 1 else b + 1)
                    if has_prev:
                        outputs(prev_p, P - 1, b if p else b - 1, 1)
                    scores(par, P, 6)
                    if has_next:
                        project_values(next_p, P + 1)
                        spread_norms(1 - par, P + 1)
                    scores(par, P, 7)
                    if p == NP - 2 and not last:
                        transposes_of_x(b + 1)

            body(0, first=True)
            with pe.Fori(1, B - 1) as b:
                body(b)
            body(B - 1, last=True)
            P = B * NP - 1
            for h in range(HP):
                last_transposes_of_k(P % 2, P, h)
            for h in range(HP):
                state_updates(P % 2, P, h)
            for h in range(HP):
                outputs(NP - 1, P, B - 1, h)

            def head_x(n):
                pe.wait_ge(nat_in, (n + 1) * 16)
                for c in range(NC):
                    mm = nc.tensor.transpose(h0_ps[:, c * C:(c + 1) * C], x_nat[:, c, :], ident[:, :])
                mm.then_inc(f_x1T, 1)

            def head_z(n):
                pe.wait_ge(a_x1T, n + 1)
                await_count(pe, v_h, n - 1)
                nc.tensor.matmul(h0_ps[:, :], swf[:, 0, 0:D], x1T[:, :], start=True, stop=True)
                nc.tensor.matmul(h1_ps[:, :], swf[:, 0, D:2 * D], x1T[:, :], start=True, stop=True).then_inc(f_z, 1)

            def head_gate(n, par):
                pe.wait_ge(v_xt, n + 1)
                for c in range(NC):
                    mm = nc.tensor.matmul(h0_ps[:, c * E:(c + 1) * E], xt_sb[par][:, c * C:(c + 1) * C], gate_t[:, :],
                                          start=True, stop=True)
                mm.then_inc(f_gate, 1)

            def up(n, par, e):
                k = n * NE + e
                await_count(pe, a_sg, k - 1)
                nc.tensor.matmul(g_ps[e % 2][:, :], ew1[:, e, :], xt_sb[par][:, :], start=True, stop=True).then_inc(f_g, 1)
                await_count(pe, v_gu, k - 1)
                nc.tensor.matmul(u_ps[e % 2][:, :], ew3[:, e, :], xt_sb[par][:, :], start=True, stop=True).then_inc(f_u, 1)
                if e < E:
                    if e == 0:
                        pe.wait_ge(v_comb, n + 1)
                        await_count(pe, v_gu, n * NE - 2)
                    else:
                        pe.wait_ge(v_gu, k)
                    for c in range(NC):
                        mm = nc.tensor.transpose(cb_ps[:, c * C:(c + 1) * C],
                                                 comb[par][:, c, e:e + 1].to_broadcast([128, 128]), ident[:, :])
                    mm.then_inc(f_cb, 1)

            def down(n, e):
                pe.wait_ge(v_gu, n * NE + e + 1)
                if e == 0:
                    await_count(pe, a_r, n)
                nc.tensor.matmul(r_ps[:, :], ew2[:, e, :], gc[e % 2][:, :], start=e == 0, stop=e == NE - 1).then_inc(f_down, 1)

            def tail_z(n):
                pe.wait_ge(a_r, n + 1)
                nc.tensor.matmul(h0_ps[:, :], swf[:, 1, 0:D], r_sb[:, :], start=True, stop=True)
                nc.tensor.matmul(h1_ps[:, :], swf[:, 1, D:2 * D], r_sb[:, :], start=True, stop=True).then_inc(f_zo, 1)

            def tail_h(n):
                pe.wait_ge(v_h, n + 1)
                for c in range(NC):
                    mm = nc.tensor.transpose(h0_ps[:, c * C:(c + 1) * C], h_sb[:, c * C:(c + 1) * C], ident[:, :])
                mm.then_inc(f_hT, 1)

            def ffn(b, first=False, last=False):
                for par in range(2):
                    n = b + par
                    has_prev = not (first and par == 0)
                    has_next = not (last and par == 1)
                    for e in range(NE):
                        up(n, par, e)
                        if e == 0 and has_prev:
                            down(n - 1, NE - 1)
                        if e > 0:
                            down(n, e - 1)
                        if e == 2 and has_prev:
                            pe.wait_ge(v_lg, n + 1)
                            tail_z(n - 1)
                        if e == 3 and has_prev:
                            tail_h(n - 1)
                        if e == 5 and has_next:
                            if has_prev:
                                pe.wait_ge(res_done, B + n)
                            else:
                                pe.wait_ge(v_lg, 1)
                            head_x(n + 1)
                        if e == 6 and has_next:
                            head_z(n + 1)
                        if e == 7 and has_next:
                            head_gate(n + 1, 1 - par)

            pe.wait_ge(res_done, B)
            head_x(0)
            head_z(0)
            head_gate(0, 0)
            pe.wait_ge(s_done, B * NP * HP * (NC - 1))
            pe.wait_ge(kt_evac, B * NP * HP)
            ffn(0, first=True)
            with pe.Fori(1, B // 2 - 1) as i:
                ffn(2 * i)
            ffn(B - 2, last=True)
            down(B - 1, NE - 1)
            tail_z(B - 1)
            tail_h(B - 1)

        @block.scalar
        def _(act):
            def take_xT(n):
                act.wait_ge(xt_full, n + 1)
                await_count(act, pj_full, n * NP * 8)
                nc.scalar.activation(xT[:, :], nb_ps[:, :], ACT.Copy).then_inc(xt_evac, 1)

            def take_qk(par, P, h):
                for i, dst in enumerate((q_sb, k_sb)):
                    act.wait_ge(pj_full, P * 8 + 2 * h + i + 1)
                    if h == 0 and i == 0:
                        await_count(act, qk_full, (P - 1) * STEPS)
                        await_count(act, kt_full, (P - 1) * HP)
                    nc.scalar.activation(dst[par][:, h * T:(h + 1) * T], pj[i][:, :], ACT.Copy).then_inc(pj_evac, 1)

            def take_gate(par, P):
                for h in range(HP):
                    act.wait_ge(pj_full, P * 8 + 5 + h)
                    if h == 0:
                        await_count(act, q1_done, (P - 1) * 2)
                        await_count(act, k_up, (P - 1) * 7)
                        await_count(act, tot_done, (P - 1) * 7)
                    nc.scalar.activation(a_sb[par][:, h * T:(h + 1) * T], pj[h][:, :], ACT.Sigmoid).then_inc(pj_evac, 1)

            def take_values(par, P):
                act.wait_ge(rn_done, P + 1)
                await_count(act, av_done, (P - 1) * HP)
                for n in range(2):
                    act.wait_ge(pj_full, P * 8 + 7 + n)
                    for i in range(2):
                        for h in range(HP):
                            c = 2 * n + i
                            at = (i * HP + h) * D
                            last = nc.scalar.activation(v_sb[par][:, c, h * D:(h + 1) * D], pj[n][:, at:at + D],
                                                        ACT.Copy, scale=rn_sb[par][:, 1, h, c:c + 1])
                    last.then_inc(pj_evac, 1)

            def take_kT(P, h):
                act.wait_ge(kt_full, P * HP + h + 1)
                await_count(act, su_full, (P - 1) * HP + h + 1)
                nc.scalar.activation(kt_sb[:, h, :, :].rearrange("p c k -> p (c k)"), kt_ps[:, 0:(NC - 1) * C],
                                     ACT.Copy).then_inc(kt_evac, 1)

            def take_scores_32(par, P):
                act.wait_ge(qk_full, P * STEPS + 7)
                act.wait_ge(sc_evac, P * 6 + 6)
                s = sc[0][:, :].rearrange("p (g t) -> p g t", t=64)
                nc.scalar.activation(at_sb[par][0:32, :, 32:64], s[0:32, :, 0:32], ACT.Copy).then_inc(sc_act, 1)
                nc.scalar.activation(at_sb[par][64:96, :, 96:128], s[64:96, :, 32:64], ACT.Copy).then_inc(sc_act, 1)

            def take_scores_64(par, P):
                act.wait_ge(qk_full, P * STEPS + 8)
                s = sc[1][:, :].rearrange("p (g t) -> p g t", t=64)
                nc.scalar.activation(at_sb[par][0:64, :, 64:128], s[0:64, :, :], ACT.Copy).then_inc(sc_act, 1)

            for n in range(2):
                act.wait_ge(fold_pe, n + 1)
                nc.scalar.activation(sq_sb[:, 0, n, :], pj[n][:, :], ACT.Copy).then_inc(fold_sb, 1)
            act.wait_ge(fold_pe, 3)
            nc.scalar.activation(s1[:, 0:2 * D], sc[0][:, 0:2 * D], ACT.Copy).then_inc(fold_sb, 1)
            nc.scalar.activation(gate_t[:, :], sc[0][:, 2 * D:2 * D + E], ACT.Copy).then_inc(fold_sb, 1)
            take_xT(0)
            for n in range(2):
                act.wait_ge(fold_pe, n + 5)
                nc.scalar.activation(wvo[:, n * 4 * D:(n + 1) * 4 * D], pj[n][:, :], ACT.Copy).then_inc(fold_sb, 1)
            act.wait_ge(fold_pe, 7)
            nc.scalar.activation(swf[:, :, :].rearrange("p i n -> p (i n)"), sc[0][:, :], ACT.Copy).then_inc(fold_sb, 1)

            for h in range(HP):
                take_qk(0, 0, h)
            take_gate(0, 0)
            take_values(0, 0)

            def body(b, first=False, last=False):
                for p, P, has_prev, has_next in slots(b, first, last):
                    par = p % 2
                    if has_prev:
                        take_kT(P - 1, 0)
                        take_kT(P - 1, 1)
                    if has_next:
                        for h in range(HP):
                            take_qk(1 - par, P + 1, h)
                        take_gate(1 - par, P + 1)
                    take_scores_32(par, P)
                    if has_next:
                        take_values(1 - par, P + 1)
                    take_scores_64(par, P)
                    if p == NP - 2 and not last:
                        take_xT(b + 1)

            body(0, first=True)
            with act.Fori(1, B - 1) as b:
                body(b)
            body(B - 1, last=True)
            for h in range(HP):
                take_kT(B * NP - 1, h)

            def head_x(n):
                act.wait_ge(f_x1T, n + 1)
                await_count(act, f_z, n)
                nc.scalar.activation(x1T[:, :], h0_ps[:, :], ACT.Copy).then_inc(a_x1T, 1)

            def head_z(n):
                act.wait_ge(f_z, n + 1)
                await_count(act, v_xt, n)
                nc.scalar.activation(s1[:, :], h0_ps[:, :], ACT.Silu, bias=swf_b[:, 0:1]).then_inc(a_s1, 1)

            def exp_logits(n):
                act.wait_ge(v_lg, n + 1)
                await_count(act, v_comb, n)
                nc.scalar.activation(ex[:, :, :], lg[:, :, :], ACT.Exp).then_inc(a_ex, 1)

            def silu_expert(n, e):
                k = n * NE + e
                act.wait_ge(f_g, k + 1)
                await_count(act, v_gu, k - 1)
                nc.scalar.activation(sg[e % 2][:, :], g_ps[e % 2][:, :], ACT.Silu).then_inc(a_sg, 1)

            def take_r(n):
                act.wait_ge(f_down, (n + 1) * NE)
                await_count(act, f_zo, n)
                nc.scalar.activation(r_sb[:, :], r_ps[:, :], ACT.Copy).then_inc(a_r, 1)

            def tail_z(n):
                act.wait_ge(f_zo, n + 1)
                await_count(act, v_h, n)
                nc.scalar.activation(s2[:, :], h0_ps[:, :], ACT.Silu, bias=swf_b[:, 2:3]).then_inc(a_s2, 1)

            def ffn(b, first=False, last=False):
                for par in range(2):
                    n = b + par
                    has_prev = not (first and par == 0)
                    has_next = not (last and par == 1)
                    for e in range(NE):
                        silu_expert(n, e)
                        if e == 0 and has_prev:
                            take_r(n - 1)
                        if e == 2 and has_prev:
                            tail_z(n - 1)
                        if e == 5 and has_next:
                            head_x(n + 1)
                        if e == 6 and has_next:
                            head_z(n + 1)
                        if e == 8 and has_next:
                            exp_logits(n + 1)

            act.wait_ge(fold_bias, 1)
            head_x(0)
            head_z(0)
            exp_logits(0)
            ffn(0, first=True)
            with act.Fori(1, B // 2 - 1) as i:
                ffn(2 * i)
            ffn(B - 2, last=True)
            take_r(B - 1)
            tail_z(B - 1)

        @block.vector
        def _(dve):
            def block_products(par, P):
                dve.wait_ge(pj_evac, P * 8 + 6)
                m, n = 1, 0
                while m < C:
                    if m > 1:
                        dve.wait_ge(tot_done, P * 7 + n)
                    src = tot(par, m).rearrange("p (n two) -> p n two", two=2)
                    nc.vector.tensor_tensor(tot(par, 2 * m), src[:, :, 0], src[:, :, 1], ALU.mult).then_inc(tot_done, 1)
                    m, n = 2 * m, n + 1

            def normalise_q(par, P):
                for h, bank in enumerate((nb_ps, kt_ps)):
                    dve.wait_ge(rb_full, P * HP + h + 1)
                    seg = q_sb[par][:, h * T:(h + 1) * T]
                    nc.vector.tensor_tensor(seg, seg, bank[:, :], ALU.mult).then_inc(qn_done, 1)

            def first_q(par, P):
                await_count(dve, av_done, (P - 1) * HP)
                dve.wait_ge(qn_done, (P + 1) * HP)
                dve.wait_ge(tot_done, P * 7 + 1)
                nc.vector.tensor_tensor(qd_sb[par][:, 0::2], q_sb[par][:, 0::2], a_sb[par][:, 0::2], ALU.mult).then_inc(q1_done, 1)
                nc.vector.tensor_tensor(qd_sb[par][:, 1::2], q_sb[par][:, 1::2], tot(par, 2), ALU.mult).then_inc(q1_done, 1)

            def grow(par, m, which):
                side = 1 if which == "q" else 0
                buf = (qd_sb if which == "q" else k_sb)[par]
                view = halves(buf[:, :], m)[:, :, side, :]
                by = tot(par, m).rearrange("p (n two) -> p n two", two=2)[:, :, 1 - side:2 - side]
                if 2 * m == C:
                    lo = 1 if which == "q" else 0
                    view = view.rearrange("p (h c) m -> p h c m", h=HP)[:, :, lo:lo + NC - 1, :]
                    by = by.rearrange("p (h c) o -> p h c o", h=HP)[:, :, lo:lo + NC - 1, :]
                    by = by.to_broadcast([128, HP, NC - 1, m])
                elif m > 1:
                    by = by.to_broadcast([128, W // (2 * m), m])
                return nc.vector.tensor_tensor(view, view, by, ALU.mult)

            def keep_scores(par, j):
                s = sc[j % 2][:, :].rearrange("p (g t) -> p g t", t=64)
                if j < 2:
                    mask = ident[:, 0::2] if j == 0 else mask_odd[:, :]
                    return nc.vector.tensor_tensor(at_sb[par][:, :, j::2], s,
                                                   mask.rearrange("p (o t) -> p o t", o=1).to_broadcast([128, G, 64]), ALU.mult)
                m = HALF[j]
                dst = at_sb[par][:, :, :].rearrange("p g (n two m) -> p (g n) two m", two=2, m=m)[:, :, 1, :]
                mask = mask_half[:, j - 2, :].rearrange("p (o t) -> p o t", o=1).to_broadcast([128, G, 64])
                return dst, mask, s, m

            def take_scores(par, P, j):
                if j == 0:
                    await_count(dve, av_done, (P - 1) * HP)
                if j < 2:
                    keep_scores(par, j).then_inc(sc_evac, 1)
                else:
                    m = HALF[j]
                    dst = at_sb[par][:, :, :].rearrange("p g (n two m) -> p g n two m", two=2, m=m)[:, :, :, 1, :]
                    mask = mask_half[:, j - 2, :].rearrange("p (o n m) -> p o n m", o=1, m=m)\
                        .to_broadcast([128, G, 64 // m, m]).bitcast(i32)
                    data = sc[j % 2][:, :].rearrange("p (g n m) -> p g n m", g=G, m=m)
                    nc.vector.copy_predicated(dst, mask, data).then_inc(sc_evac, 1)

            def states(par, P, h):
                dve.wait_ge(su_full, P * HP + h + 1)
                await_count(dve, av_done, (P - 1) * HP + h + 1)
                n = (P * HP + h) * (NC - 1)
                nc.vector.tensor_copy(s_sb[:, h, 0, :], su_ps[:, 0:D]).then_inc(s_done, 1)
                for c in range(1, NC - 1):
                    dve.wait_ge(s_done, n + c)
                    whole = tot(par, C)[:, h * NC + c:h * NC + c + 1]
                    nc.vector.scalar_tensor_tensor(out=s_sb[:, h, c, :], in0=s_sb[:, h, c - 1, :], scalar=whole,
                                                   in1=su_ps[:, c * D:(c + 1) * D], op0=ALU.mult, op1=ALU.add).then_inc(s_done, 1)

            def clamp_sums(P):
                dve.wait_ge(ss_full, P + 1)
                await_count(dve, rn_done, P)
                nc.vector.tensor_scalar(ss_sb[:, :], nb_ps[:, 0:16], L2_EPS * L2_EPS, None, ALU.max).then_inc(ss_evac, 1)

            def ln_stats(n, y, resid):
                await_count(dve, x1_done, n)
                nc.vector.tensor_tensor(res[:, :, :], y, resid, ALU.add).then_inc(res_done, 1)
                dve.wait_ge(res_done, n + 1)
                for c in range(NC):
                    nc.vector.bn_stats(stats[:, c, :], res[:, c, :]).then_inc(ln_chain, 1)
                step = n * (NC + 6) + NC
                dve.wait_ge(ln_chain, step)
                nc.vector.tensor_tensor(lt[:, 0, :], stats[:, :, 1], stats[:, :, 4], ALU.add).then_inc(ln_chain, 1)
                nc.vector.tensor_tensor(lt[:, 1, :], stats[:, :, 1], stats[:, :, 4], ALU.subtract).then_inc(ln_chain, 1)
                nc.vector.tensor_tensor(lt[:, 2, :], stats[:, :, 2], stats[:, :, 5], ALU.add).then_inc(ln_chain, 1)
                dve.wait_ge(ln_chain, step + 3)
                nc.vector.tensor_scalar(mean[:, :], lt[:, 0, :], 0.5, None, ALU.mult).then_inc(ln_chain, 1)
                nc.vector.scalar_tensor_tensor(out=lt[:, 3, :], in0=lt[:, 1, :], scalar=0.25, in1=lt[:, 1, :],
                                               op0=ALU.mult, op1=ALU.mult).then_inc(ln_chain, 1)
                nc.vector.tensor_scalar(lt[:, 4, :], lt[:, 2, :], 1.0 / D, LN_EPS, ALU.mult, ALU.add).then_inc(ln_chain, 1)
                dve.wait_ge(ln_chain, step + 6)
                await_count(dve, rstd_done, n)
                nc.vector.tensor_tensor(ve[:, :], lt[:, 3, :], lt[:, 4, :], ALU.add).then_inc(ve_done, 1)

            def ln_apply(n, dst):
                dve.wait_ge(rstd_done, n + 1)
                for c in range(NC):
                    last = nc.vector.tensor_scalar(dst(c), res[:, c, :], mean[:, c:c + 1], rstd[:, c:c + 1],
                                                   ALU.subtract, ALU.mult)
                last.then_inc(x1_done, 1)

            y3 = y_ps[:, :].rearrange("p (c d) -> p c d", c=NC)

            def x_rows(b):
                return x_all[:, bass.ds(b * NC, NC), :]

            def ln1_stats(b):
                dve.wait_ge(av_done, (b + 1) * NP * HP)
                ln_stats(b, y3, x_rows(b))

            def ln1_apply(b):
                ln_apply(b, lambda c: x_all[:, bass.ds(b * NC + c, 1), :].rearrange("p o d -> p (o d)"))

            dve.wait_ge(const_pool, CONST_POOL)
            nc.vector.tensor_tensor(mask_odd[:, :], ident[:, 0::2], ident[:, 1::2], ALU.add).then_inc(const_dve, 1)
            dve.wait_ge(fold_pe, 4)
            nc.vector.tensor_tensor(swf_b[:, :], swi_b[:, :], sc[1][:, 0:4], ALU.add).then_inc(fold_bias, 1)
            dve.wait_ge(x_in, X_ALL)
            dve.wait_ge(const_dve, 1)

            clamp_sums(0)
            block_products(0, 0)
            normalise_q(0, 0)
            first_q(0, 0)

            def body(b, first=False, last=False):
                for p, P, has_prev, has_next in slots(b, first, last):
                    par = p % 2
                    qk = P * STEPS
                    dve.wait_ge(qk_full, qk + 1)
                    grow(par, 1, "k").then_inc(k_up, 1)
                    take_scores(par, P, 0)
                    dve.wait_ge(qk_full, qk + 2)
                    take_scores(par, P, 1)
                    for j in range(2, 7):
                        dve.wait_ge(qk_full, qk + j + 1)
                        if j < 6:
                            dve.wait_ge(sc_evac, P * 6 + j)
                        grow(par, HALF[j], "q").then_inc(q_up, 1)
                        grow(par, HALF[j], "k").then_inc(k_up, 1)
                        if j < 6:
                            take_scores(par, P, j)
                        if j == 3 and has_prev:
                            states(1 - par, P - 1, 0)
                            states(1 - par, P - 1, 1)
                        if j == 4 and p == 1 and not first:
                            ln1_apply(b - 1)
                        if j == 5 and has_next:
                            clamp_sums(P + 1)
                    if has_next:
                        normalise_q(1 - par, P + 1)
                        block_products(1 - par, P + 1)
                    dve.wait_ge(qk_full, qk + 8)
                    grow(par, HALF[7], "k").then_inc(k_up, 1)
                    grow(par, HALF[7], "q").then_inc(q_up, 1)
                    if has_next:
                        first_q(1 - par, P + 1)
                    if p == 0 and has_prev:
                        ln1_stats(b - 1)

            body(0, first=True)
            with dve.Fori(1, B - 1) as b:
                body(b)
            body(B - 1, last=True)
            P = B * NP - 1
            for h in range(HP):
                states(P % 2, P, h)
            ln1_stats(B - 1)
            ln1_apply(B - 1)

            def head_z(n, par):
                dve.wait_ge(a_s1, n + 1)
                await_count(dve, f_u, (n - 1) * NE)
                nc.vector.scalar_tensor_tensor(out=xt_sb[par][:, :], in0=h1_ps[:, :], scalar=swf_b[:, 1:2], in1=s1[:, :],
                                               op0=ALU.add, op1=ALU.mult).then_inc(v_xt, 1)

            TOP = 9

            def logits(n):
                dve.wait_ge(f_gate, n + 1)
                g3 = h0_ps[:, 0:NC * E].rearrange("p (c e) -> p c e", e=E)
                nc.vector.tensor_reduce(lmax[:, :], g3, axis=AX.X, op=ALU.max).then_inc(v_top, 1)
                dve.wait_ge(v_top, n * TOP + 1)
                await_count(dve, a_ex, n)
                nc.vector.tensor_tensor(lg[:, :, :], g3, lmax[:, :].rearrange("p (c o) -> p c o", o=1).to_broadcast([128, NC, E]),
                                        ALU.subtract).then_inc(v_lg, 1)

            def choose(n, par):
                four = lambda t: t[:, :, :].rearrange("p (c e) j -> p c e j", e=E)
                of_j = ex[:, :, :].rearrange("p c (o j) -> p c o j", o=1).to_broadcast([128, NC, E, E])
                of_e = ex[:, :, :].rearrange("p c (e o) -> p c e o", o=1).to_broadcast([128, NC, E, E])
                first_of = earlier[:, :, :].rearrange("p (o e) j -> p o e j", o=1).to_broadcast([128, NC, E, E])
                top = n * TOP
                dve.wait_ge(a_ex, n + 1)
                nc.vector.tensor_tensor(four(gt), of_j, of_e, ALU.is_gt).then_inc(v_top, 1)
                nc.vector.tensor_tensor(four(eq), of_j, of_e, ALU.is_equal).then_inc(v_top, 1)
                dve.wait_ge(v_top, top + 3)
                nc.vector.tensor_tensor(four(eqe), four(eq), first_of, ALU.mult).then_inc(v_top, 1)
                dve.wait_ge(v_top, top + 4)
                nc.vector.tensor_tensor(four(gt), four(gt), four(eqe), ALU.add).then_inc(v_top, 1)
                dve.wait_ge(v_top, top + 5)
                nc.vector.tensor_reduce(rank[:, :, :], four(gt), axis=AX.X, op=ALU.add).then_inc(v_top, 1)
                dve.wait_ge(v_top, top + 6)
                nc.vector.scalar_tensor_tensor(out=picked[:, :, :], in0=rank[:, :, :], scalar=float(TOPK), in1=ex[:, :, :],
                                               op0=ALU.is_lt, op1=ALU.mult).then_inc(v_top, 1)
                dve.wait_ge(v_top, top + 7)
                nc.vector.tensor_reduce(den[:, :], picked[:, :, :], axis=AX.X, op=ALU.add).then_inc(v_top, 1)
                dve.wait_ge(v_top, top + 8)
                nc.vector.reciprocal(rden[:, :], den[:, :]).then_inc(v_top, 1)
                dve.wait_ge(v_top, top + 9)
                await_count(dve, f_cb, (n - 1) * E)
                nc.vector.tensor_tensor(comb[par][:, :, :], picked[:, :, :],
                                        rden[:, :].rearrange("p (c o) -> p c o", o=1).to_broadcast([128, NC, E]),
                                        ALU.mult).then_inc(v_comb, 1)

            def gate_expert(n, e):
                k = n * NE + e
                dve.wait_ge(a_sg, k + 1)
                dve.wait_ge(f_u, k + 1)
                await_count(dve, f_down, k - 1)
                if e < E:
                    nc.vector.tensor_tensor(gu[e % 2][:, :], sg[e % 2][:, :], u_ps[e % 2][:, :], ALU.mult).then_inc(v_mid, 1)
                    dve.wait_ge(f_cb, n * E + e + 1)
                    dve.wait_ge(v_mid, n * E + e + 1)
                    nc.vector.tensor_tensor(gc[e % 2][:, :], gu[e % 2][:, :], cb_ps[:, :], ALU.mult).then_inc(v_gu, 1)
                else:
                    nc.vector.tensor_tensor(gc[e % 2][:, :], sg[e % 2][:, :], u_ps[e % 2][:, :], ALU.mult).then_inc(v_gu, 1)

            def tail_z(n):
                dve.wait_ge(a_s2, n + 1)
                await_count(dve, f_hT, n)
                nc.vector.scalar_tensor_tensor(out=h_sb[:, :], in0=h1_ps[:, :], scalar=swf_b[:, 3:4], in1=s2[:, :],
                                               op0=ALU.add, op1=ALU.mult).then_inc(v_h, 1)

            def ln2(n, par):
                dve.wait_ge(f_hT, n + 1)
                ln_stats(B + n, h0_ps[:, :].rearrange("p (c d) -> p c d", c=NC), x_rows(n))

            def ln2_out(n, par):
                await_count(dve, out_done, (n - 1) * 16)
                ln_apply(B + n, lambda c: o_sb[par][:, c, :])

            def ffn(b, first=False, last=False):
                for par in range(2):
                    n = b + par
                    has_prev = not (first and par == 0)
                    has_next = not (last and par == 1)
                    for e in range(NE):
                        gate_expert(n, e)
                        if e == 2 and has_prev:
                            tail_z(n - 1)
                        if e == 4 and has_prev:
                            ln2(n - 1, 1 - par)
                        if e == 5 and has_prev:
                            ln2_out(n - 1, 1 - par)
                        if e == 6 and has_next:
                            head_z(n + 1, 1 - par)
                        if e == 7 and has_next:
                            logits(n + 1)
                        if e == 8 and has_next:
                            choose(n + 1, 1 - par)

            head_z(0, 0)
            logits(0)
            choose(0, 0)
            ffn(0, first=True)
            with dve.Fori(1, B // 2 - 1) as i:
                ffn(2 * i)
            ffn(B - 2, last=True)
            tail_z(B - 1)
            ln2(B - 1, 1)
            ln2_out(B - 1, 1)


_INS = ["L0_attn_x", "L0_attn_Wq", "L0_attn_Wk", "L0_attn_Wv", "L0_attn_Wg", "L0_attn_Wo",
        "L0_ffn_lin0_w", "L0_ffn_lin0_b", "L0_ffn_swi1_w1", "L0_ffn_swi1_b1", "L0_ffn_swi1_w2", "L0_ffn_swi1_b2",
        "L0_ffn_gate_w", "L0_ffn_exp_w1", "L0_ffn_exp_w3", "L0_ffn_exp_w2", "L0_ffn_sh_w1", "L0_ffn_sh_w3",
        "L0_ffn_sh_w2", "L0_ffn_lin1_w", "L0_ffn_lin1_b", "L0_ffn_swi2_w1", "L0_ffn_swi2_b1", "L0_ffn_swi2_w2",
        "L0_ffn_swi2_b2"]


def kernel(**inputs):
    import numpy as _np
    import concourse.bacc as _bacc
    from concourse import mybir as _mybir
    from concourse.bass_utils import run_bass_kernel_spmd as _run

    nc = _bacc.Bacc("TRN2", target_bir_lowering=False, num_devices=1)
    arrays, args = {}, []
    for name in _INS:
        a = _np.ascontiguousarray(inputs[name])
        arrays[f"in_{name}_dram"] = a
        args.append(nc.dram_tensor(f"in_{name}_dram", a.shape, _mybir.dt.from_np(a.dtype), kind="ExternalInput").ap())
    shape = inputs["L0_attn_x"].shape
    out = nc.dram_tensor("out_0_dram", shape, _mybir.dt.from_np(_np.dtype("float32")), kind="ExternalOutput").ap()
    gated_linear_attention_and_moe_block(nc, *args, out)
    r = _run(nc, [arrays], core_ids=[0])
    return r.results[0]["out_0_dram"]
```

```python
import concourse.bass as bass
from concourse import mybir
from contextlib import ExitStack


def gated_linear_attention_and_moe_block(
    nc: bass.Bass,
    x: bass.AP,
    Wq: bass.AP,
    Wk: bass.AP,
    Wv: bass.AP,
    Wg: bass.AP,
    Wo: bass.AP,
    lin0_w: bass.AP,
    lin0_b: bass.AP,
    swi1_w1: bass.AP,
    swi1_b1: bass.AP,
    swi1_w2: bass.AP,
    swi1_b2: bass.AP,
    gate_w: bass.AP,
    exp_w1: bass.AP,
    exp_w3: bass.AP,
    exp_w2: bass.AP,
    sh_w1: bass.AP,
    sh_w3: bass.AP,
    sh_w2: bass.AP,
    lin1_w: bass.AP,
    lin1_b: bass.AP,
    swi2_w1: bass.AP,
    swi2_b1: bass.AP,
    swi2_w2: bass.AP,
    swi2_b2: bass.AP,
    out: bass.AP,
):
    fp32 = mybir.dt.float32
    f32r = mybir.dt.float32r
    bf16 = mybir.dt.bfloat16
    i32 = mybir.dt.int32
    ALU = mybir.AluOpType
    ACT = mybir.ActivationFunctionType
    AX = mybir.AxisListType

    B, T, D = x.shape
    H = Wq.shape[1] // D
    C = 128
    NC = T // C
    HP = 2
    NP = H // HP
    G = HP * NC
    W = HP * T
    E, _, FH = exp_w1.shape
    NS = sh_w1.shape[1] // FH
    NE = E + NS
    TOPK = 4
    LN_EPS = 1e-5
    L2_EPS = 1e-12
    STEPS = 8
    SS = 32
    HALF = {j: 2 ** (j - 1) for j in range(2, STEPS)}

    ctx = ExitStack()
    with ctx:
        def sb(name, shape, dt=fp32):
            return ctx.enter_context(nc.sbuf_tensor(name, shape, dt))

        def sem(name):
            return ctx.enter_context(nc.semaphore(name))

        banks = [ctx.enter_context(nc.psum_tensor(f"bank{n}", [128, 512], fp32)) for n in range(8)]

        wq, wk, wg, wvo = ([sb(f"{n}_{part}", [128, H * D], f32r) for part in ("hi", "lo")]
                           for n in ("wq", "wk", "wg", "wvo"))
        ew1, ew3 = ([sb(f"{n}_{part}", [128, NE * FH], f32r) for part in ("hi", "lo")] for n in ("ew1", "ew3"))
        swf = [sb(f"swf_{part}", [128, 2 * 2 * D], f32r) for part in ("hi", "lo")]
        ew2 = sb("ew2", [128, NE, D])
        gate_rows = sb("gate_rows", [E, D])
        gate_t = sb("gate_t", [128, C])
        lin_b = sb("lin_b", [128, 2])
        swi_b = sb("swi_b", [128, 4])
        swf_b = sb("swf_b", [128, 4])
        ident = sb("ident", [128, 128])
        ones = sb("ones", [128, SS], bf16)
        ones_wide = sb("ones_wide", [128, 128])
        mask_odd = sb("mask_odd", [128, 64])
        mask_half = sb("mask_half", [128, 4, 64])
        earlier = sb("earlier", [128, E, E])
        expo = sb("expo", [128, 16])

        x_all = sb("x_all", [128, B * NC, D])
        x_nat = sb("x_nat", [128, NC, D])
        xT = [sb(f"xT_{part}", [128, T], f32r) for part in ("hi", "lo")]

        qq_sb = [sb(f"qq_sb{i}", [128, 2, W]) for i in range(2)]
        q_sb = [t[:, 0, :] for t in qq_sb]
        qd_sb = [t[:, 1, :] for t in qq_sb]
        e_sb = sb("e_sb", [128, W // 2])
        k_sb = [sb(f"k_sb{i}", [128, W]) for i in range(2)]
        a_sb = [sb(f"a_sb{i}", [128, W]) for i in range(2)]
        tot_sb = [sb(f"tot_sb{i}", [128, W]) for i in range(2)]
        at_sb = [sb(f"at_sb{i}", [128, G, C]) for i in range(2)]
        v_sb = [sb(f"v_sb{i}", [128, NC, HP * D]) for i in range(2)]
        sq_sb = sb("sq_sb", [128, 2, T])
        sq_hi = sb("sq_hi", [128, 2 * HP, T], bf16)
        sq_lo = sb("sq_lo", [128, 2 * HP, T], bf16)
        kt_sb = sb("kt_sb", [128, HP, NC - 1, 128])
        s_sb = sb("s_sb", [128, HP, NC - 1, D])
        ss_sb = sb("ss_sb", [128, 16])
        rn_sb = [sb(f"rn_sb{i}", [128, 2, HP, NC]) for i in range(2)]

        raw = {"wq": q_sb[0], "wk": q_sb[1], "wg": k_sb[0]}
        wv_raw = k_sb[1]
        wvT = a_sb[0]
        linT = a_sb[1]
        wo = qd_sb[0][:, :].rearrange("p (h d) -> p h d", h=H)
        lin = qd_sb[1][:, 0:2 * D].rearrange("p (i d) -> p i d", i=2)
        swi = qd_sb[1][:, 2 * D:6 * D].rearrange("p (i n) -> p i n", i=2)

        res = sb("res", [128, NC, D])
        stats = sb("stats", [128, NC, 6])
        lt = sb("lt", [128, 5, NC])
        mean = sb("mean", [128, NC])
        ve = sb("ve", [128, NC])
        rstd = sb("rstd", [128, NC])

        x1T = xT
        xt_sb = [[sb(f"xt{i}_{part}", [128, T], f32r) for part in ("hi", "lo")] for i in range(2)]
        r_sb = [sb(f"r_{part}", [128, T], f32r) for part in ("hi", "lo")]
        xt32 = k_sb[1][:, 0:T]
        comb = [sb(f"comb{i}", [128, NC, E]) for i in range(2)]
        lg = sb("lg", [128, NC, E])
        lmax = sb("lmax", [128, NC])
        ex = sb("ex", [128, NC, E])
        gt, eq, eqe = (qd_sb[0][:, n * NC * E * E:(n + 1) * NC * E * E].rearrange("p (t j) -> p t j", j=E) for n in range(3))
        rank = sb("rank", [128, NC, E])
        picked = sb("picked", [128, NC, E])
        den = sb("den", [128, NC])
        rden = sb("rden", [128, NC])
        work = sb("work", [128, 6 * T])
        sg, gu, gc = ([work[:, (2 * n + i) * T:(2 * n + i + 1) * T] for i in range(2)] for n in range(3))
        ew1_raw, ew3_raw = (work[:, i * NE * FH:(i + 1) * NE * FH] for i in range(2))
        s2, h_sb = (q_sb[0][:, i * T:(i + 1) * T] for i in range(2))
        s1 = q_sb[1][:, 0:T]
        o_sb = [k_sb[0][:, i * T:(i + 1) * T].rearrange("p (c d) -> p c d", c=NC) for i in range(2)]

        pj = [banks[0], banks[1]]
        sc = [banks[2], banks[3]]
        y_ps = banks[4]
        nb_ps = banks[5]
        kt_ps = banks[6]
        su_ps = banks[7]
        g_ps = [banks[0], banks[1]]
        u_ps = [banks[2], banks[3]]
        h0_ps = banks[4]
        h1_ps = banks[5]
        cb_ps = banks[6]
        r_ps = banks[7]

        w_in = sem("w_in")
        x_in = sem("x_in")
        xn_in = sem("xn_in")
        const_pool = sem("const_pool")
        const_dve = sem("const_dve")
        fold_pe = sem("fold_pe")
        fold_sb = sem("fold_sb")
        fold_bias = sem("fold_bias")
        w_hi = sem("w_hi")
        w_lo = sem("w_lo")
        e_hi = sem("e_hi")
        e_lo = sem("e_lo")
        x_lo = sem("x_lo")
        sq_mul = sem("sq_mul")
        sq_top = sem("sq_top")
        pj_full = sem("pj_full")
        pj_evac = sem("pj_evac")
        xt_full = sem("xt_full")
        xt_evac = sem("xt_evac")
        sq_done = sem("sq_done")
        ss_full = sem("ss_full")
        ss_evac = sem("ss_evac")
        rn_done = sem("rn_done")
        rb_full = sem("rb_full")
        qn_done = sem("qn_done")
        q1_done = sem("q1_done")
        e_done = sem("e_done")
        k_up = sem("k_up")
        q_up = sem("q_up")
        tot_done = sem("tot_done")
        qk_full = sem("qk_full")
        sc_evac = sem("sc_evac")
        sc_act = sem("sc_act")
        kt_full = sem("kt_full")
        kt_evac = sem("kt_evac")
        su_full = sem("su_full")
        s_done = sem("s_done")
        av_done = sem("av_done")
        res_done = sem("res_done")
        ln_chain = sem("ln_chain")
        ve_done = sem("ve_done")
        rstd_done = sem("rstd_done")
        x1_done = sem("x1_done")
        out_done = [sem(f"out_done{i}") for i in range(2)]
        nat_in = sem("nat_in")
        f_x1T = sem("f_x1T")
        f_z = sem("f_z")
        f_gate = sem("f_gate")
        f_g = sem("f_g")
        f_u = sem("f_u")
        f_cb = sem("f_cb")
        f_down = sem("f_down")
        f_zo = sem("f_zo")
        f_hT = sem("f_hT")
        a_x1T = sem("a_x1T")
        a_s1 = sem("a_s1")
        a_ex = sem("a_ex")
        a_sg = sem("a_sg")
        a_r = sem("a_r")
        a_xt = sem("a_xt")
        v_x1T = sem("v_x1T")
        v_xt32 = sem("v_xt32")
        v_r = sem("v_r")
        a_s2 = sem("a_s2")
        v_xt = sem("v_xt")
        v_lg = sem("v_lg")
        v_comb = sem("v_comb")
        v_top = sem("v_top")
        v_gu = sem("v_gu")
        v_mid = sem("v_mid")
        v_h = sem("v_h")

        block = ctx.enter_context(nc.Block())

        def await_count(eng, s, count):
            if not (isinstance(count, int) and count <= 0):
                eng.wait_ge(s, count)

        def halves(ap, m):
            return ap.rearrange("p (n two m) -> p n two m", two=2, m=m)

        def tot(par, m):
            if m == 1:
                return a_sb[par][:, :]
            at = W - 2 * W // m
            return tot_sb[par][:, at:at + W // m]

        def block_product(eng, ops, par, P, n):
            m = 2 ** n
            if n == 0:
                eng.wait_ge(pj_evac, P * 8 + 6)
            else:
                eng.wait_ge(tot_done, P * 7 + n)
            src = tot(par, m).rearrange("p (n two) -> p n two", two=2)
            ops.tensor_tensor(tot(par, 2 * m), src[:, :, 0], src[:, :, 1], ALU.mult).then_inc(tot_done, 1)

        def even_odd(ap):
            v = ap.rearrange("p (n k i) -> p n k i", k=2, i=2)
            return v[:, :, 0, :], v[:, :, 1, :]

        def pairs_of(ap):
            v = ap.rearrange("p (n i k) -> p n i k", k=2, i=2)
            return v[:, :, :, 0], v[:, :, :, 1]

        def bank_of_step(j):
            return sc[(j + 1) % 2]

        def slots(b, first, last):
            for p in range(NP):
                yield p, b * NP + p, not (first and p == 0), not (last and p == NP - 1)


        @block.sync
        def _(sp):
            sp.dma_start(x_nat[:, :, :], x[0].rearrange("(c t) d -> t c d", t=C)).then_inc(xn_in, 16)
            for name, w in (("wq", Wq), ("wk", Wk), ("wg", Wg)):
                sp.dma_start(raw[name][:, :], w).then_inc(w_in, 16)
            sp.dma_start(wv_raw[:, :], Wv).then_inc(w_in, 16)
            sp.dma_start(wo[:, :, :], Wo.rearrange("(h v) d -> v h d", v=D)).then_inc(w_in, 16)
            sp.dma_start(lin[:, 0, :], lin0_w).then_inc(w_in, 16)
            sp.dma_start(lin[:, 1, :], lin1_w).then_inc(w_in, 16)
            sp.dma_start(swi[:, 0, 0:D], swi1_w1).then_inc(w_in, 16)
            sp.dma_start(swi[:, 0, D:2 * D], swi1_w2).then_inc(w_in, 16)
            sp.dma_start(swi[:, 1, 0:D], swi2_w1).then_inc(w_in, 16)
            sp.dma_start(swi[:, 1, D:2 * D], swi2_w2).then_inc(w_in, 16)
            sp.dma_start(gate_rows[:, :], gate_w).then_inc(w_in, 16)
            for n, bias in enumerate((lin0_b, lin1_b)):
                sp.dma_start(lin_b[:, n:n + 1], bias.rearrange("(p a) -> p a", a=1)).then_inc(w_in, 16)
            for n, bias in enumerate((swi1_b1, swi1_b2, swi2_b1, swi2_b2)):
                sp.dma_start(swi_b[:, n:n + 1], bias.rearrange("(p a) -> p a", a=1)).then_inc(w_in, 16)
            sp.dma_start(x_all[:, :, :], x.rearrange("b (c t) d -> t (b c) d", t=C)).then_inc(x_in, 16)
            for dst, routed, shared in ((ew1_raw, exp_w1, sh_w1), (ew3_raw, exp_w3, sh_w3)):
                sp.dma_start(dst[:, 0:E * FH].rearrange("p (e f) -> p e f", e=E), routed.rearrange("e d f -> d e f")).then_inc(x_in, 16)
                sp.dma_start(dst[:, E * FH:NE * FH], shared).then_inc(x_in, 16)
            sp.dma_start(ew2[:, 0:E, :], exp_w2.rearrange("e f d -> f e d")).then_inc(x_in, 16)
            sp.dma_start(ew2[:, E:NE, :], sh_w2.rearrange("(n f) d -> f n d", f=FH)).then_inc(x_in, 16)

            def next_x(b):
                sp.wait_ge(xt_full, b)
                sp.dma_start(x_nat[:, :, :], x[bass.ds(b, 1)].rearrange("a (c t) d -> t (a c) d", t=C)).then_inc(xn_in, 16)

            with sp.Fori(1, B) as b:
                next_x(b)

            def ffn_io(b, first=False, last=False):
                for par in range(2):
                    n = b + par
                    if not (first and par == 0):
                        sp.wait_ge(f_x1T, n)
                    sp.dma_start(x_nat[:, :, :], x_all[:, bass.ds(n * NC, NC), :]).then_inc(nat_in, 16)
                    if not first:
                        store(n - 2, par)

            def store(n, par):
                sp.wait_ge(x1_done, B + n + 1)
                sp.dma_start(out[bass.ds(n, 1)].rearrange("a (c t) d -> t (a c) d", t=C), o_sb[par][:, :, :]).then_inc(out_done[par], 16)

            sp.wait_ge(x1_done, B)
            sp.wait_ge(xt_full, B)
            ffn_io(0, first=True)
            with sp.Fori(1, B // 2) as i:
                ffn_io(2 * i)
            store(B - 2, 0)
            store(B - 1, 1)
            for par in range(2):
                sp.wait_ge(out_done[par], 16 * B // 2)

        W_ALL = 18 * 16
        X_ALL = 7 * 16

        def pool_setup(pool):
            nc.gpsimd.memset(ident[:, :], 0.0).then_inc(const_pool, 1)
            nc.gpsimd.memset(ones[:, :], 1.0).then_inc(const_pool, 1)
            nc.gpsimd.memset(ones_wide[:, :], 1.0).then_inc(const_pool, 1)
            nc.gpsimd.memset(mask_half[:, :, :], 1.0).then_inc(const_pool, 1)
            nc.gpsimd.memset(earlier[:, :, :], 1.0).then_inc(const_pool, 1)
            nc.gpsimd.memset(expo[:, :], -0.5).then_inc(const_pool, 1)
            nc.gpsimd.memset(gate_t[:, :], 0.0).then_inc(const_pool, 1)
            pool.wait_ge(const_pool, 7)
            nc.gpsimd.affine_select(out=ident[:, :], in_=ident[:, :], compare_op=ALU.not_equal, fill=1.0,
                                    base=0, pattern=[[-1, 128]], channel_multiplier=1).then_inc(const_pool, 1)
            nc.gpsimd.affine_select(out=earlier[:, :, :], in_=earlier[:, :, :], compare_op=ALU.is_ge, fill=0.0,
                                    base=-1, pattern=[[1, E], [-1, E]], channel_multiplier=0).then_inc(const_pool, 1)
            for i, m in enumerate((2, 4, 8, 16)):
                view = mask_half[:, i, :].rearrange("p (n m) -> p n m", m=m)
                nc.gpsimd.affine_select(out=view, in_=view, compare_op=ALU.is_ge, fill=0.0,
                                        base=0, pattern=[[-2 * m, 64 // m], [0, m]], channel_multiplier=1).then_inc(const_pool, 1)
            pool.wait_ge(const_pool, 13)
            for i, m in enumerate((2, 4, 8, 16)):
                view = mask_half[:, i, :].rearrange("p (n m) -> p n m", m=m)
                nc.gpsimd.affine_select(out=view, in_=view, compare_op=ALU.is_ge, fill=0.0,
                                        base=m - 1, pattern=[[2 * m, 64 // m], [0, m]], channel_multiplier=-1).then_inc(const_pool, 1)

        CONST_POOL = 17

        @block.gpsimd
        def _(pool):
            pool_setup(pool)

            def norms(par, P):
                await_count(pool, ss_full, P * 2)
                for n in range(2 * HP + 1):
                    if n < 2 * HP:
                        pool.wait_ge(pj_evac, P * 8 + n + 1)
                        seg = (q_sb, k_sb)[n // HP][par][:, (n % HP) * T:(n % HP + 1) * T]
                        await_count(pool, sq_done, P * 4 + n - 1)
                        nc.gpsimd.tensor_tensor(sq_sb[:, n % 2, :], seg, seg, ALU.mult).then_inc(sq_mul, 1)
                    if n > 0:
                        pool.wait_ge(sq_mul, P * 4 + n)
                        pool.wait_ge(sq_top, P * 4 + n)
                        nc.gpsimd.tensor_tensor(sq_lo[:, n - 1, :], sq_sb[:, (n - 1) % 2, :], sq_hi[:, n - 1, :],
                                                ALU.subtract).then_inc(sq_done, 1)
                await_count(pool, q1_done, (P - 1) * 3)
                await_count(pool, k_up, (P - 1) * 6)
                await_count(pool, q_up, (P - 1) * 6)
                await_count(pool, s_done, (P - 1) * HP * (NC - 1))
                for i in range(2):
                    pool.wait_ge(ss_evac, P * 2 + i + 1)
                    nc.gpsimd.tensor_tensor(rn_sb[par][:, i, :, :].rearrange("p h c -> p (h c)"), ss_sb[:, i * G:(i + 1) * G],
                                            expo[:, 0:G], ALU.pow).then_inc(rn_done, 1)
                    block_product(pool, nc.gpsimd, par, P, i)

            def ln_rstd(n):
                pool.wait_ge(ve_done, n + 1)
                nc.gpsimd.tensor_tensor(rstd[:, :], ve[:, :], expo[:, 0:NC], ALU.pow).then_inc(rstd_done, 1)

            def body(b, first=False, last=False):
                for p, P, has_prev, has_next in slots(b, first, last):
                    if has_next:
                        norms((p + 1) % 2, P + 1)
                    if p == 1 and not first:
                        ln_rstd(b - 1)

            norms(0, 0)
            body(0, first=True)
            with pool.Fori(1, B - 1) as b:
                body(b)
            body(B - 1, last=True)
            ln_rstd(B - 1)

            with pool.Fori(0, B) as b:
                ln_rstd(b + B)

        @block.tensor
        def _(pe):
            def transposes_of_x(n):
                pe.wait_ge(xn_in, (n + 1) * 16)
                await_count(pe, qn_done, n * NP * HP - 1)
                for c in range(NC):
                    mm = nc.tensor.transpose(nb_ps[:, c * C:(c + 1) * C], x_nat[:, c, :], ident[:, :])
                mm.then_inc(xt_full, 1)

            def bank_of(P, n):
                await_count(pe, pj_evac, P * 8 + n - 1)
                return pj[n % 2]

            def three_passes(out_ap, stat, mov, start=True, stop=True):
                nc.tensor.matmul(out_ap, stat(0), mov(0), start=start, stop=False)
                nc.tensor.matmul(out_ap, stat(0), mov(1), start=False, stop=False)
                return nc.tensor.matmul(out_ap, stat(1), mov(0), start=False, stop=stop)

            def project(p, P, w, n):
                bank = bank_of(P, n)
                col = (p * HP + n % HP) * D
                if n < HP:
                    three_passes(bank[:, :].rearrange("p (n k i) -> p n k i", k=2, i=2), lambda i: w[i][:, col:col + D],
                                 lambda i: xT[i][:, :].rearrange("p (n i k) -> p n k i", k=2, i=2)).then_inc(pj_full, 1)
                else:
                    three_passes(bank[:, :], lambda i: w[i][:, col:col + D], lambda i: xT[i][:, :]).then_inc(pj_full, 1)

            def project_values(p, P, n):
                bank = bank_of(P, 6 + n)
                for i in range(2):
                    c = 2 * n + i
                    mm = three_passes(bank[:, i * HP * D:(i + 1) * HP * D], lambda k: xT[k][:, c * C:(c + 1) * C],
                                      lambda k: wvo[k][:, p * HP * D:(p + 1) * HP * D])
                mm.then_inc(pj_full, 1)

            def sums_of_squares(P, i, n_x):
                pe.wait_ge(sq_done, P * 4 + (i + 1) * HP)
                if i == 0:
                    pe.wait_ge(xt_evac, n_x)
                    pe.wait_ge(x_lo, n_x)
                    await_count(pe, qn_done, P * HP)
                else:
                    await_count(pe, s_done, (P - 1) * HP * (NC - 1))
                for h in range(HP):
                    for c in range(NC):
                        col = (h * NC + c) * SS
                        for part, sq in enumerate((sq_hi, sq_lo)):
                            mm = nc.tensor.matmul((nb_ps, su_ps)[i][:, col:col + SS], sq[:, i * HP + h, c * C:(c + 1) * C],
                                                  ones[:, :], start=part == 0, stop=part == 1)
                mm.then_inc(ss_full, 1)

            def spread_norms(par, P):
                pe.wait_ge(rn_done, P * 2 + 1)
                await_count(pe, s_done, (P - 1) * HP * (NC - 1))
                for h, bank in enumerate((nb_ps, kt_ps)):
                    for c in range(NC):
                        mm = nc.tensor.transpose(bank[:, c * C:(c + 1) * C],
                                                 rn_sb[par][:, 0, h, c:c + 1].to_broadcast([128, 128]), ident[:, :])
                    mm.then_inc(rb_full, 1)

            def scores(par, P, j):
                bank = bank_of_step(j)
                if j == 0:
                    await_count(pe, sc_act, P * 3 - 1)
                    pe.wait_ge(e_done, P + 1)
                    nc.tensor.matmul(bank[:, :], ones_wide[:, :], e_sb[:, :], start=True, stop=True).then_inc(qk_full, 1)
                    return
                if j < 3:
                    if j == 1:
                        await_count(pe, sc_act, P * 3)
                    else:
                        pe.wait_ge(sc_evac, P * 8 + 1)
                    pe.wait_ge(q1_done, 3 * (P + 1))
                    for c in range(NC):
                        lo = (j - 1) * T + c * C
                        moving = qq_sb[par][:, :, lo:lo + C].rearrange("p w (n two m) -> p w n two m", two=2, m=2)[:, :, :, 1, :]
                        mm = nc.tensor.matmul(bank[:, c * C:(c + 1) * C].rearrange("p (w n m) -> p w n m", w=2, m=2),
                                              k_sb[par][:, lo:lo + C], moving, start=True, stop=True)
                    mm.then_inc(qk_full, 1)
                    return
                pe.wait_ge(sc_evac, P * 8 + j + 1)
                pe.wait_ge(k_up, P * 6 + j - 2)
                pe.wait_ge(q_up, P * 6 + j - 2)
                for g in range(G):
                    lo = g * C
                    if j < 6:
                        mm = nc.tensor.matmul(bank[:, g * 64:(g + 1) * 64], k_sb[par][:, lo:lo + C],
                                              halves(qd_sb[par][:, lo:lo + C], HALF[j])[:, :, 1, :], start=True, stop=True)
                        continue
                    m = HALF[j]
                    for n in range(64 // m):
                        left = lo + 2 * m * n
                        mm = nc.tensor.matmul(bank[2 * m * n:2 * m * n + m, g * 64 + m * n:g * 64 + m * (n + 1)],
                                              k_sb[par][:, left:left + m], qd_sb[par][:, left + m:left + 2 * m],
                                              start=True, stop=True)
                mm.then_inc(qk_full, 1)

            def transposes_of_k(par, P, h, last=False):
                if h == 0:
                    pe.wait_ge(k_up, (P + 1) * 6)
                    if not last:
                        pe.wait_ge(qn_done, (P + 2) * HP)
                else:
                    pe.wait_ge(kt_evac, P * HP + 1)
                for c in range(NC - 1):
                    lo = h * T + c * C
                    mm = nc.tensor.transpose(kt_ps[:, c * C:(c + 1) * C], k_sb[par][:, lo:lo + C], ident[:, :])
                mm.then_inc(kt_full, 1)

            def state_updates(par, P, h):
                pe.wait_ge(kt_evac, P * HP + h + 1)
                pe.wait_ge(pj_evac, (P + 1) * 8)
                if h == 0:
                    await_count(pe, s_done, P * HP * (NC - 1))
                    pe.wait_ge(ss_evac, 2 * (P + 1))
                for c in range(NC - 1):
                    mm = nc.tensor.matmul((su_ps, kt_ps)[h][:, c * D:(c + 1) * D], kt_sb[:, h, c, :],
                                          v_sb[par][:, c, h * D:(h + 1) * D], start=True, stop=True)
                mm.then_inc(su_full, 1)

            def outputs(p, P, b, h):
                par = p % 2
                pe.wait_ge(sc_evac, (P + 1) * 8)
                pe.wait_ge(sc_act, (P + 1) * 3)
                pe.wait_ge(s_done, (P + 1) * HP * (NC - 1))
                pe.wait_ge(q_up, (P + 1) * 6)
                if p == 0 and h == 0:
                    await_count(pe, res_done, b)
                for c in range(NC):
                    first_mm = p == 0 and h == 0 and c == 0
                    last_mm = p == NP - 1 and h == HP - 1 and c == NC - 1
                    y = y_ps[:, c * D:(c + 1) * D]
                    mm = nc.tensor.matmul(y, at_sb[par][:, h * NC + c, :], v_sb[par][:, c, h * D:(h + 1) * D],
                                          start=first_mm, stop=last_mm and c == 0, skip_group_check=True)
                    if c > 0:
                        lo = h * T + c * C
                        mm = nc.tensor.matmul(y, qd_sb[par][:, lo:lo + C], s_sb[:, h, c - 1, :],
                                              start=False, stop=last_mm, skip_group_check=True)
                mm.then_inc(av_done, 1)

            pe.wait_ge(const_pool, CONST_POOL)
            transposes_of_x(0)
            pe.wait_ge(w_in, W_ALL)
            for n in range(2):
                for i in range(4):
                    h = 4 * n + i
                    mm = nc.tensor.transpose(pj[n][:, i * D:(i + 1) * D], wv_raw[:, h * D:(h + 1) * D], ident[:, :])
                mm.then_inc(fold_pe, 1)
            for i in range(2):
                nc.tensor.transpose(sc[0][:, i * D:(i + 1) * D], lin[:, i, :], ident[:, :])
            nc.tensor.transpose(sc[0][:, 2 * D:2 * D + E], gate_rows[:, :], ident[0:E, 0:E]).then_inc(fold_pe, 1)
            for i in range(2):
                for n in range(2):
                    mm = nc.tensor.matmul(sc[1][:, 2 * i + n:2 * i + n + 1], swi[:, i, n * D:(n + 1) * D],
                                          lin_b[:, i:i + 1], start=True, stop=True)
            mm.then_inc(fold_pe, 1)
            pe.wait_ge(fold_sb, 4)
            for n in range(2):
                for i in range(4):
                    h = 4 * n + i
                    mm = nc.tensor.matmul(pj[n][:, i * D:(i + 1) * D],
                                          wvT[:, (n * 4 + i) * D:(n * 4 + i + 1) * D], wo[:, h, :], start=True, stop=True)
                mm.then_inc(fold_pe, 1)
            for i in range(2):
                mm = nc.tensor.matmul(sc[0][:, i * 2 * D:(i + 1) * 2 * D], linT[:, i * D:(i + 1) * D], swi[:, i, :],
                                      start=True, stop=True)
            mm.then_inc(fold_pe, 1)
            pe.wait_ge(w_lo, 6)
            pe.wait_ge(fold_bias, 1)

            pe.wait_ge(xt_evac, 1)
            pe.wait_ge(x_lo, 1)
            for n in range(3 * HP):
                project(0, 0, (wq, wk, wg)[n // HP], n)
            for i in range(2):
                sums_of_squares(0, i, 1)
            spread_norms(0, 0)
            for n in range(2):
                project_values(0, 0, n)
            scores(0, 0, 0)

            def body(b, first=False, last=False):
                for p, P, has_prev, has_next in slots(b, first, last):
                    par = p % 2
                    prev_p, next_p = (p - 1) % NP, (p + 1) % NP
                    n_x = b + 2 if p == NP - 1 else b + 1
                    if has_next and p < NP - 1:
                        project(next_p, P + 1, wq, 0)
                    scores(par, P, 1)
                    scores(par, P, 2)
                    if has_next and p == NP - 1:
                        pe.wait_ge(xt_evac, n_x)
                        pe.wait_ge(x_lo, n_x)
                        project(next_p, P + 1, wq, 0)
                    if has_prev:
                        transposes_of_k(1 - par, P - 1, 0)
                    if has_next:
                        project(next_p, P + 1, wq, 1)
                    if has_prev:
                        transposes_of_k(1 - par, P - 1, 1)
                    if has_next:
                        project(next_p, P + 1, wk, 2)
                    scores(par, P, 3)
                    if has_prev:
                        state_updates(1 - par, P - 1, 0)
                        state_updates(1 - par, P - 1, 1)
                    if has_next:
                        project(next_p, P + 1, wk, 3)
                    scores(par, P, 4)
                    if has_next:
                        project(next_p, P + 1, wg, 4)
                        sums_of_squares(P + 1, 0, n_x)
                        project(next_p, P + 1, wg, 5)
                    scores(par, P, 5)
                    if has_prev:
                        outputs(prev_p, P - 1, b if p else b - 1, 0)
                    if has_next:
                        sums_of_squares(P + 1, 1, n_x)
                        spread_norms(1 - par, P + 1)
                    scores(par, P, 6)
                    if has_prev:
                        outputs(prev_p, P - 1, b if p else b - 1, 1)
                    if has_next:
                        project_values(next_p, P + 1, 0)
                        project_values(next_p, P + 1, 1)
                    if p == NP - 2 and not last:
                        transposes_of_x(b + 1)
                    scores(par, P, 7)
                    if has_next:
                        scores(1 - par, P + 1, 0)

            body(0, first=True)
            with pe.Fori(1, B - 1) as b:
                body(b)
            body(B - 1, last=True)
            P = B * NP - 1
            for h in range(HP):
                transposes_of_k(P % 2, P, h, last=True)
            for h in range(HP):
                state_updates(P % 2, P, h)
            for h in range(HP):
                outputs(NP - 1, P, B - 1, h)

            def head_x(n):
                pe.wait_ge(nat_in, (n + 1) * 16)
                for c in range(NC):
                    mm = nc.tensor.transpose(h0_ps[:, c * C:(c + 1) * C], x_nat[:, c, :], ident[:, :])
                mm.then_inc(f_x1T, 1)

            def head_z(n):
                pe.wait_ge(a_x1T, n + 1)
                pe.wait_ge(v_x1T, n + 1)
                await_count(pe, v_h, n - 1)
                three_passes(h0_ps[:, :], lambda i: swf[i][:, 0:D], lambda i: x1T[i][:, :])
                three_passes(h1_ps[:, :], lambda i: swf[i][:, D:2 * D], lambda i: x1T[i][:, :]).then_inc(f_z, 1)

            def head_gate(n, par):
                pe.wait_ge(v_xt32, n + 1)
                for c in range(NC):
                    mm = nc.tensor.matmul(h0_ps[:, c * C:(c + 1) * C], xt32[:, c * C:(c + 1) * C], gate_t[:, :],
                                          start=True, stop=True)
                mm.then_inc(f_gate, 1)

            def up(n, par, e):
                k = n * NE + e
                await_count(pe, a_sg, k - 1)
                if e == 0:
                    pe.wait_ge(a_xt, n + 1)
                    pe.wait_ge(v_xt, n + 1)
                three_passes(g_ps[e % 2][:, :], lambda i: ew1[i][:, e * FH:(e + 1) * FH],
                             lambda i: xt_sb[par][i][:, :]).then_inc(f_g, 1)
                await_count(pe, v_gu, k - 1)
                three_passes(u_ps[e % 2][:, :], lambda i: ew3[i][:, e * FH:(e + 1) * FH],
                             lambda i: xt_sb[par][i][:, :]).then_inc(f_u, 1)
                if e < E:
                    if e == 0:
                        pe.wait_ge(v_comb, n + 1)
                        await_count(pe, v_gu, n * NE - 2)
                    else:
                        pe.wait_ge(v_gu, k)
                    for c in range(NC):
                        mm = nc.tensor.transpose(cb_ps[:, c * C:(c + 1) * C],
                                                 comb[par][:, c, e:e + 1].to_broadcast([128, 128]), ident[:, :])
                    mm.then_inc(f_cb, 1)

            def down(n, e):
                pe.wait_ge(v_gu, n * NE + e + 1)
                if e == 0:
                    await_count(pe, a_r, n)
                    await_count(pe, v_r, n)
                nc.tensor.matmul(r_ps[:, :], ew2[:, e, :], gc[e % 2], start=e == 0, stop=e == NE - 1).then_inc(f_down, 1)

            def tail_z(n):
                pe.wait_ge(a_r, n + 1)
                pe.wait_ge(v_r, n + 1)
                three_passes(h0_ps[:, :], lambda i: swf[i][:, 2 * D:3 * D], lambda i: r_sb[i][:, :])
                three_passes(h1_ps[:, :], lambda i: swf[i][:, 3 * D:4 * D], lambda i: r_sb[i][:, :]).then_inc(f_zo, 1)

            def tail_h(n):
                pe.wait_ge(v_h, n + 1)
                for c in range(NC):
                    mm = nc.tensor.transpose(h0_ps[:, c * C:(c + 1) * C], h_sb[:, c * C:(c + 1) * C], ident[:, :])
                mm.then_inc(f_hT, 1)

            def ffn(b, first=False, last=False):
                for par in range(2):
                    n = b + par
                    has_prev = not (first and par == 0)
                    has_next = not (last and par == 1)
                    for e in range(NE):
                        up(n, par, e)
                        if e == 0 and has_prev:
                            down(n - 1, NE - 1)
                        if e > 0:
                            down(n, e - 1)
                        if e == 1 and has_prev:
                            pe.wait_ge(v_lg, n + 1)
                            tail_z(n - 1)
                        if e == 2 and has_prev:
                            tail_h(n - 1)
                        if e == 4 and has_next:
                            if has_prev:
                                pe.wait_ge(res_done, B + n)
                            else:
                                pe.wait_ge(v_lg, 1)
                            head_x(n + 1)
                        if e == 5 and has_next:
                            head_z(n + 1)
                        if e == 7 and has_next:
                            head_gate(n + 1, 1 - par)

            pe.wait_ge(res_done, B)
            head_x(0)
            head_z(0)
            head_gate(0, 0)
            pe.wait_ge(s_done, B * NP * HP * (NC - 1))
            pe.wait_ge(kt_evac, B * NP * HP)
            pe.wait_ge(e_lo, 2)
            ffn(0, first=True)
            with pe.Fori(1, B // 2 - 1) as i:
                ffn(2 * i)
            ffn(B - 2, last=True)
            down(B - 1, NE - 1)
            tail_z(B - 1)
            tail_h(B - 1)

        @block.scalar
        def _(act):
            def take_xT(n):
                act.wait_ge(xt_full, n + 1)
                await_count(act, pj_full, n * NP * 8)
                nc.scalar.activation(xT[0][:, :], nb_ps[:, :], ACT.Copy).then_inc(xt_evac, 1)

            def take_tile(par, P, n):
                act.wait_ge(pj_full, P * 8 + n + 1)
                if n == 0:
                    await_count(act, qk_full, (P - 1) * STEPS)
                if n == HP:
                    await_count(act, kt_full, (P - 1) * HP)
                dst = (q_sb, k_sb)[n // HP][par]
                nc.scalar.activation(dst[:, (n % HP) * T:(n % HP + 1) * T], pj[n % 2][:, :], ACT.Copy).then_inc(pj_evac, 1)

            def square(par, P, n):
                act.wait_ge(pj_evac, P * 8 + n + 1)
                await_count(act, ss_full, P * 2)
                src = (q_sb, k_sb)[n // HP][par]
                nc.scalar.activation(sq_hi[:, n, :], src[:, (n % HP) * T:(n % HP + 1) * T], ACT.Square).then_inc(sq_top, 1)

            def take_gate(par, P):
                for h in range(HP):
                    act.wait_ge(pj_full, P * 8 + 5 + h)
                    if h == 0:
                        await_count(act, q1_done, (P - 1) * 3)
                        await_count(act, k_up, (P - 1) * 6)
                        await_count(act, tot_done, (P - 1) * 7)
                    nc.scalar.activation(a_sb[par][:, h * T:(h + 1) * T], pj[h][:, :], ACT.Sigmoid).then_inc(pj_evac, 1)

            def take_values(par, P, n):
                act.wait_ge(rn_done, (P + 1) * 2)
                await_count(act, av_done, (P - 1) * HP)
                act.wait_ge(pj_full, P * 8 + 7 + n)
                for i in range(2):
                    for h in range(HP):
                        c = 2 * n + i
                        at = (i * HP + h) * D
                        last = nc.scalar.activation(v_sb[par][:, c, h * D:(h + 1) * D], pj[n][:, at:at + D],
                                                    ACT.Copy, scale=rn_sb[par][:, 1, h, c:c + 1])
                last.then_inc(pj_evac, 1)

            def take_kT(P, h):
                act.wait_ge(kt_full, P * HP + h + 1)
                await_count(act, su_full, (P - 1) * HP + h + 1)
                nc.scalar.activation(kt_sb[:, h, :, :].rearrange("p c k -> p (c k)"), kt_ps[:, 0:(NC - 1) * C],
                                     ACT.Copy).then_inc(kt_evac, 1)

            def first_states(P):
                act.wait_ge(su_full, (P + 1) * HP)
                await_count(act, av_done, P * HP)
                for h in range(HP):
                    nc.scalar.activation(s_sb[:, h, 0, :], (su_ps, kt_ps)[h][:, 0:D], ACT.Copy).then_inc(s_done, 1)

            def take_scores_32(par, P):
                act.wait_ge(qk_full, P * STEPS + 7)
                act.wait_ge(sc_evac, (P + 1) * 8)
                s = bank_of_step(6)[:, :].rearrange("p (g t) -> p g t", t=64)
                nc.scalar.activation(at_sb[par][0:32, :, 32:64], s[0:32, :, 0:32], ACT.Copy).then_inc(sc_act, 1)
                nc.scalar.activation(at_sb[par][64:96, :, 96:128], s[64:96, :, 32:64], ACT.Copy).then_inc(sc_act, 1)

            def take_scores_64(par, P):
                act.wait_ge(qk_full, P * STEPS + 8)
                s = bank_of_step(7)[:, :].rearrange("p (g t) -> p g t", t=64)
                nc.scalar.activation(at_sb[par][0:64, :, 64:128], s[0:64, :, :], ACT.Copy).then_inc(sc_act, 1)

            act.wait_ge(w_in, W_ALL)
            for n in range(2):
                act.wait_ge(fold_pe, n + 1)
                nc.scalar.activation(wvT[:, n * 4 * D:(n + 1) * 4 * D], pj[n][:, :], ACT.Copy).then_inc(fold_sb, 1)
            act.wait_ge(fold_pe, 3)
            nc.scalar.activation(linT[:, 0:2 * D], sc[0][:, 0:2 * D], ACT.Copy).then_inc(fold_sb, 1)
            nc.scalar.activation(gate_t[:, 0:E], sc[0][:, 2 * D:2 * D + E], ACT.Copy).then_inc(fold_sb, 1)
            take_xT(0)
            for w, name in ((wq, "wq"), (wk, "wk"), (wg, "wg")):
                nc.scalar.activation(w[0][:, :], raw[name][:, :], ACT.Copy).then_inc(w_hi, 1)
            for n in range(2):
                act.wait_ge(fold_pe, n + 5)
                nc.scalar.activation(wvo[0][:, n * 4 * D:(n + 1) * 4 * D], pj[n][:, :], ACT.Copy).then_inc(w_hi, 1)
            act.wait_ge(fold_pe, 7)
            nc.scalar.activation(swf[0][:, :], sc[0][:, :], ACT.Copy).then_inc(w_hi, 1)

            act.wait_ge(w_lo, 6)
            for n in range(2 * HP):
                take_tile(0, 0, n)
                square(0, 0, n)
            take_gate(0, 0)
            for n in range(2):
                take_values(0, 0, n)
            act.wait_ge(x_in, X_ALL)
            for w, src in ((ew1, ew1_raw), (ew3, ew3_raw)):
                nc.scalar.activation(w[0][:, :], src, ACT.Copy).then_inc(e_hi, 1)

            def body(b, first=False, last=False):
                for p, P, has_prev, has_next in slots(b, first, last):
                    par = p % 2
                    if has_next:
                        take_tile(1 - par, P + 1, 0)
                        square(1 - par, P + 1, 0)
                    if has_prev:
                        take_kT(P - 1, 0)
                    if has_next:
                        take_tile(1 - par, P + 1, 1)
                    if has_prev:
                        take_kT(P - 1, 1)
                    if has_next:
                        square(1 - par, P + 1, 1)
                        take_tile(1 - par, P + 1, 2)
                        square(1 - par, P + 1, 2)
                    if has_prev:
                        first_states(P - 1)
                    if has_next:
                        take_tile(1 - par, P + 1, 3)
                        square(1 - par, P + 1, 3)
                        take_gate(1 - par, P + 1)
                    take_scores_32(par, P)
                    if has_next:
                        take_values(1 - par, P + 1, 0)
                        take_values(1 - par, P + 1, 1)
                    if p == NP - 2 and not last:
                        take_xT(b + 1)
                    take_scores_64(par, P)

            body(0, first=True)
            with act.Fori(1, B - 1) as b:
                body(b)
            body(B - 1, last=True)
            for h in range(HP):
                take_kT(B * NP - 1, h)
            first_states(B * NP - 1)

            def head_x(n):
                act.wait_ge(f_x1T, n + 1)
                await_count(act, f_z, n)
                nc.scalar.activation(x1T[0][:, :], h0_ps[:, :], ACT.Copy).then_inc(a_x1T, 1)

            def head_z(n):
                act.wait_ge(f_z, n + 1)
                await_count(act, v_xt32, n)
                nc.scalar.activation(s1, h0_ps[:, :], ACT.Silu, bias=swf_b[:, 0:1]).then_inc(a_s1, 1)

            def head_xt(n, par):
                act.wait_ge(v_xt32, n + 1)
                await_count(act, f_u, (n - 1) * NE)
                nc.scalar.activation(xt_sb[par][0][:, :], xt32, ACT.Copy).then_inc(a_xt, 1)

            def exp_logits(n):
                act.wait_ge(v_lg, n + 1)
                await_count(act, v_comb, n)
                nc.scalar.activation(ex[:, :, :], lg[:, :, :], ACT.Exp).then_inc(a_ex, 1)

            def silu_expert(n, e):
                k = n * NE + e
                act.wait_ge(f_g, k + 1)
                await_count(act, v_gu, k - 1)
                nc.scalar.activation(sg[e % 2], g_ps[e % 2][:, :], ACT.Silu).then_inc(a_sg, 1)

            def take_r(n):
                act.wait_ge(f_down, (n + 1) * NE)
                await_count(act, f_zo, n)
                nc.scalar.activation(r_sb[0][:, :], r_ps[:, :], ACT.Copy).then_inc(a_r, 1)

            def tail_z(n):
                act.wait_ge(f_zo, n + 1)
                await_count(act, v_h, n)
                nc.scalar.activation(s2, h0_ps[:, :], ACT.Silu, bias=swf_b[:, 2:3]).then_inc(a_s2, 1)

            def ffn(b, first=False, last=False):
                for par in range(2):
                    n = b + par
                    has_prev = not (first and par == 0)
                    has_next = not (last and par == 1)
                    for e in range(NE):
                        silu_expert(n, e)
                        if e == 0 and has_prev:
                            take_r(n - 1)
                        if e == 1 and has_prev:
                            tail_z(n - 1)
                        if e == 4 and has_next:
                            head_x(n + 1)
                        if e == 5 and has_next:
                            head_z(n + 1)
                        if e == 7 and has_next:
                            head_xt(n + 1, 1 - par)
                        if e == 8 and has_next:
                            exp_logits(n + 1)

            act.wait_ge(fold_bias, 1)
            head_x(0)
            head_z(0)
            head_xt(0, 0)
            exp_logits(0)
            ffn(0, first=True)
            with act.Fori(1, B // 2 - 1) as i:
                ffn(2 * i)
            ffn(B - 2, last=True)
            take_r(B - 1)
            tail_z(B - 1)

        @block.vector
        def _(dve):
            def normalise_q(par, P, h):
                dve.wait_ge(rb_full, P * HP + h + 1)
                seg = q_sb[par][:, h * T:(h + 1) * T]
                nc.vector.tensor_tensor(seg, seg, (nb_ps, kt_ps)[h][:, :], ALU.mult).then_inc(qn_done, 1)

            def low_xT(n):
                dve.wait_ge(xt_evac, n + 1)
                nc.vector.tensor_tensor(xT[1][:, :], nb_ps[:, :], xT[0][:, :].bitcast(fp32), ALU.subtract).then_inc(x_lo, 1)

            def own_products(par, P):
                dve.wait_ge(qn_done, (P + 1) * HP)
                await_count(dve, qk_full, (P - 1) * STEPS + 1)
                nc.vector.tensor_tensor(e_sb[:, :].rearrange("p (n i) -> p n i", i=2), even_odd(q_sb[par])[0],
                                        pairs_of(k_sb[par][:, :])[0], ALU.mult).then_inc(e_done, 1)

            def first_growth(par, P):
                dve.wait_ge(tot_done, P * 7 + 1)
                grow(par, 1, "k").then_inc(q1_done, 1)
                await_count(dve, av_done, (P - 1) * HP)
                for odd in range(2):
                    by = pairs_of(a_sb[par][:, :])[0] if odd == 0 else \
                        tot(par, 2).rearrange("p (n i) -> p n i", i=2)
                    nc.vector.tensor_tensor(pairs_of(qd_sb[par])[odd], even_odd(q_sb[par])[odd], by, ALU.mult).then_inc(q1_done, 1)

            def grow(par, m, which):
                side = 1 if which == "q" else 0
                buf = (qd_sb if which == "q" else k_sb)[par]
                view = halves(buf[:, :], m)[:, :, side, :]
                by = tot(par, m).rearrange("p (n two) -> p n two", two=2)[:, :, 1 - side:2 - side]
                if 2 * m == C:
                    lo = 1 if which == "q" else 0
                    view = view.rearrange("p (h c) m -> p h c m", h=HP)[:, :, lo:lo + NC - 1, :]
                    by = by.rearrange("p (h c) o -> p h c o", h=HP)[:, :, lo:lo + NC - 1, :]
                    by = by.to_broadcast([128, HP, NC - 1, m])
                elif m > 1:
                    by = by.to_broadcast([128, W // (2 * m), m])
                return nc.vector.tensor_tensor(view, view, by, ALU.mult)

            def keep_masked(dst, s, mask, groups):
                nc.vector.tensor_tensor(dst, s, mask.rearrange("p (o t) -> p o t", o=1).to_broadcast([128, groups, 64]),
                                        ALU.mult).then_inc(sc_evac, 1)

            def keep_level(par, j, first_group, groups, s):
                m = HALF[j]
                dst = at_sb[par][:, first_group:first_group + groups, :]\
                    .rearrange("p g (n two m) -> p g n two m", two=2, m=m)[:, :, :, 1, :]
                mask = mask_half[:, j - 2, :].rearrange("p (o n m) -> p o n m", o=1, m=m)\
                    .to_broadcast([128, groups, 64 // m, m]).bitcast(i32)
                nc.vector.copy_predicated(dst, mask, s.rearrange("p g (n m) -> p g n m", m=m)).then_inc(sc_evac, 1)

            def take_own(par, P):
                await_count(dve, av_done, (P - 1) * HP)
                dve.wait_ge(qk_full, P * STEPS + 1)
                s = bank_of_step(0)[:, :].rearrange("p (g t) -> p g t", t=64)
                keep_masked(at_sb[par][:, :, 0::2], s, ident[:, 0::2], G)

            def merged(h):
                return bank_of_step(1 + h)[:, :].rearrange("p (c w t) -> p c w t", w=2, t=64)

            def take_level(par, j):
                keep_level(par, j, 0, G, bank_of_step(j)[:, :].rearrange("p (g t) -> p g t", t=64))

            def states(par, P):
                dve.wait_ge(su_full, (P + 1) * HP)
                await_count(dve, av_done, P * HP)
                n = P * HP * (NC - 1)
                for c in range(1, NC - 1):
                    for h in range(HP):
                        dve.wait_ge(s_done, n + (HP if c == 1 else HP * (c - 1) + h + 1))
                        whole = tot(par, C)[:, h * NC + c:h * NC + c + 1]
                        nc.vector.scalar_tensor_tensor(out=s_sb[:, h, c, :], in0=s_sb[:, h, c - 1, :], scalar=whole,
                                                       in1=(su_ps, kt_ps)[h][:, c * D:(c + 1) * D],
                                                       op0=ALU.mult, op1=ALU.add).then_inc(s_done, 1)

            def clamp_sums(P, i):
                dve.wait_ge(ss_full, P * 2 + i + 1)
                await_count(dve, rn_done, (P - 1) * 2 + i + 1)
                nc.vector.tensor_scalar(ss_sb[:, i * G:(i + 1) * G], (nb_ps, su_ps)[i][:, 0:G * SS:SS], L2_EPS * L2_EPS, None,
                                        ALU.max).then_inc(ss_evac, 1)

            def ln_halves(n, y, resid):
                await_count(dve, x1_done, n)
                nc.vector.tensor_tensor(res[:, :, :], y, resid, ALU.add).then_inc(res_done, 1)
                dve.wait_ge(res_done, n + 1)
                for c in range(NC):
                    nc.vector.bn_stats(stats[:, c, :], res[:, c, :]).then_inc(ln_chain, 1)

            def ln_variance(n):
                step = n * (NC + 6) + NC
                dve.wait_ge(ln_chain, step)
                nc.vector.tensor_tensor(lt[:, 0, :], stats[:, :, 1], stats[:, :, 4], ALU.add).then_inc(ln_chain, 1)
                nc.vector.tensor_tensor(lt[:, 1, :], stats[:, :, 1], stats[:, :, 4], ALU.subtract).then_inc(ln_chain, 1)
                nc.vector.tensor_tensor(lt[:, 2, :], stats[:, :, 2], stats[:, :, 5], ALU.add).then_inc(ln_chain, 1)
                dve.wait_ge(ln_chain, step + 3)
                nc.vector.tensor_scalar(mean[:, :], lt[:, 0, :], 0.5, None, ALU.mult).then_inc(ln_chain, 1)
                nc.vector.scalar_tensor_tensor(out=lt[:, 3, :], in0=lt[:, 1, :], scalar=0.25, in1=lt[:, 1, :],
                                               op0=ALU.mult, op1=ALU.mult).then_inc(ln_chain, 1)
                nc.vector.tensor_scalar(lt[:, 4, :], lt[:, 2, :], 1.0 / D, LN_EPS, ALU.mult, ALU.add).then_inc(ln_chain, 1)
                dve.wait_ge(ln_chain, step + 6)
                await_count(dve, rstd_done, n)
                nc.vector.tensor_tensor(ve[:, :], lt[:, 3, :], lt[:, 4, :], ALU.add).then_inc(ve_done, 1)

            def ln_apply(n, dst):
                dve.wait_ge(rstd_done, n + 1)
                for c in range(NC):
                    last = nc.vector.tensor_scalar(dst(c), res[:, c, :], mean[:, c:c + 1], rstd[:, c:c + 1],
                                                   ALU.subtract, ALU.mult)
                last.then_inc(x1_done, 1)

            y3 = y_ps[:, :].rearrange("p (c d) -> p c d", c=NC)

            def x_rows(b):
                return x_all[:, bass.ds(b * NC, NC), :]

            def ln1_apply(b):
                ln_apply(b, lambda c: x_all[:, bass.ds(b * NC + c, 1), :].rearrange("p o d -> p (o d)"))

            dve.wait_ge(const_pool, CONST_POOL)
            nc.vector.tensor_tensor(mask_odd[:, :], ident[:, 0::2], ident[:, 1::2], ALU.add).then_inc(const_dve, 1)
            dve.wait_ge(fold_pe, 4)
            nc.vector.tensor_tensor(swf_b[:, :], swi_b[:, :], sc[1][:, 0:4], ALU.add).then_inc(fold_bias, 1)
            dve.wait_ge(const_dve, 1)
            low_xT(0)
            for n, (w, name) in enumerate(((wq, "wq"), (wk, "wk"), (wg, "wg"))):
                dve.wait_ge(w_hi, n + 1)
                nc.vector.tensor_tensor(w[1][:, :], raw[name][:, :], w[0][:, :].bitcast(fp32), ALU.subtract).then_inc(w_lo, 1)
            for n in range(2):
                dve.wait_ge(w_hi, n + 4)
                cols = slice(n * 4 * D, (n + 1) * 4 * D)
                nc.vector.tensor_tensor(wvo[1][:, cols], pj[n][:, :], wvo[0][:, cols].bitcast(fp32), ALU.subtract).then_inc(w_lo, 1)
            dve.wait_ge(w_hi, 6)
            nc.vector.tensor_tensor(swf[1][:, :], sc[0][:, :], swf[0][:, :].bitcast(fp32), ALU.subtract).then_inc(w_lo, 1)

            for i in range(2):
                clamp_sums(0, i)
            for h in range(HP):
                normalise_q(0, 0, h)
            own_products(0, 0)
            first_growth(0, 0)
            take_own(0, 0)
            dve.wait_ge(x_in, X_ALL)
            for n, (w, src) in enumerate(((ew1, ew1_raw), (ew3, ew3_raw))):
                dve.wait_ge(e_hi, n + 1)
                nc.vector.tensor_tensor(w[1][:, :], src, w[0][:, :].bitcast(fp32), ALU.subtract).then_inc(e_lo, 1)

            def body(b, first=False, last=False):
                for p, P, has_prev, has_next in slots(b, first, last):
                    par = p % 2
                    qk = P * STEPS
                    for h in range(HP):
                        dve.wait_ge(qk_full, qk + 2 + h)
                        keep_masked(at_sb[par][:, h * NC:(h + 1) * NC, 1::2], merged(h)[:, :, 0, :], mask_odd[:, :], NC)
                    dve.wait_ge(sc_evac, P * 8 + 3)
                    grow(par, 2, "q").then_inc(q_up, 1)
                    grow(par, 2, "k").then_inc(k_up, 1)
                    for h in range(HP):
                        keep_level(par, 2, h * NC, NC, merged(h)[:, :, 1, :])
                    for n in range(2, 7):
                        block_product(dve, nc.vector, par, P, n)
                    for j in range(3, 7):
                        if j == 6 and has_next:
                            for h in range(HP):
                                normalise_q(1 - par, P + 1, h)
                        dve.wait_ge(qk_full, qk + j + 1)
                        if j < 6:
                            dve.wait_ge(sc_evac, P * 8 + j + 2)
                        grow(par, HALF[j], "q").then_inc(q_up, 1)
                        grow(par, HALF[j], "k").then_inc(k_up, 1)
                        if j < 6:
                            take_level(par, j)
                        if j == 4 and has_next:
                            clamp_sums(P + 1, 0)
                        if j == 4 and has_prev:
                            states(1 - par, P - 1)
                        if j == 3 and p == 1 and not first:
                            dve.wait_ge(av_done, b * NP * HP)
                            ln_halves(b - 1, y3, x_rows(b - 1))
                        if j == 5 and p == 1 and not first:
                            ln_variance(b - 1)
                        if j == 3 and p == 2 and not first:
                            ln1_apply(b - 1)
                        if j == 5 and has_next:
                            clamp_sums(P + 1, 1)
                    if has_next:
                        own_products(1 - par, P + 1)
                    if has_next:
                        first_growth(1 - par, P + 1)
                    if p == NP - 2 and not last:
                        low_xT(b + 1)
                    dve.wait_ge(qk_full, qk + 8)
                    grow(par, HALF[7], "k").then_inc(k_up, 1)
                    if has_next:
                        take_own(1 - par, P + 1)
                    grow(par, HALF[7], "q").then_inc(q_up, 1)

            body(0, first=True)
            with dve.Fori(1, B - 1) as b:
                body(b)
            body(B - 1, last=True)
            P = B * NP - 1
            states(P % 2, P)
            dve.wait_ge(av_done, B * NP * HP)
            ln_halves(B - 1, y3, x_rows(B - 1))
            ln_variance(B - 1)
            ln1_apply(B - 1)

            def head_x(n):
                dve.wait_ge(a_x1T, n + 1)
                nc.vector.tensor_tensor(x1T[1][:, :], h0_ps[:, :], x1T[0][:, :].bitcast(fp32), ALU.subtract).then_inc(v_x1T, 1)

            def head_z(n):
                dve.wait_ge(a_s1, n + 1)
                await_count(dve, a_xt, n)
                await_count(dve, f_gate, n)
                nc.vector.scalar_tensor_tensor(out=xt32, in0=h1_ps[:, :], scalar=swf_b[:, 1:2], in1=s1,
                                               op0=ALU.add, op1=ALU.mult).then_inc(v_xt32, 1)

            def head_xt(n, par):
                dve.wait_ge(a_xt, n + 1)
                await_count(dve, f_u, (n - 1) * NE)
                nc.vector.tensor_tensor(xt_sb[par][1][:, :], xt32, xt_sb[par][0][:, :].bitcast(fp32),
                                        ALU.subtract).then_inc(v_xt, 1)

            def low_r(n):
                dve.wait_ge(a_r, n + 1)
                nc.vector.tensor_tensor(r_sb[1][:, :], r_ps[:, :], r_sb[0][:, :].bitcast(fp32), ALU.subtract).then_inc(v_r, 1)

            TOP = 9

            def logits(n):
                dve.wait_ge(f_gate, n + 1)
                g3 = h0_ps[:, :].rearrange("p (c e) -> p c e", c=NC)[:, :, 0:E]
                nc.vector.tensor_reduce(lmax[:, :], g3, axis=AX.X, op=ALU.max).then_inc(v_top, 1)
                dve.wait_ge(v_top, n * TOP + 1)
                await_count(dve, a_ex, n)
                nc.vector.tensor_tensor(lg[:, :, :], g3, lmax[:, :].rearrange("p (c o) -> p c o", o=1).to_broadcast([128, NC, E]),
                                        ALU.subtract).then_inc(v_lg, 1)

            def choose(n, par):
                four = lambda t: t[:, :, :].rearrange("p (c e) j -> p c e j", e=E)
                of_j = ex[:, :, :].rearrange("p c (o j) -> p c o j", o=1).to_broadcast([128, NC, E, E])
                of_e = ex[:, :, :].rearrange("p c (e o) -> p c e o", o=1).to_broadcast([128, NC, E, E])
                first_of = earlier[:, :, :].rearrange("p (o e) j -> p o e j", o=1).to_broadcast([128, NC, E, E])
                top = n * TOP
                dve.wait_ge(a_ex, n + 1)
                nc.vector.tensor_tensor(four(gt), of_j, of_e, ALU.is_gt).then_inc(v_top, 1)
                nc.vector.tensor_tensor(four(eq), of_j, of_e, ALU.is_equal).then_inc(v_top, 1)
                dve.wait_ge(v_top, top + 3)
                nc.vector.tensor_tensor(four(eqe), four(eq), first_of, ALU.mult).then_inc(v_top, 1)
                dve.wait_ge(v_top, top + 4)
                nc.vector.tensor_tensor(four(gt), four(gt), four(eqe), ALU.add).then_inc(v_top, 1)
                dve.wait_ge(v_top, top + 5)
                nc.vector.tensor_reduce(rank[:, :, :], four(gt), axis=AX.X, op=ALU.add).then_inc(v_top, 1)
                dve.wait_ge(v_top, top + 6)
                nc.vector.scalar_tensor_tensor(out=picked[:, :, :], in0=rank[:, :, :], scalar=float(TOPK), in1=ex[:, :, :],
                                               op0=ALU.is_lt, op1=ALU.mult).then_inc(v_top, 1)
                dve.wait_ge(v_top, top + 7)
                nc.vector.tensor_reduce(den[:, :], picked[:, :, :], axis=AX.X, op=ALU.add).then_inc(v_top, 1)
                dve.wait_ge(v_top, top + 8)
                nc.vector.reciprocal(rden[:, :], den[:, :]).then_inc(v_top, 1)
                dve.wait_ge(v_top, top + 9)
                await_count(dve, f_cb, (n - 1) * E)
                nc.vector.tensor_tensor(comb[par][:, :, :], picked[:, :, :],
                                        rden[:, :].rearrange("p (c o) -> p c o", o=1).to_broadcast([128, NC, E]),
                                        ALU.mult).then_inc(v_comb, 1)

            def gate_expert(n, e):
                k = n * NE + e
                dve.wait_ge(a_sg, k + 1)
                dve.wait_ge(f_u, k + 1)
                await_count(dve, f_down, k - 1)
                if e < E:
                    nc.vector.tensor_tensor(gu[e % 2], sg[e % 2], u_ps[e % 2][:, :], ALU.mult).then_inc(v_mid, 1)
                    dve.wait_ge(f_cb, n * E + e + 1)
                    dve.wait_ge(v_mid, n * E + e + 1)
                    nc.vector.tensor_tensor(gc[e % 2], gu[e % 2], cb_ps[:, :], ALU.mult).then_inc(v_gu, 1)
                else:
                    nc.vector.tensor_tensor(gc[e % 2], sg[e % 2], u_ps[e % 2][:, :], ALU.mult).then_inc(v_gu, 1)

            def tail_z(n):
                dve.wait_ge(a_s2, n + 1)
                await_count(dve, f_hT, n)
                nc.vector.scalar_tensor_tensor(out=h_sb, in0=h1_ps[:, :], scalar=swf_b[:, 3:4], in1=s2,
                                               op0=ALU.add, op1=ALU.mult).then_inc(v_h, 1)

            def ln2(n, par):
                dve.wait_ge(f_hT, n + 1)
                ln_halves(B + n, h0_ps[:, :].rearrange("p (c d) -> p c d", c=NC), x_rows(n))
                ln_variance(B + n)

            def ln2_out(n, par):
                await_count(dve, out_done[par], (n - par) * 8)
                ln_apply(B + n, lambda c: o_sb[par][:, c, :])

            def ffn(b, first=False, last=False):
                for par in range(2):
                    n = b + par
                    has_prev = not (first and par == 0)
                    has_next = not (last and par == 1)
                    for e in range(NE):
                        gate_expert(n, e)
                        if e == 0 and has_prev:
                            low_r(n - 1)
                        if e == 1 and has_prev:
                            tail_z(n - 1)
                        if e == 3 and has_prev:
                            ln2(n - 1, 1 - par)
                        if e == 4 and has_prev:
                            ln2_out(n - 1, 1 - par)
                        if e == 4 and has_next:
                            head_x(n + 1)
                        if e == 5 and has_next:
                            head_z(n + 1)
                        if e == 7 and has_next:
                            head_xt(n + 1, 1 - par)
                            logits(n + 1)
                        if e == 8 and has_next:
                            choose(n + 1, 1 - par)

            head_x(0)
            head_z(0)
            head_xt(0, 0)
            logits(0)
            choose(0, 0)
            ffn(0, first=True)
            with dve.Fori(1, B // 2 - 1) as i:
                ffn(2 * i)
            ffn(B - 2, last=True)
            low_r(B - 1)
            tail_z(B - 1)
            ln2(B - 1, 1)
            ln2_out(B - 1, 1)


_INS = ["L0_attn_x", "L0_attn_Wq", "L0_attn_Wk", "L0_attn_Wv", "L0_attn_Wg", "L0_attn_Wo",
        "L0_ffn_lin0_w", "L0_ffn_lin0_b", "L0_ffn_swi1_w1", "L0_ffn_swi1_b1", "L0_ffn_swi1_w2", "L0_ffn_swi1_b2",
        "L0_ffn_gate_w", "L0_ffn_exp_w1", "L0_ffn_exp_w3", "L0_ffn_exp_w2", "L0_ffn_sh_w1", "L0_ffn_sh_w3",
        "L0_ffn_sh_w2", "L0_ffn_lin1_w", "L0_ffn_lin1_b", "L0_ffn_swi2_w1", "L0_ffn_swi2_b1", "L0_ffn_swi2_w2",
        "L0_ffn_swi2_b2"]


def kernel(**inputs):
    import numpy as _np
    import concourse.bacc as _bacc
    from concourse import mybir as _mybir
    from concourse.bass_utils import run_bass_kernel_spmd as _run

    nc = _bacc.Bacc("TRN2", target_bir_lowering=False, num_devices=1)
    arrays, args = {}, []
    for name in _INS:
        a = _np.ascontiguousarray(inputs[name])
        arrays[f"in_{name}_dram"] = a
        args.append(nc.dram_tensor(f"in_{name}_dram", a.shape, _mybir.dt.from_np(a.dtype), kind="ExternalInput").ap())
    shape = inputs["L0_attn_x"].shape
    out = nc.dram_tensor("out_0_dram", shape, _mybir.dt.from_np(_np.dtype("float32")), kind="ExternalOutput").ap()
    gated_linear_attention_and_moe_block(nc, *args, out)
    r = _run(nc, [arrays], core_ids=[0])
    return r.results[0]["out_0_dram"]
```

```python
import concourse.bass as bass
from concourse import mybir
from contextlib import ExitStack


def gated_linear_attention_and_moe_block(
    nc: bass.Bass,
    x: bass.AP,
    Wq: bass.AP,
    Wk: bass.AP,
    Wv: bass.AP,
    Wg: bass.AP,
    Wo: bass.AP,
    lin0_w: bass.AP,
    lin0_b: bass.AP,
    swi1_w1: bass.AP,
    swi1_b1: bass.AP,
    swi1_w2: bass.AP,
    swi1_b2: bass.AP,
    gate_w: bass.AP,
    exp_w1: bass.AP,
    exp_w3: bass.AP,
    exp_w2: bass.AP,
    sh_w1: bass.AP,
    sh_w3: bass.AP,
    sh_w2: bass.AP,
    lin1_w: bass.AP,
    lin1_b: bass.AP,
    swi2_w1: bass.AP,
    swi2_b1: bass.AP,
    swi2_w2: bass.AP,
    swi2_b2: bass.AP,
    out: bass.AP,
):
    fp32 = mybir.dt.float32
    f32r = mybir.dt.float32r
    bf16 = mybir.dt.bfloat16
    i32 = mybir.dt.int32
    ALU = mybir.AluOpType
    ACT = mybir.ActivationFunctionType
    AX = mybir.AxisListType

    B, T, D = x.shape
    H = Wq.shape[1] // D
    C = 128
    NC = T // C
    HP = 2
    NP = H // HP
    G = HP * NC
    W = HP * T
    E, _, FH = exp_w1.shape
    NS = sh_w1.shape[1] // FH
    NE = E + NS
    TOPK = 4
    LN_EPS = 1e-5
    L2_EPS = 1e-12
    STEPS = 8
    SS = 32
    HALF = {j: 2 ** (j - 1) for j in range(2, STEPS)}

    ctx = ExitStack()
    with ctx:
        def sb(name, shape, dt=fp32):
            return ctx.enter_context(nc.sbuf_tensor(name, shape, dt))

        def sem(name):
            return ctx.enter_context(nc.semaphore(name))

        banks = [ctx.enter_context(nc.psum_tensor(f"bank{n}", [128, 512], fp32)) for n in range(8)]

        wq, wk, wg, wvo = ([sb(f"{n}_{part}", [128, H * D], f32r) for part in ("hi", "lo")]
                           for n in ("wq", "wk", "wg", "wvo"))
        ew1, ew3 = ([sb(f"{n}_{part}", [128, NE * FH], f32r) for part in ("hi", "lo")] for n in ("ew1", "ew3"))
        swf = [sb(f"swf_{part}", [128, 2 * 2 * D], f32r) for part in ("hi", "lo")]
        ew2 = [sb(f"ew2_{part}", [128, NE * D], f32r) for part in ("hi", "lo")]
        ew_raw = sb("ew_raw", [128, 3, NE * FH])
        ew1_raw, ew3_raw, ew2_raw = (ew_raw[:, i, :] for i in range(3))
        PARTS = 3
        spread = sb("spread", [PARTS * E, E, 128], bf16)
        eye_bf = sb("eye_bf", [128, 128], bf16)
        gate_rows = sb("gate_rows", [E, D])
        gate_t = sb("gate_t", [128, C])
        lin_b = sb("lin_b", [128, 2])
        swi_b = sb("swi_b", [128, 4])
        swf_b = sb("swf_b", [128, 4])
        ident = sb("ident", [128, 128])
        ones = sb("ones", [128, SS], bf16)
        ones_wide = sb("ones_wide", [128, 128])
        mask_odd = sb("mask_odd", [128, 64])
        mask_half = sb("mask_half", [128, 4, 64])
        earlier = sb("earlier", [128, E, E])
        expo = sb("expo", [128, 16])

        x_all = sb("x_all", [128, B * NC, D])
        x_nat = sb("x_nat", [128, NC, D])
        xT = [sb(f"xT_{part}", [128, T], f32r) for part in ("hi", "lo")]

        qq_sb = [sb(f"qq_sb{i}", [128, 2, W]) for i in range(2)]
        q_sb = [t[:, 0, :] for t in qq_sb]
        qd_sb = [t[:, 1, :] for t in qq_sb]
        e_sb = sb("e_sb", [128, W // 2])
        k_sb = [sb(f"k_sb{i}", [128, W]) for i in range(2)]
        a_sb = [sb(f"a_sb{i}", [128, W]) for i in range(2)]
        tot_sb = [sb(f"tot_sb{i}", [128, W]) for i in range(2)]
        at_sb = [sb(f"at_sb{i}", [128, G, C]) for i in range(2)]
        v_sb = [sb(f"v_sb{i}", [128, NC, HP * D]) for i in range(2)]
        sq_sb = sb("sq_sb", [128, 2, T])
        sq_hi = sb("sq_hi", [128, 2 * HP, T], bf16)
        sq_lo = sb("sq_lo", [128, 2 * HP, T], bf16)
        kt_sb = sb("kt_sb", [128, HP, NC - 1, 128])
        s_sb = sb("s_sb", [128, HP, NC - 1, D])
        ss_sb = sb("ss_sb", [128, 16])
        rn_sb = [sb(f"rn_sb{i}", [128, 2, HP, NC]) for i in range(2)]

        raw = {"wq": q_sb[0], "wk": q_sb[1], "wg": k_sb[0]}
        wv_raw = k_sb[1]
        wvT = a_sb[1]
        linT = tot_sb[1]
        wo = qd_sb[0][:, :].rearrange("p (h d) -> p h d", h=H)
        lin = qd_sb[1][:, 0:2 * D].rearrange("p (i d) -> p i d", i=2)
        swi = qd_sb[1][:, 2 * D:6 * D].rearrange("p (i n) -> p i n", i=2)

        res = sb("res", [128, NC, D])
        stats = sb("stats", [128, NC, 6])
        lt = sb("lt", [128, 5, NC])
        mean = sb("mean", [128, NC])
        ve = sb("ve", [128, NC])
        rstd = sb("rstd", [128, NC])

        x1T = xT
        xt_sb = [[w[:, i * T:(i + 1) * T] for w in wg] for i in range(2)]
        r_sb = [w[:, 0:T] for w in wvo]
        xt32 = k_sb[1][:, 0:T]
        comb = sb("comb", [128, NC, E])
        comb_rest = sb("comb_rest", [128, NC, E])
        comb_parts = sb("comb_parts", [128, NC, PARTS, E], bf16)
        comb_t = sb("comb_t", [PARTS * E, T], bf16)
        lg = sb("lg", [128, NC, E])
        lmax = sb("lmax", [128, NC])
        ex = sb("ex", [128, NC, E])
        gt, eq, eqe = (qd_sb[0][:, n * NC * E * E:(n + 1) * NC * E * E].rearrange("p (t j) -> p t j", j=E) for n in range(3))
        rank = sb("rank", [128, NC, E])
        picked = sb("picked", [128, NC, E])
        den = sb("den", [128, NC])
        rden = sb("rden", [128, NC])
        gc_part = [[(wq, wk)[i // 2][part][:, i % 2 * T:(i % 2 + 1) * T] for i in range(4)] for part in range(2)]
        gc = [v_sb[i // 2][:, i % 2 * HP:(i % 2 + 1) * HP, :].rearrange("p c d -> p (c d)") for i in range(4)]
        sg = [sq_sb[:, i, :] for i in range(2)]
        gu = [t[:, :, :, :].rearrange("p h c d -> p (h c d)")[:, 0:T] for t in (kt_sb, s_sb)]
        s2, h_sb = (q_sb[0][:, i * T:(i + 1) * T] for i in range(2))
        s1 = q_sb[1][:, 0:T]
        o_sb = [k_sb[0][:, i * T:(i + 1) * T].rearrange("p (c d) -> p c d", c=NC) for i in range(2)]

        fold_ps = [banks[6], banks[7]]
        pj = [banks[0], banks[1]]
        sc = [banks[2], banks[3]]
        y_ps = banks[4]
        nb_ps = banks[5]
        kt_ps = banks[6]
        su_ps = banks[7]
        g_ps = [banks[0], banks[1]]
        u_ps = [banks[2], banks[3]]
        h0_ps = banks[4]
        h1_ps = banks[5]
        cb_ps = banks[6]
        r_ps = banks[7]

        w_in = sem("w_in")
        raw_in = {name: sem(f"{name}_in") for name in ("wq", "wk", "wg")}
        x_in = sem("x_in")
        xn_in = sem("xn_in")
        ident_done = sem("ident_done")
        const_pool = sem("const_pool")
        const_dve = sem("const_dve")
        fold_pe = sem("fold_pe")
        fold_sb = sem("fold_sb")
        fold_bias = sem("fold_bias")
        w_hi = sem("w_hi")
        w_lo = sem("w_lo")
        e_hi = sem("e_hi")
        e_lo = sem("e_lo")
        x_lo = sem("x_lo")
        sq_full = sem("sq_full")
        sq_top = sem("sq_top")
        pj_full = sem("pj_full")
        pj_evac = sem("pj_evac")
        xt_full = sem("xt_full")
        xt_evac = sem("xt_evac")
        sq_done = sem("sq_done")
        ss_full = sem("ss_full")
        ss_evac = sem("ss_evac")
        rn_done = sem("rn_done")
        rb_full = sem("rb_full")
        qn_done = sem("qn_done")
        q1_done = sem("q1_done")
        e_done = sem("e_done")
        k_up = sem("k_up")
        q_up = sem("q_up")
        tot_pool = sem("tot_pool")
        tot_done = sem("tot_done")
        qk_full = sem("qk_full")
        sc_evac = sem("sc_evac")
        sc_act = sem("sc_act")
        kt_full = sem("kt_full")
        kt_evac = sem("kt_evac")
        su_full = sem("su_full")
        s_done = sem("s_done")
        av_done = sem("av_done")
        res_done = sem("res_done")
        ln_chain = sem("ln_chain")
        ve_done = sem("ve_done")
        rstd_done = sem("rstd_done")
        x1_done = sem("x1_done")
        out_done = [sem(f"out_done{i}") for i in range(2)]
        nat_in = sem("nat_in")
        f_x1T = sem("f_x1T")
        f_z = sem("f_z")
        f_gate = sem("f_gate")
        f_g = sem("f_g")
        f_u = sem("f_u")
        f_cb = sem("f_cb")
        f_down = sem("f_down")
        f_zo = sem("f_zo")
        f_hT = sem("f_hT")
        a_x1T = sem("a_x1T")
        a_s1 = sem("a_s1")
        a_ex = sem("a_ex")
        a_sg = sem("a_sg")
        a_r = sem("a_r")
        a_xt = sem("a_xt")
        v_x1T = sem("v_x1T")
        v_xt32 = sem("v_xt32")
        v_r = sem("v_r")
        a_s2 = sem("a_s2")
        a_gc = sem("a_gc")
        p_gc = sem("p_gc")
        f_ct = sem("f_ct")
        a_ct = sem("a_ct")
        v_xt = sem("v_xt")
        v_lg = sem("v_lg")
        v_comb = sem("v_comb")
        v_top = sem("v_top")
        v_gu = sem("v_gu")
        v_mid = sem("v_mid")
        v_h = sem("v_h")

        LAG = 3

        def expert(e):
            return (e - NS) % NE

        block = ctx.enter_context(nc.Block())

        def await_count(eng, s, count):
            if not (isinstance(count, int) and count <= 0):
                eng.wait_ge(s, count)

        def halves(ap, m):
            return ap.rearrange("p (n two m) -> p n two m", two=2, m=m)

        def tot(par, m):
            if m == 1:
                return a_sb[par][:, :]
            at = W - 2 * W // m
            return tot_sb[par][:, at:at + W // m]

        def block_product(eng, ops, par, P, n):
            m = 2 ** n
            if n == 0:
                eng.wait_ge(pj_evac, P * 8 + 6)
            else:
                before, count = (tot_pool, P * 2 + n) if n <= 2 else (tot_done, P * 5 + n - 2)
                eng.wait_ge(before, count)
            src = tot(par, m).rearrange("p (n two) -> p n two", two=2)
            ops.tensor_tensor(tot(par, 2 * m), src[:, :, 0], src[:, :, 1], ALU.mult).then_inc(tot_pool if n < 2 else tot_done, 1)

        def even_odd(ap):
            v = ap.rearrange("p (n k i) -> p n k i", k=2, i=2)
            return v[:, :, 0, :], v[:, :, 1, :]

        def pairs_of(ap):
            v = ap.rearrange("p (n i k) -> p n i k", k=2, i=2)
            return v[:, :, :, 0], v[:, :, :, 1]

        def bank_of_step(j):
            return sc[(j + 1) % 2]

        def slots(b, first, last):
            for p in range(NP):
                yield p, b * NP + p, not (first and p == 0), not (last and p == NP - 1)


        @block.sync
        def _(sp):
            sp.dma_start(x_nat[:, :, :], x[0].rearrange("(c t) d -> t c d", t=C)).then_inc(xn_in, 16)
            for name, w in (("wq", Wq), ("wk", Wk), ("wg", Wg)):
                sp.dma_start(raw[name][:, :], w).then_inc(raw_in[name], 16)
            sp.dma_start(wv_raw[:, :], Wv).then_inc(w_in, 16)
            sp.dma_start(wo[:, :, :], Wo.rearrange("(h v) d -> v h d", v=D)).then_inc(w_in, 16)
            sp.dma_start(lin[:, 0, :], lin0_w).then_inc(w_in, 16)
            sp.dma_start(lin[:, 1, :], lin1_w).then_inc(w_in, 16)
            sp.dma_start(swi[:, 0, 0:D], swi1_w1).then_inc(w_in, 16)
            sp.dma_start(swi[:, 0, D:2 * D], swi1_w2).then_inc(w_in, 16)
            sp.dma_start(swi[:, 1, 0:D], swi2_w1).then_inc(w_in, 16)
            sp.dma_start(swi[:, 1, D:2 * D], swi2_w2).then_inc(w_in, 16)
            sp.dma_start(gate_rows[:, :], gate_w).then_inc(w_in, 16)
            for n, bias in enumerate((lin0_b, lin1_b)):
                sp.dma_start(lin_b[:, n:n + 1], bias.rearrange("(p a) -> p a", a=1)).then_inc(w_in, 16)
            for n, bias in enumerate((swi1_b1, swi1_b2, swi2_b1, swi2_b2)):
                sp.dma_start(swi_b[:, n:n + 1], bias.rearrange("(p a) -> p a", a=1)).then_inc(w_in, 16)
            sp.dma_start(x_all[:, :, :], x.rearrange("b (c t) d -> t (b c) d", t=C)).then_inc(x_in, 16)
            for dst, routed, shared in ((ew1_raw, exp_w1, sh_w1), (ew3_raw, exp_w3, sh_w3)):
                sp.dma_start(dst[:, 0:E * FH].rearrange("p (e f) -> p e f", e=E), routed.rearrange("e d f -> d e f")).then_inc(x_in, 16)
                sp.dma_start(dst[:, E * FH:NE * FH], shared).then_inc(x_in, 16)
            w2 = ew2_raw.rearrange("p (e d) -> p e d", e=NE)
            sp.dma_start(w2[:, 0:E, :], exp_w2.rearrange("e f d -> f e d")).then_inc(x_in, 16)
            sp.dma_start(w2[:, E:NE, :], sh_w2.rearrange("(n f) d -> f n d", f=FH)).then_inc(x_in, 16)

            def next_x(b):
                sp.wait_ge(xt_full, b)
                sp.dma_start(x_nat[:, :, :], x[bass.ds(b, 1)].rearrange("a (c t) d -> t (a c) d", t=C)).then_inc(xn_in, 16)

            with sp.Fori(1, B) as b:
                next_x(b)

            def ffn_io(b, first=False, last=False):
                for par in range(2):
                    n = b + par
                    if not (first and par == 0):
                        sp.wait_ge(f_x1T, n)
                    if first and par == 1:
                        sp.wait_ge(x1_done, B)
                    sp.dma_start(x_nat[:, :, :], x_all[:, bass.ds(n * NC, NC), :]).then_inc(nat_in, 16)
                    if not first:
                        store(n - 2, par)

            def store(n, par):
                sp.wait_ge(x1_done, B + n + 1)
                sp.dma_start(out[bass.ds(n, 1)].rearrange("a (c t) d -> t (a c) d", t=C), o_sb[par][:, :, :]).then_inc(out_done[par], 16)

            sp.wait_ge(x1_done, 1)
            sp.wait_ge(xt_full, B)
            ffn_io(0, first=True)
            with sp.Fori(1, B // 2) as i:
                ffn_io(2 * i)
            store(B - 2, 0)
            store(B - 1, 1)
            for par in range(2):
                sp.wait_ge(out_done[par], 16 * B // 2)

        W_ALL = 15 * 16
        X_ALL = 7 * 16

        def pool_setup(pool):
            nc.gpsimd.memset(ident[:, :], 0.0).then_inc(ident_done, 1)
            pool.wait_ge(ident_done, 1)
            nc.gpsimd.affine_select(out=ident[:, :], in_=ident[:, :], compare_op=ALU.not_equal, fill=1.0,
                                    base=0, pattern=[[-1, 128]], channel_multiplier=1).then_inc(ident_done, 1)
            nc.gpsimd.memset(ones[:, :], 1.0).then_inc(const_pool, 1)
            nc.gpsimd.memset(ones_wide[:, :], 1.0).then_inc(const_pool, 1)
            nc.gpsimd.memset(mask_half[:, :, :], 1.0).then_inc(const_pool, 1)
            nc.gpsimd.memset(earlier[:, :, :], 1.0).then_inc(const_pool, 1)
            nc.gpsimd.memset(expo[:, :], -0.5).then_inc(const_pool, 1)
            nc.gpsimd.memset(gate_t[:, :], 0.0).then_inc(const_pool, 1)
            nc.gpsimd.memset(spread[:, :, :], 0.0).then_inc(const_pool, 1)
            pool.wait_ge(const_pool, 7)
            nc.gpsimd.affine_select(out=earlier[:, :, :], in_=earlier[:, :, :], compare_op=ALU.is_ge, fill=0.0,
                                    base=-1, pattern=[[1, E], [-1, E]], channel_multiplier=0).then_inc(const_pool, 1)
            for i, m in enumerate((2, 4, 8, 16)):
                view = mask_half[:, i, :].rearrange("p (n m) -> p n m", m=m)
                nc.gpsimd.affine_select(out=view, in_=view, compare_op=ALU.is_ge, fill=0.0,
                                        base=0, pattern=[[-2 * m, 64 // m], [0, m]], channel_multiplier=1).then_inc(const_pool, 1)
            for i in range(PARTS):
                pool.wait_ge(const_pool, 12 + i)
                nc.gpsimd.affine_select(out=spread[:, :, :], in_=spread[:, :, :], compare_op=ALU.not_equal, fill=1.0,
                                        base=-i * E, pattern=[[-1, E], [0, 128]], channel_multiplier=1).then_inc(const_pool, 1)
            for i, m in enumerate((2, 4, 8, 16)):
                view = mask_half[:, i, :].rearrange("p (n m) -> p n m", m=m)
                nc.gpsimd.affine_select(out=view, in_=view, compare_op=ALU.is_ge, fill=0.0,
                                        base=m - 1, pattern=[[2 * m, 64 // m], [0, m]], channel_multiplier=-1).then_inc(const_pool, 1)

        CONST_POOL = 19

        @block.gpsimd
        def _(pool):
            pool_setup(pool)

            def norms(par, P):
                await_count(pool, ss_full, P * 2)
                def low_square(n):
                    pool.wait_ge(sq_full, P * 4 + n + 1)
                    pool.wait_ge(sq_top, P * 4 + n + 1)
                    nc.gpsimd.tensor_tensor(sq_lo[:, n, :], sq_sb[:, n % 2, :], sq_hi[:, n, :], ALU.subtract).then_inc(sq_done, 1)

                def inverse_norms(i):
                    pool.wait_ge(ss_evac, P * 2 + i + 1)
                    nc.gpsimd.tensor_tensor(rn_sb[par][:, i, :, :].rearrange("p h c -> p (h c)"), ss_sb[:, i * G:(i + 1) * G],
                                            expo[:, 0:G], ALU.pow).then_inc(rn_done, 1)

                for n in range(2 * HP - 1):
                    low_square(n)
                inverse_norms(0)
                low_square(2 * HP - 1)
                await_count(pool, q1_done, (P - 1) * 3)
                await_count(pool, k_up, (P - 1) * 6)
                await_count(pool, q_up, (P - 1) * 6)
                await_count(pool, s_done, (P - 1) * HP * (NC - 1))
                block_product(pool, nc.gpsimd, par, P, 0)
                inverse_norms(1)
                block_product(pool, nc.gpsimd, par, P, 1)

            def ln_rstd(n):
                pool.wait_ge(ve_done, n + 1)
                nc.gpsimd.tensor_tensor(rstd[:, :], ve[:, :], expo[:, 0:NC], ALU.pow).then_inc(rstd_done, 1)

            def body(b, first=False, last=False):
                for p, P, has_prev, has_next in slots(b, first, last):
                    if has_next:
                        norms((p + 1) % 2, P + 1)
                    if p == 1 and not first:
                        ln_rstd(b - 1)

            norms(0, 0)
            body(0, first=True)
            with pool.Fori(1, B - 1) as b:
                body(b)
            body(B - 1, last=True)
            ln_rstd(B - 1)

            def low_gc(n, par, e):
                k = n * NE + e
                pool.wait_ge(a_gc, k + 1)
                nc.gpsimd.tensor_tensor(gc_part[1][(par * NE + e) % 4], gc[(par * NE + e) % 4], gc_part[0][(par * NE + e) % 4].bitcast(fp32), ALU.subtract).then_inc(p_gc, 1)

            def ffn(b, first=False):
                for par in range(2):
                    for e in range(NE):
                        low_gc(b + par, par, e)
                        if e == 4 and not (first and par == 0):
                            ln_rstd(B + b + par - 1)

            ffn(0, first=True)
            with pool.Fori(1, B // 2) as i:
                ffn(2 * i)
            ln_rstd(2 * B - 1)

        @block.tensor
        def _(pe):
            def transposes_of_x(n):
                pe.wait_ge(xn_in, (n + 1) * 16)
                await_count(pe, qn_done, n * NP * HP - 1)
                for c in range(NC):
                    mm = nc.tensor.transpose(nb_ps[:, c * C:(c + 1) * C], x_nat[:, c, :], ident[:, :])
                mm.then_inc(xt_full, 1)

            def bank_of(P, n):
                await_count(pe, pj_evac, P * 8 + n - 1)
                return pj[n % 2]

            def three_passes(out_ap, stat, mov, start=True, stop=True):
                nc.tensor.matmul(out_ap, stat(0), mov(0), start=start, stop=False)
                nc.tensor.matmul(out_ap, stat(0), mov(1), start=False, stop=False)
                return nc.tensor.matmul(out_ap, stat(1), mov(0), start=False, stop=stop)

            def project(p, P, w, n):
                bank = bank_of(P, n)
                col = (p * HP + n % HP) * D
                if n < HP:
                    three_passes(bank[:, :].rearrange("p (n k i) -> p n k i", k=2, i=2), lambda i: w[i][:, col:col + D],
                                 lambda i: xT[i][:, :].rearrange("p (n i k) -> p n k i", k=2, i=2)).then_inc(pj_full, 1)
                else:
                    three_passes(bank[:, :], lambda i: w[i][:, col:col + D], lambda i: xT[i][:, :]).then_inc(pj_full, 1)

            def project_values(p, P, n):
                bank = bank_of(P, 6 + n)
                for i in range(2):
                    c = 2 * n + i
                    mm = three_passes(bank[:, i * HP * D:(i + 1) * HP * D], lambda k: xT[k][:, c * C:(c + 1) * C],
                                      lambda k: wvo[k][:, p * HP * D:(p + 1) * HP * D])
                mm.then_inc(pj_full, 1)

            def sums_of_squares(P, i, n_x):
                pe.wait_ge(sq_done, P * 4 + (i + 1) * HP)
                if i == 0:
                    pe.wait_ge(xt_evac, n_x)
                    pe.wait_ge(x_lo, n_x)
                    await_count(pe, qn_done, P * HP)
                else:
                    await_count(pe, s_done, (P - 1) * HP * (NC - 1))
                for h in range(HP):
                    for c in range(NC):
                        col = (h * NC + c) * SS
                        for part, sq in enumerate((sq_hi, sq_lo)):
                            mm = nc.tensor.matmul((nb_ps, su_ps)[i][:, col:col + SS], sq[:, i * HP + h, c * C:(c + 1) * C],
                                                  ones[:, :], start=part == 0, stop=part == 1)
                mm.then_inc(ss_full, 1)

            def spread_norms(par, P):
                pe.wait_ge(rn_done, P * 2 + 1)
                await_count(pe, s_done, (P - 1) * HP * (NC - 1))
                for h, bank in enumerate((nb_ps, kt_ps)):
                    for c in range(NC):
                        mm = nc.tensor.transpose(bank[:, c * C:(c + 1) * C],
                                                 rn_sb[par][:, 0, h, c:c + 1].to_broadcast([128, 128]), ident[:, :])
                    mm.then_inc(rb_full, 1)

            def scores(par, P, j):
                bank = bank_of_step(j)
                if j == 0:
                    await_count(pe, sc_act, P * 3 - 1)
                    pe.wait_ge(e_done, P + 1)
                    nc.tensor.matmul(bank[:, :], ones_wide[:, :], e_sb[:, :], start=True, stop=True).then_inc(qk_full, 1)
                    return
                if j < 3:
                    if j == 1:
                        await_count(pe, sc_act, P * 3)
                    else:
                        pe.wait_ge(sc_evac, P * 8 + 1)
                    pe.wait_ge(q1_done, 3 * (P + 1))
                    for c in range(NC):
                        lo = (j - 1) * T + c * C
                        moving = qq_sb[par][:, :, lo:lo + C].rearrange("p w (n two m) -> p w n two m", two=2, m=2)[:, :, :, 1, :]
                        mm = nc.tensor.matmul(bank[:, c * C:(c + 1) * C].rearrange("p (w n m) -> p w n m", w=2, m=2),
                                              k_sb[par][:, lo:lo + C], moving, start=True, stop=True)
                    mm.then_inc(qk_full, 1)
                    return
                pe.wait_ge(sc_evac, P * 8 + j + 1)
                pe.wait_ge(k_up, P * 6 + j - 2)
                pe.wait_ge(q_up, P * 6 + j - 2)
                for g in range(G):
                    lo = g * C
                    if j < 6:
                        mm = nc.tensor.matmul(bank[:, g * 64:(g + 1) * 64], k_sb[par][:, lo:lo + C],
                                              halves(qd_sb[par][:, lo:lo + C], HALF[j])[:, :, 1, :], start=True, stop=True)
                        continue
                    m = HALF[j]
                    for n in range(64 // m):
                        left = lo + 2 * m * n
                        mm = nc.tensor.matmul(bank[2 * m * n:2 * m * n + m, g * 64 + m * n:g * 64 + m * (n + 1)],
                                              k_sb[par][:, left:left + m], qd_sb[par][:, left + m:left + 2 * m],
                                              start=True, stop=True)
                mm.then_inc(qk_full, 1)

            def transposes_of_k(par, P, h, last=False):
                if h == 0:
                    pe.wait_ge(k_up, (P + 1) * 6)
                    if not last:
                        pe.wait_ge(qn_done, (P + 2) * HP)
                else:
                    pe.wait_ge(kt_evac, P * HP + 1)
                for c in range(NC - 1):
                    lo = h * T + c * C
                    mm = nc.tensor.transpose(kt_ps[:, c * C:(c + 1) * C], k_sb[par][:, lo:lo + C], ident[:, :])
                mm.then_inc(kt_full, 1)

            def state_updates(par, P, h):
                pe.wait_ge(kt_evac, P * HP + h + 1)
                pe.wait_ge(pj_evac, (P + 1) * 8)
                if h == 0:
                    await_count(pe, s_done, P * HP * (NC - 1))
                    pe.wait_ge(ss_evac, 2 * (P + 1))
                for c in range(NC - 1):
                    mm = nc.tensor.matmul((su_ps, kt_ps)[h][:, c * D:(c + 1) * D], kt_sb[:, h, c, :],
                                          v_sb[par][:, c, h * D:(h + 1) * D], start=True, stop=True)
                mm.then_inc(su_full, 1)

            def outputs_of_chunk(p, P, b, h):
                par = p % 2
                pe.wait_ge(sc_evac, (P + 1) * 8)
                pe.wait_ge(sc_act, (P + 1) * 3)
                pe.wait_ge(pj_evac, (P + 1) * 8)
                if p == 0 and h == 0:
                    await_count(pe, res_done, b)
                for c in range(NC):
                    nc.tensor.matmul(y_ps[:, c * D:(c + 1) * D], at_sb[par][:, h * NC + c, :], v_sb[par][:, c, h * D:(h + 1) * D],
                                     start=p == 0 and h == 0 and c == 0, stop=False, skip_group_check=True)

            def outputs_of_state(p, P, h):
                par = p % 2
                pe.wait_ge(s_done, (P + 1) * HP * (NC - 1))
                pe.wait_ge(q_up, (P + 1) * 6)
                for c in range(1, NC):
                    lo = h * T + c * C
                    mm = nc.tensor.matmul(y_ps[:, c * D:(c + 1) * D], qd_sb[par][:, lo:lo + C], s_sb[:, h, c - 1, :],
                                          start=False, stop=p == NP - 1 and h == HP - 1 and c == NC - 1, skip_group_check=True)
                mm.then_inc(av_done, 1)

            def outputs(p, P, b, h):
                outputs_of_chunk(p, P, b, h)
                outputs_of_state(p, P, h)

            pe.wait_ge(ident_done, 2)
            transposes_of_x(0)
            pe.wait_ge(xt_evac, 1)
            pe.wait_ge(x_lo, 1)
            for n in range(3 * HP):
                pe.wait_ge(w_lo, n // HP + 1)
                project(0, 0, (wq, wk, wg)[n // HP], n)
            pe.wait_ge(w_in, W_ALL)
            pe.wait_ge(const_pool, CONST_POOL)
            for n in range(2):
                for i in range(4):
                    h = 4 * n + i
                    mm = nc.tensor.transpose(fold_ps[n][:, i * D:(i + 1) * D], wv_raw[:, h * D:(h + 1) * D], ident[:, :])
                mm.then_inc(fold_pe, 1)
            for i in range(2):
                nc.tensor.transpose(sc[0][:, i * D:(i + 1) * D], lin[:, i, :], ident[:, :])
            nc.tensor.transpose(sc[0][:, 2 * D:2 * D + E], gate_rows[:, :], ident[0:E, 0:E]).then_inc(fold_pe, 1)
            for i in range(2):
                for n in range(2):
                    mm = nc.tensor.matmul(sc[1][:, 2 * i + n:2 * i + n + 1], swi[:, i, n * D:(n + 1) * D],
                                          lin_b[:, i:i + 1], start=True, stop=True)
            mm.then_inc(fold_pe, 1)
            sums_of_squares(0, 0, 1)
            pe.wait_ge(fold_sb, 4)
            for n in range(2):
                for i in range(4):
                    h = 4 * n + i
                    mm = nc.tensor.matmul(fold_ps[n][:, i * D:(i + 1) * D],
                                          wvT[:, (n * 4 + i) * D:(n * 4 + i + 1) * D], wo[:, h, :], start=True, stop=True)
                mm.then_inc(fold_pe, 1)
            for i in range(2):
                mm = nc.tensor.matmul(sc[0][:, i * 2 * D:(i + 1) * 2 * D], linT[:, i * D:(i + 1) * D], swi[:, i, :],
                                      start=True, stop=True)
            mm.then_inc(fold_pe, 1)
            pe.wait_ge(w_lo, 6)
            pe.wait_ge(fold_bias, 1)

            sums_of_squares(0, 1, 1)
            spread_norms(0, 0)
            for n in range(2):
                project_values(0, 0, n)
            scores(0, 0, 0)

            def body(b, first=False, last=False):
                for p, P, has_prev, has_next in slots(b, first, last):
                    par = p % 2
                    prev_p, next_p = (p - 1) % NP, (p + 1) % NP
                    n_x = b + 2 if p == NP - 1 else b + 1
                    if has_next and p < NP - 1:
                        project(next_p, P + 1, wq, 0)
                    scores(par, P, 1)
                    scores(par, P, 2)
                    if has_prev:
                        transposes_of_k(1 - par, P - 1, 0)
                    if has_next:
                        if p == NP - 1:
                            pe.wait_ge(xt_evac, n_x)
                            pe.wait_ge(x_lo, n_x)
                            project(next_p, P + 1, wq, 0)
                            transposes_of_k(1 - par, P - 1, 1)
                        project(next_p, P + 1, wq, 1)
                    if has_prev and not (has_next and p == NP - 1):
                        transposes_of_k(1 - par, P - 1, 1)
                    if has_next:
                        project(next_p, P + 1, wk, 2)
                    if has_prev:
                        state_updates(1 - par, P - 1, 0)
                    scores(par, P, 3)
                    if has_prev:
                        state_updates(1 - par, P - 1, 1)
                    if has_next:
                        project(next_p, P + 1, wk, 3)
                        sums_of_squares(P + 1, 0, n_x)
                    scores(par, P, 4)
                    if has_prev:
                        outputs_of_chunk(prev_p, P - 1, b if p else b - 1, 0)
                    if has_next:
                        project(next_p, P + 1, wg, 4)
                        project(next_p, P + 1, wg, 5)
                    scores(par, P, 5)
                    if has_prev:
                        outputs_of_state(prev_p, P - 1, 0)
                    if has_next:
                        sums_of_squares(P + 1, 1, n_x)
                        spread_norms(1 - par, P + 1)
                    scores(par, P, 6)
                    if has_prev:
                        outputs(prev_p, P - 1, b if p else b - 1, 1)
                    if has_next:
                        project_values(next_p, P + 1, 0)
                        project_values(next_p, P + 1, 1)
                    scores(par, P, 7)
                    if has_next:
                        scores(1 - par, P + 1, 0)
                    if p == NP - 2 and not last:
                        transposes_of_x(b + 1)

            body(0, first=True)
            with pe.Fori(1, B - 1) as b:
                body(b)
            body(B - 1, last=True)
            P = B * NP - 1
            for h in range(HP):
                transposes_of_k(P % 2, P, h, last=True)
            for h in range(HP):
                state_updates(P % 2, P, h)
            for h in range(HP):
                outputs(NP - 1, P, B - 1, h)

            def head_x(n):
                pe.wait_ge(nat_in, (n + 1) * 16)
                for c in range(NC):
                    mm = nc.tensor.transpose(h0_ps[:, c * C:(c + 1) * C], x_nat[:, c, :], ident[:, :])
                mm.then_inc(f_x1T, 1)

            def head_z(n):
                pe.wait_ge(a_x1T, n + 1)
                pe.wait_ge(v_x1T, n + 1)
                await_count(pe, v_h, n - 2)
                three_passes(h0_ps[:, :], lambda i: swf[i][:, 0:D], lambda i: x1T[i][:, :])
                three_passes(h1_ps[:, :], lambda i: swf[i][:, D:2 * D], lambda i: x1T[i][:, :]).then_inc(f_z, 1)

            def head_gate(n, par):
                pe.wait_ge(v_xt32, n + 1)
                for c in range(NC):
                    mm = nc.tensor.matmul(h0_ps[:, c * C:(c + 1) * C], xt32[:, c * C:(c + 1) * C], gate_t[:, :],
                                          start=True, stop=True)
                mm.then_inc(f_gate, 1)

            def weights_t(n):
                pe.wait_ge(v_comb, n + 1)
                for c in range(NC):
                    mm = nc.tensor.matmul(h0_ps[0:PARTS * E, c * C:(c + 1) * C],
                                          comb_parts[:, c, :, :].rearrange("p i e -> p (i e)"), eye_bf[:, :], start=True, stop=True)
                mm.then_inc(f_ct, 1)

            def up(n, par, e):
                k = n * NE + e
                await_count(pe, a_sg, k - 1)
                if e == 0:
                    pe.wait_ge(a_xt, n + 1)
                    pe.wait_ge(v_xt, n + 1)
                three_passes(g_ps[e % 2][:, :], lambda i: ew1[i][:, expert(e) * FH:(expert(e) + 1) * FH],
                             lambda i: xt_sb[par][i][:, :]).then_inc(f_g, 1)
                await_count(pe, v_gu, k - 1)
                three_passes(u_ps[e % 2][:, :], lambda i: ew3[i][:, expert(e) * FH:(expert(e) + 1) * FH],
                             lambda i: xt_sb[par][i][:, :]).then_inc(f_u, 1)

            def spread_weights(n, e):
                if e == NS:
                    pe.wait_ge(a_ct, n + 1)
                    await_count(pe, v_gu, n * NE)
                else:
                    pe.wait_ge(v_gu, n * NE + e)
                nc.tensor.matmul(cb_ps[:, :], spread[:, expert(e), :], comb_t[:, :], start=True, stop=True).then_inc(f_cb, 1)

            def down(n, par, e):
                pe.wait_ge(p_gc, n * NE + e + 1)
                if e == 0:
                    await_count(pe, a_r, n)
                    await_count(pe, v_r, n)
                three_passes(r_ps[:, :], lambda i: ew2[i][:, expert(e) * D:(expert(e) + 1) * D], lambda i: gc_part[i][(par * NE + e) % 4],
                             start=e == 0, stop=e == NE - 1).then_inc(f_down, 1)

            def tail_z(n):
                pe.wait_ge(a_r, n + 1)
                pe.wait_ge(v_r, n + 1)
                three_passes(h0_ps[:, :], lambda i: swf[i][:, 2 * D:3 * D], lambda i: r_sb[i][:, :])
                three_passes(h1_ps[:, :], lambda i: swf[i][:, 3 * D:4 * D], lambda i: r_sb[i][:, :]).then_inc(f_zo, 1)

            def tail_h(n):
                pe.wait_ge(v_h, n + 1)
                for c in range(NC):
                    mm = nc.tensor.transpose(h0_ps[:, c * C:(c + 1) * C], h_sb[:, c * C:(c + 1) * C], ident[:, :])
                mm.then_inc(f_hT, 1)

            def ffn(b, first=False, last=False):
                for par in range(2):
                    n = b + par
                    has_prev = not (first and par == 0)
                    has_next = not (last and par == 1)
                    for e in range(NE):
                        up(n, par, e)
                        if e < LAG and has_prev:
                            down(n - 1, 1 - par, NE + e - LAG)
                        if e >= LAG:
                            down(n, par, e - LAG)
                        if e >= NS:
                            spread_weights(n, e)
                        if e == 0 and has_next:
                            pe.wait_ge(v_lg, n + 1)
                            head_x(n + 1)
                        if e == 1:
                            if has_next:
                                pe.wait_ge(a_x1T, n + 2)
                                pe.wait_ge(v_x1T, n + 2)
                            weights_t(n)
                        if e == 2:
                            pe.wait_ge(a_ct, n + 1)
                            if has_next:
                                head_z(n + 1)
                        if e == 3 and has_prev:
                            if has_next:
                                pe.wait_ge(v_xt32, n + 2)
                            tail_z(n - 1)
                        if e == 4 and has_prev:
                            tail_h(n - 1)
                        if e == 6 and has_next:
                            if has_prev:
                                pe.wait_ge(res_done, B + n)
                            head_gate(n + 1, 1 - par)

            pe.wait_ge(res_done, B)
            head_x(0)
            head_z(0)
            head_gate(0, 0)
            pe.wait_ge(s_done, B * NP * HP * (NC - 1))
            pe.wait_ge(kt_evac, B * NP * HP)
            pe.wait_ge(e_lo, 3)
            pe.wait_ge(const_dve, 2)
            ffn(0, first=True)
            with pe.Fori(1, B // 2 - 1) as i:
                ffn(2 * i)
            ffn(B - 2, last=True)
            for e in range(NE - LAG, NE):
                down(B - 1, 1, e)
            tail_z(B - 1)
            tail_h(B - 1)

        @block.scalar
        def _(act):
            def take_xT(n):
                act.wait_ge(xt_full, n + 1)
                await_count(act, pj_full, n * NP * 8)
                nc.scalar.activation(xT[0][:, :], nb_ps[:, :], ACT.Copy).then_inc(xt_evac, 1)

            def take_tile(par, P, n):
                act.wait_ge(pj_full, P * 8 + n + 1)
                if n == 0:
                    await_count(act, qk_full, (P - 1) * STEPS)
                if n == HP:
                    await_count(act, kt_full, (P - 1) * HP)
                dst = (q_sb, k_sb)[n // HP][par]
                nc.scalar.activation(dst[:, (n % HP) * T:(n % HP + 1) * T], pj[n % 2][:, :], ACT.Copy).then_inc(pj_evac, 1)

            def square(par, P, n):
                act.wait_ge(pj_evac, P * 8 + n + 1)
                await_count(act, ss_full, P * 2)
                await_count(act, sq_done, P * 4 + n - 1)
                src = (q_sb, k_sb)[n // HP][par][:, (n % HP) * T:(n % HP + 1) * T]
                nc.scalar.activation(sq_sb[:, n % 2, :], src, ACT.Square).then_inc(sq_full, 1)
                nc.scalar.activation(sq_hi[:, n, :], src, ACT.Square).then_inc(sq_top, 1)

            def take_gate(par, P):
                for h in range(HP):
                    act.wait_ge(pj_full, P * 8 + 5 + h)
                    if h == 0:
                        await_count(act, q1_done, (P - 1) * 3)
                        await_count(act, k_up, (P - 1) * 6)
                        await_count(act, tot_pool, (P - 1) * 2)
                        await_count(act, tot_done, (P - 1) * 5)
                    nc.scalar.activation(a_sb[par][:, h * T:(h + 1) * T], pj[h][:, :], ACT.Sigmoid).then_inc(pj_evac, 1)

            def take_values(par, P, n):
                act.wait_ge(rn_done, (P + 1) * 2)
                await_count(act, av_done, (P - 1) * HP)
                act.wait_ge(pj_full, P * 8 + 7 + n)
                for i in range(2):
                    for h in range(HP):
                        c = 2 * n + i
                        at = (i * HP + h) * D
                        last = nc.scalar.activation(v_sb[par][:, c, h * D:(h + 1) * D], pj[n][:, at:at + D],
                                                    ACT.Copy, scale=rn_sb[par][:, 1, h, c:c + 1])
                last.then_inc(pj_evac, 1)

            def take_kT(P, h):
                act.wait_ge(kt_full, P * HP + h + 1)
                await_count(act, su_full, (P - 1) * HP + h + 1)
                nc.scalar.activation(kt_sb[:, h, :, :].rearrange("p c k -> p (c k)"), kt_ps[:, 0:(NC - 1) * C],
                                     ACT.Copy).then_inc(kt_evac, 1)

            def first_states(P):
                act.wait_ge(su_full, (P + 1) * HP)
                await_count(act, av_done, P * HP)
                for h in range(HP):
                    nc.scalar.activation(s_sb[:, h, 0, :], (su_ps, kt_ps)[h][:, 0:D], ACT.Copy).then_inc(s_done, 1)

            def take_scores_32(par, P):
                act.wait_ge(qk_full, P * STEPS + 7)
                act.wait_ge(sc_evac, (P + 1) * 8)
                s = bank_of_step(6)[:, :].rearrange("p (g t) -> p g t", t=64)
                nc.scalar.activation(at_sb[par][0:32, :, 32:64], s[0:32, :, 0:32], ACT.Copy).then_inc(sc_act, 1)
                nc.scalar.activation(at_sb[par][64:96, :, 96:128], s[64:96, :, 32:64], ACT.Copy).then_inc(sc_act, 1)

            def take_scores_64(par, P):
                act.wait_ge(qk_full, P * STEPS + 8)
                s = bank_of_step(7)[:, :].rearrange("p (g t) -> p g t", t=64)
                nc.scalar.activation(at_sb[par][0:64, :, 64:128], s[0:64, :, :], ACT.Copy).then_inc(sc_act, 1)

            take_xT(0)
            for w, name in ((wq, "wq"), (wk, "wk"), (wg, "wg")):
                act.wait_ge(raw_in[name], 16)
                nc.scalar.activation(w[0][:, :], raw[name][:, :], ACT.Copy).then_inc(w_hi, 1)
            act.wait_ge(w_lo, 3)
            for n in range(2 * HP):
                take_tile(0, 0, n)
                square(0, 0, n)
            act.wait_ge(w_in, W_ALL)
            for n in range(2):
                act.wait_ge(fold_pe, n + 1)
                nc.scalar.activation(wvT[:, n * 4 * D:(n + 1) * 4 * D], fold_ps[n][:, :], ACT.Copy).then_inc(fold_sb, 1)
            act.wait_ge(fold_pe, 3)
            nc.scalar.activation(linT[:, 0:2 * D], sc[0][:, 0:2 * D], ACT.Copy).then_inc(fold_sb, 1)
            nc.scalar.activation(gate_t[:, 0:E], sc[0][:, 2 * D:2 * D + E], ACT.Copy).then_inc(fold_sb, 1)
            for n in range(2):
                act.wait_ge(fold_pe, n + 5)
                nc.scalar.activation(wvo[0][:, n * 4 * D:(n + 1) * 4 * D], fold_ps[n][:, :], ACT.Copy).then_inc(w_hi, 1)
            act.wait_ge(fold_pe, 7)
            nc.scalar.activation(swf[0][:, :], sc[0][:, :], ACT.Copy).then_inc(w_hi, 1)
            take_gate(0, 0)
            for n in range(2):
                take_values(0, 0, n)

            def high_experts(n):
                act.wait_ge(x_in, X_ALL)
                w, src = ((ew1, ew1_raw), (ew3, ew3_raw), (ew2, ew2_raw))[n]
                nc.scalar.activation(w[0][:, :], src, ACT.Copy).then_inc(e_hi, 1)

            def body(b, first=False, last=False):
                for p, P, has_prev, has_next in slots(b, first, last):
                    par = p % 2
                    if has_prev and p == NP - 1:
                        take_kT(P - 1, 0)
                    if has_next:
                        take_tile(1 - par, P + 1, 0)
                    if has_prev:
                        take_kT(P - 1, 1 if p == NP - 1 else 0)
                    if has_next:
                        square(1 - par, P + 1, 0)
                        take_tile(1 - par, P + 1, 1)
                    if has_prev and p < NP - 1:
                        take_kT(P - 1, 1)
                    if has_next:
                        square(1 - par, P + 1, 1)
                        take_tile(1 - par, P + 1, 2)
                        square(1 - par, P + 1, 2)
                    if has_prev:
                        first_states(P - 1)
                    if has_next:
                        take_tile(1 - par, P + 1, 3)
                        square(1 - par, P + 1, 3)
                        take_gate(1 - par, P + 1)
                    take_scores_32(par, P)
                    if has_next:
                        take_values(1 - par, P + 1, 0)
                        take_values(1 - par, P + 1, 1)
                    take_scores_64(par, P)
                    if p == NP - 2 and not last:
                        take_xT(b + 1)
                    if first and p < 3:
                        high_experts(p)

            body(0, first=True)
            with act.Fori(1, B - 1) as b:
                body(b)
            body(B - 1, last=True)
            for h in range(HP):
                take_kT(B * NP - 1, h)
            first_states(B * NP - 1)

            def head_x(n):
                act.wait_ge(f_x1T, n + 1)
                await_count(act, f_z, n)
                nc.scalar.activation(x1T[0][:, :], h0_ps[:, :], ACT.Copy).then_inc(a_x1T, 1)

            def head_z(n):
                act.wait_ge(f_z, n + 1)
                await_count(act, v_xt32, n)
                nc.scalar.activation(s1, h0_ps[:, :], ACT.Silu, bias=swf_b[:, 0:1]).then_inc(a_s1, 1)

            def head_xt(n, par):
                act.wait_ge(v_xt32, n + 1)
                await_count(act, f_u, (n - 1) * NE)
                nc.scalar.activation(xt_sb[par][0][:, :], xt32, ACT.Copy).then_inc(a_xt, 1)

            def exp_logits(n):
                act.wait_ge(v_lg, n + 1)
                await_count(act, v_comb, n)
                nc.scalar.activation(ex[:, :, :], lg[:, :, :], ACT.Exp).then_inc(a_ex, 1)

            def silu_expert(n, e):
                k = n * NE + e
                act.wait_ge(f_g, k + 1)
                await_count(act, v_gu, k - 1)
                nc.scalar.activation(sg[e % 2], g_ps[e % 2][:, :], ACT.Silu).then_inc(a_sg, 1)

            def high_gc(n, par, e):
                k = n * NE + e
                act.wait_ge(v_gu, k + 1)
                await_count(act, f_down, k - 3)
                nc.scalar.activation(gc_part[0][(par * NE + e) % 4], gc[(par * NE + e) % 4], ACT.Copy).then_inc(a_gc, 1)

            def take_weights_t(n):
                act.wait_ge(f_ct, n + 1)
                nc.scalar.activation(comb_t[:, :], h0_ps[0:PARTS * E, :], ACT.Copy).then_inc(a_ct, 1)

            def take_r(n):
                act.wait_ge(f_down, (n + 1) * NE)
                await_count(act, f_zo, n)
                nc.scalar.activation(r_sb[0][:, :], r_ps[:, :], ACT.Copy).then_inc(a_r, 1)

            def tail_z(n):
                act.wait_ge(f_zo, n + 1)
                await_count(act, v_h, n)
                nc.scalar.activation(s2, h0_ps[:, :], ACT.Silu, bias=swf_b[:, 2:3]).then_inc(a_s2, 1)

            def ffn(b, first=False, last=False):
                for par in range(2):
                    n = b + par
                    has_prev = not (first and par == 0)
                    has_next = not (last and par == 1)
                    for e in range(NE):
                        silu_expert(n, e)
                        if e > 0:
                            high_gc(n, par, e - 1)
                        elif has_prev:
                            high_gc(n - 1, 1 - par, NE - 1)
                        if e == 0 and has_next:
                            head_x(n + 1)
                        if e == 1:
                            take_weights_t(n)
                        if e == 2 and has_prev:
                            take_r(n - 1)
                        if e == 2 and has_next:
                            head_z(n + 1)
                        if e == 3 and has_next:
                            head_xt(n + 1, 1 - par)
                        if e == 3 and has_prev:
                            tail_z(n - 1)
                        if e == 7 and has_next:
                            exp_logits(n + 1)

            act.wait_ge(av_done, B * NP * HP)
            act.wait_ge(fold_bias, 1)
            head_x(0)
            head_z(0)
            head_xt(0, 0)
            exp_logits(0)
            ffn(0, first=True)
            with act.Fori(1, B // 2 - 1) as i:
                ffn(2 * i)
            ffn(B - 2, last=True)
            high_gc(B - 1, 1, NE - 1)
            take_r(B - 1)
            tail_z(B - 1)

        @block.vector
        def _(dve):
            def normalise_q(par, P, h):
                dve.wait_ge(rb_full, P * HP + h + 1)
                seg = q_sb[par][:, h * T:(h + 1) * T]
                nc.vector.tensor_tensor(seg, seg, (nb_ps, kt_ps)[h][:, :], ALU.mult).then_inc(qn_done, 1)

            def low_xT(n):
                dve.wait_ge(xt_evac, n + 1)
                nc.vector.tensor_tensor(xT[1][:, :], nb_ps[:, :], xT[0][:, :].bitcast(fp32), ALU.subtract).then_inc(x_lo, 1)

            def own_products(par, P):
                dve.wait_ge(qn_done, (P + 1) * HP)
                await_count(dve, qk_full, (P - 1) * STEPS + 1)
                nc.vector.tensor_tensor(e_sb[:, :].rearrange("p (n i) -> p n i", i=2), even_odd(q_sb[par])[0],
                                        pairs_of(k_sb[par][:, :])[0], ALU.mult).then_inc(e_done, 1)

            def first_growth(par, P):
                dve.wait_ge(tot_pool, P * 2 + 1)
                grow(par, 1, "k").then_inc(q1_done, 1)
                await_count(dve, av_done, (P - 1) * HP)
                for odd in range(2):
                    by = pairs_of(a_sb[par][:, :])[0] if odd == 0 else \
                        tot(par, 2).rearrange("p (n i) -> p n i", i=2)
                    nc.vector.tensor_tensor(pairs_of(qd_sb[par])[odd], even_odd(q_sb[par])[odd], by, ALU.mult).then_inc(q1_done, 1)

            def grow(par, m, which):
                side = 1 if which == "q" else 0
                buf = (qd_sb if which == "q" else k_sb)[par]
                view = halves(buf[:, :], m)[:, :, side, :]
                by = tot(par, m).rearrange("p (n two) -> p n two", two=2)[:, :, 1 - side:2 - side]
                if 2 * m == C:
                    lo = 1 if which == "q" else 0
                    view = view.rearrange("p (h c) m -> p h c m", h=HP)[:, :, lo:lo + NC - 1, :]
                    by = by.rearrange("p (h c) o -> p h c o", h=HP)[:, :, lo:lo + NC - 1, :]
                    by = by.to_broadcast([128, HP, NC - 1, m])
                elif m > 1:
                    by = by.to_broadcast([128, W // (2 * m), m])
                return nc.vector.tensor_tensor(view, view, by, ALU.mult)

            def keep_masked(dst, s, mask, groups):
                nc.vector.tensor_tensor(dst, s, mask.rearrange("p (o t) -> p o t", o=1).to_broadcast([128, groups, 64]),
                                        ALU.mult).then_inc(sc_evac, 1)

            def keep_level(par, j, first_group, groups, s):
                m = HALF[j]
                dst = at_sb[par][:, first_group:first_group + groups, :]\
                    .rearrange("p g (n two m) -> p g n two m", two=2, m=m)[:, :, :, 1, :]
                mask = mask_half[:, j - 2, :].rearrange("p (o n m) -> p o n m", o=1, m=m)\
                    .to_broadcast([128, groups, 64 // m, m]).bitcast(i32)
                nc.vector.copy_predicated(dst, mask, s.rearrange("p g (n m) -> p g n m", m=m)).then_inc(sc_evac, 1)

            def take_own(par, P):
                await_count(dve, av_done, (P - 1) * HP)
                dve.wait_ge(qk_full, P * STEPS + 1)
                s = bank_of_step(0)[:, :].rearrange("p (g t) -> p g t", t=64)
                keep_masked(at_sb[par][:, :, 0::2], s, ident[:, 0::2], G)

            def merged(h):
                return bank_of_step(1 + h)[:, :].rearrange("p (c w t) -> p c w t", w=2, t=64)

            def take_level(par, j):
                keep_level(par, j, 0, G, bank_of_step(j)[:, :].rearrange("p (g t) -> p g t", t=64))

            def states(par, P):
                dve.wait_ge(su_full, (P + 1) * HP)
                dve.wait_ge(tot_done, (P + 1) * 5)
                await_count(dve, av_done, P * HP)
                n = P * HP * (NC - 1)
                for c in range(1, NC - 1):
                    for h in range(HP):
                        dve.wait_ge(s_done, n + (HP if c == 1 else HP * (c - 1) + h + 1))
                        whole = tot(par, C)[:, h * NC + c:h * NC + c + 1]
                        nc.vector.scalar_tensor_tensor(out=s_sb[:, h, c, :], in0=s_sb[:, h, c - 1, :], scalar=whole,
                                                       in1=(su_ps, kt_ps)[h][:, c * D:(c + 1) * D],
                                                       op0=ALU.mult, op1=ALU.add).then_inc(s_done, 1)

            def clamp_sums(P, i):
                dve.wait_ge(ss_full, P * 2 + i + 1)
                await_count(dve, rn_done, (P - 1) * 2 + i + 1)
                nc.vector.tensor_scalar(ss_sb[:, i * G:(i + 1) * G], (nb_ps, su_ps)[i][:, 0:G * SS:SS], L2_EPS * L2_EPS, None,
                                        ALU.max).then_inc(ss_evac, 1)

            def ln_halves(n, y, resid):
                await_count(dve, x1_done, n)
                nc.vector.tensor_tensor(res[:, :, :], y, resid, ALU.add).then_inc(res_done, 1)
                dve.wait_ge(res_done, n + 1)
                for c in range(NC):
                    nc.vector.bn_stats(stats[:, c, :], res[:, c, :]).then_inc(ln_chain, 1)

            def ln_variance(n):
                step = n * (NC + 6) + NC
                dve.wait_ge(ln_chain, step)
                nc.vector.tensor_tensor(lt[:, 0, :], stats[:, :, 1], stats[:, :, 4], ALU.add).then_inc(ln_chain, 1)
                nc.vector.tensor_tensor(lt[:, 1, :], stats[:, :, 1], stats[:, :, 4], ALU.subtract).then_inc(ln_chain, 1)
                nc.vector.tensor_tensor(lt[:, 2, :], stats[:, :, 2], stats[:, :, 5], ALU.add).then_inc(ln_chain, 1)
                dve.wait_ge(ln_chain, step + 3)
                nc.vector.tensor_scalar(mean[:, :], lt[:, 0, :], 0.5, None, ALU.mult).then_inc(ln_chain, 1)
                nc.vector.scalar_tensor_tensor(out=lt[:, 3, :], in0=lt[:, 1, :], scalar=0.25, in1=lt[:, 1, :],
                                               op0=ALU.mult, op1=ALU.mult).then_inc(ln_chain, 1)
                nc.vector.tensor_scalar(lt[:, 4, :], lt[:, 2, :], 1.0 / D, LN_EPS, ALU.mult, ALU.add).then_inc(ln_chain, 1)
                dve.wait_ge(ln_chain, step + 6)
                await_count(dve, rstd_done, n)
                nc.vector.tensor_tensor(ve[:, :], lt[:, 3, :], lt[:, 4, :], ALU.add).then_inc(ve_done, 1)

            def ln_apply(n, dst):
                dve.wait_ge(rstd_done, n + 1)
                for c in range(NC):
                    last = nc.vector.tensor_scalar(dst(c), res[:, c, :], mean[:, c:c + 1], rstd[:, c:c + 1],
                                                   ALU.subtract, ALU.mult)
                last.then_inc(x1_done, 1)

            y3 = y_ps[:, :].rearrange("p (c d) -> p c d", c=NC)

            def x_rows(b):
                return x_all[:, bass.ds(b * NC, NC), :]

            def ln1_apply(b):
                ln_apply(b, lambda c: x_all[:, bass.ds(b * NC + c, 1), :].rearrange("p o d -> p (o d)"))

            low_xT(0)
            for n, (w, name) in enumerate(((wq, "wq"), (wk, "wk"), (wg, "wg"))):
                dve.wait_ge(w_hi, n + 1)
                nc.vector.tensor_tensor(w[1][:, :], raw[name][:, :], w[0][:, :].bitcast(fp32), ALU.subtract).then_inc(w_lo, 1)
            dve.wait_ge(const_pool, CONST_POOL)
            dve.wait_ge(ident_done, 2)
            nc.vector.tensor_tensor(mask_odd[:, :], ident[:, 0::2], ident[:, 1::2], ALU.add).then_inc(const_dve, 1)
            nc.vector.tensor_copy(eye_bf[:, :], ident[:, :]).then_inc(const_dve, 1)
            dve.wait_ge(fold_pe, 4)
            nc.vector.tensor_tensor(swf_b[:, :], swi_b[:, :], sc[1][:, 0:4], ALU.add).then_inc(fold_bias, 1)
            clamp_sums(0, 0)
            for n in range(2):
                dve.wait_ge(w_hi, n + 4)
                cols = slice(n * 4 * D, (n + 1) * 4 * D)
                nc.vector.tensor_tensor(wvo[1][:, cols], fold_ps[n][:, :], wvo[0][:, cols].bitcast(fp32), ALU.subtract).then_inc(w_lo, 1)
            dve.wait_ge(w_hi, 6)
            nc.vector.tensor_tensor(swf[1][:, :], sc[0][:, :], swf[0][:, :].bitcast(fp32), ALU.subtract).then_inc(w_lo, 1)
            clamp_sums(0, 1)
            dve.wait_ge(const_dve, 1)
            for h in range(HP):
                normalise_q(0, 0, h)
            own_products(0, 0)
            first_growth(0, 0)
            take_own(0, 0)

            def low_experts(n):
                dve.wait_ge(x_in, X_ALL)
                dve.wait_ge(e_hi, n + 1)
                w, src = ((ew1, ew1_raw), (ew3, ew3_raw), (ew2, ew2_raw))[n]
                nc.vector.tensor_tensor(w[1][:, :], src, w[0][:, :].bitcast(fp32), ALU.subtract).then_inc(e_lo, 1)

            def body(b, first=False, last=False):
                for p, P, has_prev, has_next in slots(b, first, last):
                    par = p % 2
                    qk = P * STEPS
                    for h in range(HP):
                        dve.wait_ge(qk_full, qk + 2 + h)
                        keep_masked(at_sb[par][:, h * NC:(h + 1) * NC, 1::2], merged(h)[:, :, 0, :], mask_odd[:, :], NC)
                    dve.wait_ge(sc_evac, P * 8 + 3)
                    grow(par, 2, "q").then_inc(q_up, 1)
                    grow(par, 2, "k").then_inc(k_up, 1)
                    for h in range(HP):
                        keep_level(par, 2, h * NC, NC, merged(h)[:, :, 1, :])
                    for j in range(3, 7):
                        if j == 6 and has_next:
                            for h in range(HP):
                                normalise_q(1 - par, P + 1, h)
                        if j == 3:
                            dve.wait_ge(tot_pool, P * 2 + 2)
                        else:
                            dve.wait_ge(tot_done, P * 5 + j - 3)
                        dve.wait_ge(qk_full, qk + j + 1)
                        if j < 6:
                            dve.wait_ge(sc_evac, P * 8 + j + 2)
                        grow(par, HALF[j], "q").then_inc(q_up, 1)
                        grow(par, HALF[j], "k").then_inc(k_up, 1)
                        if j < 6:
                            take_level(par, j)
                            for n in range(j - 1, j if j < 5 else 7):
                                block_product(dve, nc.vector, par, P, n)
                        if j == 3 and has_next:
                            clamp_sums(P + 1, 0)
                        if j == 4 and has_prev:
                            states(1 - par, P - 1)
                        if j == 3 and p == 1 and not first:
                            dve.wait_ge(av_done, b * NP * HP)
                            ln_halves(b - 1, y3, x_rows(b - 1))
                        if j == 3 and first and p > 0:
                            low_experts(p - 1)
                        if j == 5 and p == 1 and not first:
                            ln_variance(b - 1)
                        if j == 3 and p == 2 and not first:
                            ln1_apply(b - 1)
                        if j == 5 and has_next:
                            clamp_sums(P + 1, 1)
                    if has_next:
                        own_products(1 - par, P + 1)
                    if has_next:
                        first_growth(1 - par, P + 1)
                    dve.wait_ge(qk_full, qk + 8)
                    dve.wait_ge(tot_done, P * 5 + 4)
                    grow(par, HALF[7], "k").then_inc(k_up, 1)
                    if has_next:
                        take_own(1 - par, P + 1)
                    grow(par, HALF[7], "q").then_inc(q_up, 1)
                    if p == NP - 2 and not last:
                        low_xT(b + 1)

            body(0, first=True)
            with dve.Fori(1, B - 1) as b:
                body(b)
            body(B - 1, last=True)
            P = B * NP - 1
            states(P % 2, P)
            dve.wait_ge(av_done, B * NP * HP)
            ln_halves(B - 1, y3, x_rows(B - 1))
            ln_variance(B - 1)
            ln1_apply(B - 1)

            def head_x(n):
                dve.wait_ge(a_x1T, n + 1)
                nc.vector.tensor_tensor(x1T[1][:, :], h0_ps[:, :], x1T[0][:, :].bitcast(fp32), ALU.subtract).then_inc(v_x1T, 1)

            def head_z(n):
                dve.wait_ge(a_s1, n + 1)
                await_count(dve, a_xt, n)
                await_count(dve, f_gate, n)
                nc.vector.scalar_tensor_tensor(out=xt32, in0=h1_ps[:, :], scalar=swf_b[:, 1:2], in1=s1,
                                               op0=ALU.add, op1=ALU.mult).then_inc(v_xt32, 1)

            def head_xt(n, par):
                dve.wait_ge(a_xt, n + 1)
                await_count(dve, f_u, (n - 1) * NE)
                nc.vector.tensor_tensor(xt_sb[par][1][:, :], xt32, xt_sb[par][0][:, :].bitcast(fp32),
                                        ALU.subtract).then_inc(v_xt, 1)

            def low_r(n):
                dve.wait_ge(a_r, n + 1)
                nc.vector.tensor_tensor(r_sb[1][:, :], r_ps[:, :], r_sb[0][:, :].bitcast(fp32), ALU.subtract).then_inc(v_r, 1)

            TOP = 13

            def logits(n):
                dve.wait_ge(f_gate, n + 1)
                g3 = h0_ps[:, :].rearrange("p (c e) -> p c e", c=NC)[:, :, 0:E]
                nc.vector.tensor_reduce(lmax[:, :], g3, axis=AX.X, op=ALU.max).then_inc(v_top, 1)
                dve.wait_ge(v_top, n * TOP + 1)
                await_count(dve, a_ex, n)
                nc.vector.tensor_tensor(lg[:, :, :], g3, lmax[:, :].rearrange("p (c o) -> p c o", o=1).to_broadcast([128, NC, E]),
                                        ALU.subtract).then_inc(v_lg, 1)

            def rank_experts(n):
                four = lambda t: t[:, :, :].rearrange("p (c e) j -> p c e j", e=E)
                of_j = ex[:, :, :].rearrange("p c (o j) -> p c o j", o=1).to_broadcast([128, NC, E, E])
                of_e = ex[:, :, :].rearrange("p c (e o) -> p c e o", o=1).to_broadcast([128, NC, E, E])
                first_of = earlier[:, :, :].rearrange("p (o e) j -> p o e j", o=1).to_broadcast([128, NC, E, E])
                top = n * TOP
                dve.wait_ge(a_ex, n + 1)
                nc.vector.tensor_tensor(four(gt), of_j, of_e, ALU.is_gt).then_inc(v_top, 1)
                nc.vector.tensor_tensor(four(eq), of_j, of_e, ALU.is_equal).then_inc(v_top, 1)
                dve.wait_ge(v_top, top + 3)
                nc.vector.tensor_tensor(four(eqe), four(eq), first_of, ALU.mult).then_inc(v_top, 1)
                dve.wait_ge(v_top, top + 4)
                nc.vector.tensor_tensor(four(gt), four(gt), four(eqe), ALU.add).then_inc(v_top, 1)
                dve.wait_ge(v_top, top + 5)
                nc.vector.tensor_reduce(rank[:, :, :], four(gt), axis=AX.X, op=ALU.add).then_inc(v_top, 1)

            def choose(n):
                top = n * TOP
                dve.wait_ge(v_top, top + 6)
                nc.vector.scalar_tensor_tensor(out=picked[:, :, :], in0=rank[:, :, :], scalar=float(TOPK), in1=ex[:, :, :],
                                               op0=ALU.is_lt, op1=ALU.mult).then_inc(v_top, 1)
                dve.wait_ge(v_top, top + 7)
                nc.vector.tensor_reduce(den[:, :], picked[:, :, :], axis=AX.X, op=ALU.add).then_inc(v_top, 1)
                dve.wait_ge(v_top, top + 8)
                nc.vector.reciprocal(rden[:, :], den[:, :]).then_inc(v_top, 1)
                dve.wait_ge(v_top, top + 9)
                nc.vector.tensor_tensor(comb[:, :, :], picked[:, :, :],
                                        rden[:, :].rearrange("p (c o) -> p c o", o=1).to_broadcast([128, NC, E]),
                                        ALU.mult).then_inc(v_top, 1)
                dve.wait_ge(v_top, top + 10)
                await_count(dve, f_ct, n)
                nc.vector.tensor_copy(comb_parts[:, :, 0, :], comb[:, :, :]).then_inc(v_top, 1)
                dve.wait_ge(v_top, top + 11)
                nc.vector.tensor_tensor(comb_rest[:, :, :], comb[:, :, :], comb_parts[:, :, 0, :], ALU.subtract).then_inc(v_top, 1)
                dve.wait_ge(v_top, top + 12)
                nc.vector.tensor_copy(comb_parts[:, :, 1, :], comb_rest[:, :, :]).then_inc(v_top, 1)
                dve.wait_ge(v_top, top + 13)
                nc.vector.tensor_tensor(comb_parts[:, :, 2, :], comb_rest[:, :, :], comb_parts[:, :, 1, :],
                                        ALU.subtract).then_inc(v_comb, 1)

            def gate_expert(n, par, e):
                k = n * NE + e
                dve.wait_ge(a_sg, k + 1)
                dve.wait_ge(f_u, k + 1)
                await_count(dve, p_gc, k - 3)
                if e >= NS:
                    nc.vector.tensor_tensor(gu[e % 2], sg[e % 2], u_ps[e % 2][:, :], ALU.mult).then_inc(v_mid, 1)
                    dve.wait_ge(f_cb, n * E + e - NS + 1)
                    dve.wait_ge(v_mid, n * E + e - NS + 1)
                    nc.vector.tensor_tensor(gc[(par * NE + e) % 4], gu[e % 2], cb_ps[:, :], ALU.mult).then_inc(v_gu, 1)
                else:
                    nc.vector.tensor_tensor(gc[(par * NE + e) % 4], sg[e % 2], u_ps[e % 2][:, :], ALU.mult).then_inc(v_gu, 1)

            def tail_z(n):
                dve.wait_ge(a_s2, n + 1)
                await_count(dve, f_hT, n)
                nc.vector.scalar_tensor_tensor(out=h_sb, in0=h1_ps[:, :], scalar=swf_b[:, 3:4], in1=s2,
                                               op0=ALU.add, op1=ALU.mult).then_inc(v_h, 1)

            def ln2(n, par):
                dve.wait_ge(f_hT, n + 1)
                ln_halves(B + n, h0_ps[:, :].rearrange("p (c d) -> p c d", c=NC), x_rows(n))
                ln_variance(B + n)

            def ln2_out(n, par):
                await_count(dve, out_done[par], (n - par) * 8)
                ln_apply(B + n, lambda c: o_sb[par][:, c, :])

            def ffn(b, first=False, last=False):
                for par in range(2):
                    n = b + par
                    has_prev = not (first and par == 0)
                    has_next = not (last and par == 1)
                    for e in range(NE):
                        gate_expert(n, par, e)
                        if e == 0 and has_next:
                            head_x(n + 1)
                        if e == 2 and has_prev:
                            low_r(n - 1)
                        if e == 2 and has_next:
                            head_z(n + 1)
                        if e == 3 and has_next:
                            head_xt(n + 1, 1 - par)
                        if e == 3 and has_prev:
                            tail_z(n - 1)
                        if e == 4 and has_prev:
                            ln2(n - 1, 1 - par)
                        if e == 5 and has_prev:
                            ln2_out(n - 1, 1 - par)
                        if e == 6 and has_next:
                            logits(n + 1)
                        if e == 7 and has_next:
                            rank_experts(n + 1)
                        if e == 8 and has_next:
                            choose(n + 1)

            head_x(0)
            head_z(0)
            head_xt(0, 0)
            logits(0)
            rank_experts(0)
            choose(0)
            ffn(0, first=True)
            with dve.Fori(1, B // 2 - 1) as i:
                ffn(2 * i)
            ffn(B - 2, last=True)
            low_r(B - 1)
            tail_z(B - 1)
            ln2(B - 1, 1)
            ln2_out(B - 1, 1)


_INS = ["L0_attn_x", "L0_attn_Wq", "L0_attn_Wk", "L0_attn_Wv", "L0_attn_Wg", "L0_attn_Wo",
        "L0_ffn_lin0_w", "L0_ffn_lin0_b", "L0_ffn_swi1_w1", "L0_ffn_swi1_b1", "L0_ffn_swi1_w2", "L0_ffn_swi1_b2",
        "L0_ffn_gate_w", "L0_ffn_exp_w1", "L0_ffn_exp_w3", "L0_ffn_exp_w2", "L0_ffn_sh_w1", "L0_ffn_sh_w3",
        "L0_ffn_sh_w2", "L0_ffn_lin1_w", "L0_ffn_lin1_b", "L0_ffn_swi2_w1", "L0_ffn_swi2_b1", "L0_ffn_swi2_w2",
        "L0_ffn_swi2_b2"]


def kernel(**inputs):
    import numpy as _np
    import concourse.bacc as _bacc
    from concourse import mybir as _mybir
    from concourse.bass_utils import run_bass_kernel_spmd as _run

    nc = _bacc.Bacc("TRN2", target_bir_lowering=False, num_devices=1)
    arrays, args = {}, []
    for name in _INS:
        a = _np.ascontiguousarray(inputs[name])
        arrays[f"in_{name}_dram"] = a
        args.append(nc.dram_tensor(f"in_{name}_dram", a.shape, _mybir.dt.from_np(a.dtype), kind="ExternalInput").ap())
    shape = inputs["L0_attn_x"].shape
    out = nc.dram_tensor("out_0_dram", shape, _mybir.dt.from_np(_np.dtype("float32")), kind="ExternalOutput").ap()
    gated_linear_attention_and_moe_block(nc, *args, out)
    r = _run(nc, [arrays], core_ids=[0])
    return r.results[0]["out_0_dram"]
```
